# Optimizing a Trainium2 kernel written in Bass

```python
import numpy as np
import jax
import jax.numpy as jnp

def _softmax(x, axis=-1):
    return jax.nn.softmax(x, axis=axis)
def _gelu(x):
    return jax.nn.gelu(x, approximate=True)
def _silu(x):
    return jax.nn.silu(x)
def _sigmoid(x):
    return jax.nn.sigmoid(x)
def _layernorm(x, axis=-1, eps=1e-5):
    m = jnp.mean(x, axis=axis, keepdims=True)
    v = jnp.var(x, axis=axis, keepdims=True)
    return (x - m) / jnp.sqrt(v + eps)
def _scatter_add(tgt, idx, src, axis=0):
    return tgt.at[idx].add(src)
def _segment_sum(src, seg, n):
    return jax.ops.segment_sum(src, seg, n)

kernel_name = 'mk_metaformer_d1_conv_nchw256_6e4000'

def setup_inputs(seed: int = 0):
    np.random.seed(seed)
    _w = jnp.asarray
    def _rec_inputs():
        import jax
        import jax.numpy as jnp
        _gk = jax.random.key(seed)
        x = -0.0002928 + 1 * jax.random.normal(jax.random.fold_in(_gk, 1), (4, 256, 64, 64), jnp.float32)
        return x
    x = _rec_inputs()
    def _L0_conv_setup():
        import jax, jax.numpy as jnp
        import numpy as np
        from jax import lax
        DIM, D_INNER, D_STATE, D_CONV, DT_RANK = (256, 512, 16, 4, 16)
        B_, H_, W_ = (4, 64, 64)

        def _mamba_forward(x, in_proj_w, conv_w, conv_b, x_proj_w, dt_proj_w, dt_proj_b, A_log, D, out_proj_w):
            b, c, h, w = x.shape
            L = h * w
            xs = x.reshape(b, c, L).transpose(0, 2, 1)
            xz = jnp.einsum('bld,ed->ble', xs, in_proj_w)
            u, res = jnp.split(xz, 2, axis=-1)
            u_t = u.transpose(0, 2, 1)
            u_t = lax.conv_general_dilated(u_t, conv_w, window_strides=(1,), padding=[(D_CONV - 1, 0)], feature_group_count=D_INNER, dimension_numbers=('NCH', 'OIH', 'NCH'))
            u = jax.nn.silu(u_t.transpose(0, 2, 1) + conv_b)
            dbc = jnp.einsum('bld,ed->ble', u, x_proj_w)
            dt, Bm, Cm = jnp.split(dbc, [DT_RANK, DT_RANK + D_STATE], axis=-1)
            delta = jax.nn.softplus(jnp.einsum('blr,dr->bld', dt, dt_proj_w) + dt_proj_b)
            A = -jnp.exp(A_log)
            deltaA = jnp.exp(jnp.einsum('bld,dn->bldn', delta, A))
            deltaBu = jnp.einsum('bld,bln,bld->bldn', delta, Bm, u)

            def step(state, inp):
                dA, dBu, c_t = inp
                state = dA * state + dBu
                y = jnp.einsum('bdn,bn->bd', state, c_t)
                return (state, y)
            init = jnp.zeros((b, D_INNER, D_STATE), dtype=x.dtype)
            _, ys = lax.scan(step, init, (jnp.moveaxis(deltaA, 1, 0), jnp.moveaxis(deltaBu, 1, 0), jnp.moveaxis(Cm, 1, 0)))
            y = jnp.moveaxis(ys, 0, 1) + u * D
            y = y * jax.nn.silu(res)
            out = jnp.einsum('ble,de->bld', y, out_proj_w)
            return out.transpose(0, 2, 1).reshape(b, c, h, w)
        key = jax.random.key(seed)
        ks = jax.random.split(key, 10)
        s = lambda k, shape, scale: jax.random.normal(k, shape, dtype=jnp.float32) * scale
        inp = {'x': s(ks[0], (B_, DIM, H_, W_), 1.0), 'in_proj_w': s(ks[1], (2 * D_INNER, DIM), DIM ** (-0.5)), 'conv_w': s(ks[2], (D_INNER, 1, D_CONV), D_CONV ** (-0.5)), 'conv_b': s(ks[3], (D_INNER,), 0.02), 'x_proj_w': s(ks[4], (DT_RANK + 2 * D_STATE, D_INNER), D_INNER ** (-0.5)), 'dt_proj_w': s(ks[5], (D_INNER, DT_RANK), DT_RANK ** (-0.5)), 'dt_proj_b': s(ks[6], (D_INNER,), 0.02), 'A_log': jnp.broadcast_to(jnp.log(jnp.arange(1, D_STATE + 1, dtype=jnp.float32)), (D_INNER, D_STATE)).copy(), 'D': jnp.ones((D_INNER,), dtype=jnp.float32), 'out_proj_w': s(ks[7], (DIM, D_INNER), D_INNER ** (-0.5))}
        return inp
    _L0_conv_all = _L0_conv_setup()
    _L0_conv_in = {k: v for k, v in _L0_conv_all.items() if k in ('in_proj_w', 'conv_w', 'conv_b', 'x_proj_w', 'dt_proj_w', 'dt_proj_b', 'A_log', 'D', 'out_proj_w', )}
    del _L0_conv_all

    def _L0_ffn_setup():
        import jax, jax.numpy as jnp
        import numpy as np
        B, N, D = (16, 4096, 256)
        NUM_EXPERTS, TOP_K, HEADS = (4, 2, 4)
        N_EDGES = 1048576
        LN_EPS = 1e-05

        def _layernorm(x, g, b):
            mu = x.mean(-1, keepdims=True)
            var = ((x - mu) ** 2).mean(-1, keepdims=True)
            return (x - mu) * jax.lax.rsqrt(var + LN_EPS) * g + b

        def _forward(x, edge_index, W_gat, att_src, att_dst, b_gat, ln_gamma, ln_beta, W1, b1, W2, b2):
            Bc, Nc, Dc = x.shape
            M = Bc * Nc
            x_flat = x.reshape(M, Dc)
            h = (x_flat @ W_gat).reshape(M, HEADS, NUM_EXPERTS)
            loops = jnp.arange(M, dtype=edge_index.dtype)
            src = jnp.concatenate([edge_index[0], loops])
            dst = jnp.concatenate([edge_index[1], loops])
            a_src = (h * att_src).sum(-1)
            a_dst = (h * att_dst).sum(-1)
            e = jax.nn.leaky_relu(a_src[src] + a_dst[dst], negative_slope=0.2)
            e_max = jax.ops.segment_max(e, dst, num_segments=M)
            ee = jnp.exp(e - e_max[dst])
            denom = jax.ops.segment_sum(ee, dst, num_segments=M)
            alpha = ee / (denom[dst] + 1e-16)
            msg = h[src] * alpha[:, :, None]
            agg = jax.ops.segment_sum(msg, dst, num_segments=M).reshape(M, HEADS * NUM_EXPERTS) + b_gat
            scores = _layernorm(agg, ln_gamma, ln_beta).reshape(M, HEADS, NUM_EXPERTS).mean(1)
            scores = scores.reshape(Bc, Nc, NUM_EXPERTS)
            topk_s, topk_i = jax.lax.top_k(scores, TOP_K)
            w = jax.nn.softmax(topk_s, axis=-1)
            out = jnp.zeros_like(x)
            for ei in range(NUM_EXPERTS):
                g = jnp.where(topk_i == ei, w, 0.0).sum(-1)
                hh = jax.nn.gelu(x @ W1[ei] + b1[ei], approximate=False)
                out = out + g[..., None] * (hh @ W2[ei] + b2[ei])
            return out
        key = jax.random.key(seed)
        ks = jax.random.split(key, 8)
        s = 0.05
        return {'x': jax.random.normal(ks[0], (B, N, D), jnp.float32), 'W_gat': jax.random.normal(ks[1], (D, HEADS * NUM_EXPERTS), jnp.float32) * s, 'att_src': jax.random.normal(ks[2], (HEADS, NUM_EXPERTS), jnp.float32) * s, 'att_dst': jax.random.normal(ks[3], (HEADS, NUM_EXPERTS), jnp.float32) * s, 'b_gat': jnp.zeros((HEADS * NUM_EXPERTS,), jnp.float32), 'ln_gamma': jnp.ones((HEADS * NUM_EXPERTS,), jnp.float32), 'ln_beta': jnp.zeros((HEADS * NUM_EXPERTS,), jnp.float32), 'W1': jax.random.normal(ks[4], (NUM_EXPERTS, D, 2 * D), jnp.float32) * s, 'b1': jnp.zeros((NUM_EXPERTS, 2 * D), jnp.float32), 'W2': jax.random.normal(ks[5], (NUM_EXPERTS, 2 * D, D), jnp.float32) * s, 'b2': jnp.zeros((NUM_EXPERTS, D), jnp.float32), 'edge_index': jax.random.randint(ks[6], (2, N_EDGES), 0, B * N, jnp.int32)}
    _L0_ffn_all = _L0_ffn_setup()
    _L0_ffn_in = {k: v for k, v in _L0_ffn_all.items() if k in ('W_gat', 'att_src', 'att_dst', 'b_gat', 'ln_gamma', 'ln_beta', 'W1', 'b1', 'W2', 'b2', 'edge_index', )}
    del _L0_ffn_all

    return {
        "x": x,
        "L0_conv_in_proj_w": _L0_conv_in["in_proj_w"],
        "L0_conv_conv_w": _L0_conv_in["conv_w"],
        "L0_conv_conv_b": _L0_conv_in["conv_b"],
        "L0_conv_x_proj_w": _L0_conv_in["x_proj_w"],
        "L0_conv_dt_proj_w": _L0_conv_in["dt_proj_w"],
        "L0_conv_dt_proj_b": _L0_conv_in["dt_proj_b"],
        "L0_conv_A_log": _L0_conv_in["A_log"],
        "L0_conv_D": _L0_conv_in["D"],
        "L0_conv_out_proj_w": _L0_conv_in["out_proj_w"],
        "L0_ffn_W_gat": _L0_ffn_in["W_gat"],
        "L0_ffn_att_src": _L0_ffn_in["att_src"],
        "L0_ffn_att_dst": _L0_ffn_in["att_dst"],
        "L0_ffn_b_gat": _L0_ffn_in["b_gat"],
        "L0_ffn_ln_gamma": _L0_ffn_in["ln_gamma"],
        "L0_ffn_ln_beta": _L0_ffn_in["ln_beta"],
        "L0_ffn_W1": _L0_ffn_in["W1"],
        "L0_ffn_b1": _L0_ffn_in["b1"],
        "L0_ffn_W2": _L0_ffn_in["W2"],
        "L0_ffn_b2": _L0_ffn_in["b2"],
        "L0_ffn_edge_index": _L0_ffn_in["edge_index"],
    }

def reference(x, L0_conv_in_proj_w, L0_conv_conv_w, L0_conv_conv_b, L0_conv_x_proj_w, L0_conv_dt_proj_w, L0_conv_dt_proj_b, L0_conv_A_log, L0_conv_D, L0_conv_out_proj_w, L0_ffn_W_gat, L0_ffn_att_src, L0_ffn_att_dst, L0_ffn_b_gat, L0_ffn_ln_gamma, L0_ffn_ln_beta, L0_ffn_W1, L0_ffn_b1, L0_ffn_W2, L0_ffn_b2, L0_ffn_edge_index):
    import jax
    import jax.numpy as jnp
    def _L0_conv_ref(x, in_proj_w, conv_w, conv_b, x_proj_w, dt_proj_w, dt_proj_b, A_log, D, out_proj_w):
        import jax, jax.numpy as jnp
        import numpy as np
        from jax import lax
        DIM, D_INNER, D_STATE, D_CONV, DT_RANK = (256, 512, 16, 4, 16)
        B_, H_, W_ = (4, 64, 64)

        def _mamba_forward(x, in_proj_w, conv_w, conv_b, x_proj_w, dt_proj_w, dt_proj_b, A_log, D, out_proj_w):
            b, c, h, w = x.shape
            L = h * w
            xs = x.reshape(b, c, L).transpose(0, 2, 1)
            xz = jnp.einsum('bld,ed->ble', xs, in_proj_w)
            u, res = jnp.split(xz, 2, axis=-1)
            u_t = u.transpose(0, 2, 1)
            u_t = lax.conv_general_dilated(u_t, conv_w, window_strides=(1,), padding=[(D_CONV - 1, 0)], feature_group_count=D_INNER, dimension_numbers=('NCH', 'OIH', 'NCH'))
            u = jax.nn.silu(u_t.transpose(0, 2, 1) + conv_b)
            dbc = jnp.einsum('bld,ed->ble', u, x_proj_w)
            dt, Bm, Cm = jnp.split(dbc, [DT_RANK, DT_RANK + D_STATE], axis=-1)
            delta = jax.nn.softplus(jnp.einsum('blr,dr->bld', dt, dt_proj_w) + dt_proj_b)
            A = -jnp.exp(A_log)
            deltaA = jnp.exp(jnp.einsum('bld,dn->bldn', delta, A))
            deltaBu = jnp.einsum('bld,bln,bld->bldn', delta, Bm, u)

            def step(state, inp):
                dA, dBu, c_t = inp
                state = dA * state + dBu
                y = jnp.einsum('bdn,bn->bd', state, c_t)
                return (state, y)
            init = jnp.zeros((b, D_INNER, D_STATE), dtype=x.dtype)
            _, ys = lax.scan(step, init, (jnp.moveaxis(deltaA, 1, 0), jnp.moveaxis(deltaBu, 1, 0), jnp.moveaxis(Cm, 1, 0)))
            y = jnp.moveaxis(ys, 0, 1) + u * D
            y = y * jax.nn.silu(res)
            out = jnp.einsum('ble,de->bld', y, out_proj_w)
            return out.transpose(0, 2, 1).reshape(b, c, h, w)
        return _mamba_forward(x, in_proj_w, conv_w, conv_b, x_proj_w, dt_proj_w, dt_proj_b, A_log, D, out_proj_w)

    def _L0_ffn_ref(x, W_gat, att_src, att_dst, b_gat, ln_gamma, ln_beta, W1, b1, W2, b2, edge_index):
        import jax, jax.numpy as jnp
        import numpy as np
        B, N, D = (16, 4096, 256)
        NUM_EXPERTS, TOP_K, HEADS = (4, 2, 4)
        N_EDGES = 1048576
        LN_EPS = 1e-05

        def _layernorm(x, g, b):
            mu = x.mean(-1, keepdims=True)
            var = ((x - mu) ** 2).mean(-1, keepdims=True)
            return (x - mu) * jax.lax.rsqrt(var + LN_EPS) * g + b

        def _forward(x, edge_index, W_gat, att_src, att_dst, b_gat, ln_gamma, ln_beta, W1, b1, W2, b2):
            Bc, Nc, Dc = x.shape
            M = Bc * Nc
            x_flat = x.reshape(M, Dc)
            h = (x_flat @ W_gat).reshape(M, HEADS, NUM_EXPERTS)
            loops = jnp.arange(M, dtype=edge_index.dtype)
            src = jnp.concatenate([edge_index[0], loops])
            dst = jnp.concatenate([edge_index[1], loops])
            a_src = (h * att_src).sum(-1)
            a_dst = (h * att_dst).sum(-1)
            e = jax.nn.leaky_relu(a_src[src] + a_dst[dst], negative_slope=0.2)
            e_max = jax.ops.segment_max(e, dst, num_segments=M)
            ee = jnp.exp(e - e_max[dst])
            denom = jax.ops.segment_sum(ee, dst, num_segments=M)
            alpha = ee / (denom[dst] + 1e-16)
            msg = h[src] * alpha[:, :, None]
            agg = jax.ops.segment_sum(msg, dst, num_segments=M).reshape(M, HEADS * NUM_EXPERTS) + b_gat
            scores = _layernorm(agg, ln_gamma, ln_beta).reshape(M, HEADS, NUM_EXPERTS).mean(1)
            scores = scores.reshape(Bc, Nc, NUM_EXPERTS)
            topk_s, topk_i = jax.lax.top_k(scores, TOP_K)
            w = jax.nn.softmax(topk_s, axis=-1)
            out = jnp.zeros_like(x)
            for ei in range(NUM_EXPERTS):
                g = jnp.where(topk_i == ei, w, 0.0).sum(-1)
                hh = jax.nn.gelu(x @ W1[ei] + b1[ei], approximate=False)
                out = out + g[..., None] * (hh @ W2[ei] + b2[ei])
            return out
        return _forward(x, edge_index, W_gat, att_src, att_dst, b_gat, ln_gamma, ln_beta, W1, b1, W2, b2)

    def _gn(v, G=32, eps=1e-5):
        B_, C_, H_, W_ = v.shape
        g = v.reshape(B_, G, C_ // G, H_, W_)
        m = jnp.mean(g, axis=(2, 3, 4), keepdims=True)
        s = jnp.var(g, axis=(2, 3, 4), keepdims=True)
        return ((g - m) / jnp.sqrt(s + eps)).reshape(v.shape)

    def _ln_c(v, eps=1e-6):
        m = jnp.mean(v, axis=1, keepdims=True)
        s = jnp.var(v, axis=1, keepdims=True)
        return (v - m) / jnp.sqrt(s + eps)

    def _ln_t(v, eps=1e-5):
        m = jnp.mean(v, axis=-1, keepdims=True)
        s = jnp.var(v, axis=-1, keepdims=True)
        return (v - m) / jnp.sqrt(s + eps)

    def _to_tokens(v):
        B_, C_, H_, W_ = v.shape
        return v.reshape(B_, C_, H_ * W_).transpose(0, 2, 1)
    def _from_tokens(t, like):
        B_, C_, H_, W_ = like.shape
        return t.transpose(0, 2, 1).reshape(B_, C_, H_, W_)

    x = x + _L0_conv_ref(_ln_c(x), L0_conv_in_proj_w, L0_conv_conv_w, L0_conv_conv_b, L0_conv_x_proj_w, L0_conv_dt_proj_w, L0_conv_dt_proj_b, L0_conv_A_log, L0_conv_D, L0_conv_out_proj_w)
    t = _to_tokens(x)
    t = t + _L0_ffn_ref(_ln_t(t), L0_ffn_W_gat, L0_ffn_att_src, L0_ffn_att_dst, L0_ffn_b_gat, L0_ffn_ln_gamma, L0_ffn_ln_beta, L0_ffn_W1, L0_ffn_b1, L0_ffn_W2, L0_ffn_b2, L0_ffn_edge_index)
    x = _from_tokens(t, x)
    return x


_drawn_inputs = setup_inputs


def setup_inputs(seed=0):
    import zlib

    import numpy as np

    out = dict(_drawn_inputs(seed))
    spreads = {'L0_conv_D': (1.0, 0.2),
     'L0_ffn_b_gat': (0.0, 0.46),
     'L0_ffn_ln_gamma': (1.0, 0.6),
     'L0_ffn_ln_beta': (0.0, 0.422),
     'L0_ffn_b1': (0.0, 0.1),
     'L0_ffn_b2': (0.0, 0.1)}
    factors = {'L0_conv_conv_b': 3.835,
     'L0_conv_dt_proj_b': 8.0,
     'L0_ffn_att_src': 8.0,
     'L0_ffn_att_dst': 27.989}
    for name, (base, spread) in spreads.items():
        noise = np.random.default_rng([zlib.crc32(name.encode()), seed]).standard_normal(out[name].shape)
        drawn = base * np.exp(spread * noise) if base else spread * noise
        out[name] = jnp.asarray(drawn.astype(out[name].dtype))
    for name, factor in factors.items():
        out[name] = (out[name] * factor).astype(out[name].dtype)
    return out
```

```python
import numpy as np
import concourse.bass as bass
from concourse import mybir
from contextlib import ExitStack

ALU = mybir.AluOpType
ACT = mybir.ActivationFunctionType
F32 = mybir.dt.float32
BF16 = mybir.dt.bfloat16
I32 = mybir.dt.int32
U32 = mybir.dt.uint32

P = 128
NODES = 16384
EDGES = 1048576
EC = EDGES // P
LB = EC.bit_length() - 1
PB = 7
SRC_BITS = 14
SRC_MASK = NODES - 1
OFF = 1024
GROUPS = 2 * NODES
CHUNK = 8192
CW = CHUNK // P


def float_of(bits):
    return float(np.array([bits], np.uint32).view(np.float32)[0])


class Steps:

    def __init__(self, engine, sem, base=0):
        self.engine, self.sem, self.base, self.n = engine, sem, base, 0

    def __call__(self, instruction):
        instruction.then_inc(self.sem, 1)
        self.n += 1

    def settle(self, back=0):
        self.engine.wait_ge(self.sem, self.base + (self.n - back))


def wait_alone(engine, sem, value, passed):
    engine.wait_ge(sem, value)
    if not isinstance(value, int):
        engine.sem_inc(passed, 1)


def sort_edges(nc, edge_src, edge_dst, keys_dram, ends_at_dram, ends_dram, src_dram, dst_dram, counts):
    with ExitStack() as ctx:
        sb = lambda name, shape, dt: ctx.enter_context(nc.sbuf_tensor(name, shape, dt))
        sem = lambda name: ctx.enter_context(nc.semaphore(name))
        x = sb("sort_x", [P, EC], F32)
        y = sb("sort_y", [P, EC], F32)
        z = sb("sort_z", [P, EC], F32)
        ident = sb("sort_ident", [P, P], F32)
        lane = sb("lane", [P, 1], I32)
        lane_bit = sb("lane_bit", [P, PB], I32)
        sign = sb("sign", [P, PB + 1], F32)
        ones = sb("sort_ones", [P, P], F32)
        below = sb("below", [P, 2], F32)
        sentinel = sb("sentinel", [1, 1], I32)
        zeros = sb("zero_rows", [P, (GROUPS + OFF) // P], I32)
        ps = [ctx.enter_context(nc.psum_tensor(f"sort_ps{k}", [P, 1024], F32)) for k in range(4)]
        loaded, const, lanes, keys_made = sem("edges_loaded"), sem("const_ready"), sem("lane_iota"), sem("keys_made")
        dve_steps, act_steps = sem("dve_steps"), sem("act_steps")
        run_sorted, transposed = sem("run_sorted"), sem("transposed")
        out = sem("evacuated_by_scalar"), sem("evacuated_by_vector")
        stored, reloaded, counted = sem("keys_stored"), sem("next_loaded"), sem("lane_counts_summed")
        counted_dve, idx_made, idx_stored, zeroed = sem("lane_counts"), sem("ends_at_made"), sem("ends_at_stored"), sem("ends_zeroed")
        src_made, dst_made, src_stored, dst_stored = sem("src_made"), sem("dst_made"), sem("src_stored"), sem("dst_stored")
        xi, yi, zi = (t[:, :].bitcast(I32) for t in (x, y, z))
        TILES = EC // P
        GROUP = 8
        NG = TILES // GROUP
        upper = range(LB + 1, LB + PB + 1)
        sides, at = [], LB * (LB + 1) // 2 + 1
        for level in upper:
            for stages in (level - LB, LB):
                sides.append(((y, x) if at % 2 == 0 else (x, y)))
                at += 1 + stages

        def halves(n, k):
            src, dst = ps[(n * NG + k) % 4][:, :], sides[n][1][:, k * GROUP * P:(k + 1) * GROUP * P]
            if n % 2 == 0:
                view = lambda w, d: w.rearrange("p (h d l) -> p h d l", d=2, l=1 << (n // 2))[:, :, d]
                return [(view(dst, 0), view(src, 0), 1.0), (view(dst, 1), view(src, 1), -1.0)]
            half = GROUP * P // 2
            return [(dst[:, c:c + half], src[:, c:c + half], sign[:, n // 2 + 1:n // 2 + 2]) for c in (0, half)]

        with nc.Block() as block:
            @block.sync
            def _(sp):
                sp.dma_start(xi, edge_src).then_inc(loaded, 16)
                sp.dma_start(yi, edge_dst).then_inc(loaded, 16)
                sp.wait_ge(const, 4)
                sp.dma_start(keys_dram[0:1, :], sentinel[:, :]).then_inc(zeroed, 16)
                sp.dma_start(keys_dram[EDGES + 1:EDGES + 2, :], sentinel[:, :]).then_inc(zeroed, 16)
                sp.dma_start(ends_dram.rearrange("(p c) o -> p (c o)", p=P), zeros[:, :]).then_inc(zeroed, 16)
                sp.wait_ge(keys_made, 1)
                body = keys_dram[1:EDGES + 1, :].rearrange("(p c) o -> p (c o)", p=P)
                sp.dma_start(body, xi).then_inc(stored, 16)
                sp.wait_ge(stored, 16)
                sp.wait_ge(zeroed, 48)
                shifted = keys_dram[2:EDGES + 2, :].rearrange("(p c) o -> p (c o)", p=P)
                sp.dma_start(yi, shifted).then_inc(reloaded, 16)
                lanes_of = lambda t: t.rearrange("(p c) o -> p (c o)", p=P)
                sp.wait_ge(src_made, 1)
                sp.dma_start(lanes_of(src_dram), zi).then_inc(src_stored, 16)
                sp.wait_ge(idx_made, 1)
                sp.dma_start(ends_at_dram.rearrange("(p c) o -> p (c o)", p=P), zi).then_inc(idx_stored, 16)
                sp.wait_ge(dst_made, 1)
                sp.dma_start(lanes_of(dst_dram), yi).then_inc(dst_stored, 16)
                sp.wait_ge(src_stored, 16)
                sp.wait_ge(dst_stored, 16)
                sp.wait_ge(idx_stored, 16)

            @block.gpsimd
            def _(pool):
                nc.gpsimd.iota(lane[:, :], pattern=[[0, 1]], base=0, channel_multiplier=1).then_inc(lanes, 1)
                nc.gpsimd.memset(ones[:, :], 1.0).then_inc(const, 1)
                nc.gpsimd.memset(sentinel[:, :], 0).then_inc(const, 1)
                nc.gpsimd.memset(zeros[:, :], 0).then_inc(const, 1)
                pool.wait_ge(const, 1)
                nc.gpsimd.affine_select(out=ident[:, :], in_=ones[:, :], compare_op=ALU.is_equal, fill=0.0, base=0,
                                        pattern=[[-1, P]], channel_multiplier=1).then_inc(const, 1)

            @block.vector
            def _(dve):
                step = Steps(dve, dve_steps)
                v = nc.vector
                dve.wait_ge(lanes, 1)
                for b in range(PB):
                    step(v.tensor_scalar(lane_bit[:, b:b + 1], lane[:, :], b, 1, ALU.logical_shift_right, ALU.bitwise_and))
                step.settle()
                step(v.tensor_scalar(sign[:, 0:PB], lane_bit[:, :], -2, 1, ALU.mult, ALU.add))
                step(v.memset(sign[:, PB:PB + 1], 1.0))
                dve.wait_ge(loaded, 32)
                def one(out, in_, a, b, op0, op1):
                    step(v.tensor_scalar(out, in_, a, b, op0, op1)); step.settle()
                def two(out, a, b, op):
                    step(v.tensor_tensor(out, a, b, op)); step.settle()
                one(zi, xi, 0, NODES, ALU.is_lt, ALU.mult)
                two(xi, xi, zi, ALU.add)
                one(xi, xi, 0, NODES - 1, ALU.max, ALU.min)
                one(yi, yi, -1, NODES, ALU.max, ALU.min)
                one(yi, yi, 0x1FFFF, None, ALU.bitwise_and, ALU.bypass)
                one(zi, xi, NODES - 1, NODES, ALU.is_equal, ALU.mult)
                two(zi, zi, yi, ALU.add)
                one(yi, yi, NODES, 4 * NODES, ALU.is_ge, ALU.mult)
                two(yi, yi, zi, ALU.add)
                one(yi, yi, GROUPS, OFF, ALU.min, ALU.add)
                one(yi, yi, SRC_BITS, None, ALU.logical_shift_left, ALU.bypass)
                two(yi, xi, yi, ALU.bitwise_or)

                cur, nxt = y, x

                def stage(bit, direction):
                    nonlocal cur, nxt
                    lo = 1 << bit
                    if direction is None:
                        a, o = (t[:, :].rearrange("p (m t l) -> p m t l", t=2, l=lo) for t in (cur, nxt))
                        step.settle()
                        step(v.tensor_tensor(o[:, :, 0], a[:, :, 0], a[:, :, 1], ALU.min))
                        step(v.tensor_tensor(o[:, :, 1], a[:, :, 0], a[:, :, 1], ALU.max))
                    else:
                        a, o = (t[:, :].rearrange("p (h d m t l) -> p h d m t l", d=2, m=1 << (direction - 1 - bit), t=2, l=lo)
                                for t in (cur, nxt))
                        for d in range(2):
                            step.settle(0 if bit == direction - 1 and d == 0 else 2)
                            low, high = (ALU.min, ALU.max) if d == 0 else (ALU.max, ALU.min)
                            step(v.tensor_tensor(o[:, :, d, :, 0], a[:, :, d, :, 0], a[:, :, d, :, 1], low))
                            step(v.tensor_tensor(o[:, :, d, :, 1], a[:, :, d, :, 0], a[:, :, d, :, 1], high))
                    cur, nxt = nxt, cur

                for level in range(1, LB):
                    for bit in reversed(range(level)):
                        stage(bit, level)
                step.settle()
                step(v.tensor_scalar(nxt[:, :], cur[:, :], sign[:, 0:1], None, ALU.mult))
                cur, nxt = nxt, cur
                for bit in reversed(range(LB)):
                    stage(bit, None)
                for n, (_, other) in enumerate(sides):
                    step.settle()
                    dve.sem_inc(run_sorted, 1)
                    for k in range(1, NG, 2):
                        dve.wait_ge(transposed, n * NG + k + 1)
                        for dst, src, factor in halves(n, k):
                            v.tensor_scalar(dst, src, factor, None, ALU.mult).then_inc(out[1], 1)
                    dve.wait_ge(out[0], (n + 1) * NG)
                    dve.wait_ge(out[1], (n + 1) * NG)
                    cur, nxt = nxt, cur
                    level = upper[n // 2]
                    bits, direction = (level - LB, level - LB) if n % 2 == 0 else (LB, None)
                    for bit in reversed(range(bits)):
                        stage(bit, direction if level < LB + PB else None)
                step.settle()
                assert cur is x, "the network ends in x"
                dve.sem_inc(keys_made, 1)
                for n, top in enumerate((NODES, GROUPS)):
                    step(v.tensor_scalar(z[:, :], x[:, :], float_of((top + OFF) << SRC_BITS), 0.0, ALU.is_lt, ALU.add,
                                         accum_out=below[:, n:n + 1]))
                    step.settle()
                dve.sem_inc(counted_dve, 1)
                dve.wait_ge(counted, 1)
                one(counts[:, :], ps[0][:, 0:2], float(CHUNK - 1), None, ALU.add, ALU.bypass)
                one(counts[:, :], counts[:, :], CHUNK.bit_length() - 1, None, ALU.logical_shift_right, ALU.bypass)
                one(counts[:, :], counts[:, :], 3, None, ALU.max, ALU.bypass)
                dve.wait_ge(reloaded, 16)
                one(yi, yi, SRC_BITS, None, ALU.logical_shift_right, ALU.bypass)
                v.tensor_scalar(zi, xi, SRC_MASK, None, ALU.bitwise_and).then_inc(src_made, 1)
                dve.wait_ge(stored, 16)
                dve.wait_ge(src_made, 1)
                one(xi, xi, SRC_BITS, None, ALU.logical_shift_right, ALU.bypass)
                two(yi, yi, xi, ALU.is_equal)
                dve.wait_ge(src_stored, 16)
                v.scalar_tensor_tensor(zi, yi, float(4 * GROUPS), xi, ALU.mult, ALU.add).then_inc(idx_made, 1)
                dve.wait_ge(idx_made, 1)
                v.tensor_scalar(yi, xi, OFF, NODES - 1, ALU.subtract, ALU.min).then_inc(dst_made, 1)

            @block.tensor
            def _(pe):
                pe.wait_ge(const, 4)
                for n, (src, _) in enumerate(sides):
                    pe.wait_ge(run_sorted, n + 1)
                    for k in range(NG):
                        g = n * NG + k
                        if g >= 4:
                            pe.wait_ge(out[g % 2], 2 * ((g - 4) // 2 + 1))
                        for q in range(GROUP):
                            t = k * GROUP + q
                            last = nc.tensor.transpose(ps[g % 4][:, q * P:(q + 1) * P], src[:, t * P:(t + 1) * P], ident[:, :])
                        last.then_inc(transposed, 1)
                pe.wait_ge(counted_dve, 1)
                pe.wait_ge(out[0], len(sides) * NG)
                nc.tensor.matmul(ps[0][:, 0:2], ones[:, :], below[:, :], start=True, stop=True).then_inc(counted, 1)

            @block.scalar
            def _(act):
                for n in range(len(sides)):
                    for k in range(0, NG, 2):
                        act.wait_ge(transposed, n * NG + k + 1)
                        for dst, src, factor in halves(n, k):
                            nc.scalar.activation(dst, src, ACT.Copy, scale=factor).then_inc(out[0], 1)

T = 512
CHUNKS = NODES // T
PER_BATCH = 4096 // T
CT = 2
DT = 4
NS = 16
GQ = 4
NGR = NS // GQ
STEPS = NGR * DT
HALO = 3
TAPS = 4
SRC_F = 20
DST_F = 4
H_F = SRC_F + DST_F

PRE = ["mean", "var"] + [f"u{d}" for d in range(DT)] + [f"conv{d}" for d in range(DT)] + [f"res{d}" for d in range(DT)] \
    + ["dbc"] + [f"dt{d}" for d in range(DT)]
POST = ["out0", "out1", "mean2", "var2", "h"]
PE_AT = {"out0": 0, "out1": 0, "mean2": 1, "mean": 2, "var2": 3, "var": 4, "h": 6, "dbc": 12,
         **{f"u{d}": 7 for d in range(DT)}, **{f"conv{d}": 9 for d in range(DT)},
         **{f"res{d}": 10 for d in range(DT)}, **{f"dt{d}": 13 for d in range(DT)}}
VEC_AT = {"x2": 0, "centre2": 1, "centre": 2, "norm2": 5, "norm": 6, "low_parts": 12, "lowest_part": 14}
ACT_AT = {"square2": 3, "square": 4, "rstd2": 5, "rstd": 7, "h_out": 8, "u_out": 9, "u_silu": 10, "res_silu": 11,
          "dbc_out": 13, "mid_part": 14}


def mamba(nc, x_dram, w, tables, ends_at_dram, ends_dram, counts):
    with ExitStack() as ctx:
        sb = lambda name, shape, dt=F32: ctx.enter_context(nc.sbuf_tensor(name, shape, dt))
        sem = lambda name: ctx.enter_context(nc.semaphore(name))
        xt = [sb(f"x_in{k}", [P, CT, T]) for k in range(2)]
        xn, sq, rs, rs2 = sb("xn", [P, CT, T]), sb("sq", [P, CT, T]), sb("rs", [P, T]), sb("rs2", [P, T])
        upre = sb("upre", [P, DT, HALO + T])
        u = [sb(f"u{k}", [P, DT, T]) for k in range(2)]
        sres = [sb(f"sres{k}", [P, DT, T]) for k in range(2)]
        delta, du, yt = sb("delta", [P, DT, T]), sb("du", [P, DT, T]), sb("yt", [P, DT, T])
        soft = yt
        hb = [sb(f"hb{k}", [P, GQ, T]) for k in range(4)]
        da = [sb(f"da{k}", [P, GQ, T]) for k in range(2)]
        bb = [sb(f"bb{k}", [P, GQ, T]) for k in range(2)]
        cb = [sb(f"cb{k}", [P, GQ, T]) for k in range(2)]
        x2, xn2, hst = sb("x2", [P, CT, T]), sb("xn2", [P, CT, T]), sb("hst", [P, T // P, H_F])
        parts = [sb(f"bc_parts{k}", [96, T], BF16) for k in range(2)]
        rest, mid, dtr = sb("bc_rest", [64, T]), sb("bc_mid", [64, T], BF16), sb("dtr", [32, T])
        carry, keep = sb("carry", [P, DT, NS]), sb("keep", [P, CHUNKS + 1])
        w_in, w_x = sb("w_in", [P, CT, 2 * DT * P]), sb("w_x", [P, DT, 64])
        w_dt, w_out = sb("w_dt", [32, DT * P]), sb("w_out", [P, DT, CT * P])
        w_g, att = sb("w_g", [P, CT, H_F]), sb("att", [P, 2, 16])
        w_att = sb("w_att", [P, CT, 2, 16])
        w_conv, diag = sb("w_conv", [P, DT, TAPS]), sb("diag", [P, DT * TAPS, P])
        conv_b, dt_b, skip = sb("conv_b", [P, DT]), sb("dt_b", [P, DT]), sb("skip", [P, DT])
        a_neg, eps = sb("a_neg", [P, DT, NS]), sb("eps", [P, 3])
        ident, mean_w, sel = sb("ident", [P, P]), sb("mean_w", [P, P]), sb("sel", [96, 2 * NS], BF16)
        end_idx, end_pos = sb("end_idx", [P, CW], I32), sb("end_pos", [P, CW], I32)
        chunk_step = sb("chunk_step", [P, CW], I32)
        psy = ctx.enter_context(nc.psum_tensor("psy", [P, DT, T], F32))
        pst = [ctx.enter_context(nc.psum_tensor(f"pst{k}", [P, T], F32)) for k in range(2)]
        psg = [ctx.enter_context(nc.psum_tensor(f"psg{k}", [P, T], F32)) for k in range(2)]

        w_loaded, const, weights_made, setup = sem("w_loaded"), sem("mamba_const"), sem("weights_made"), sem("setup_steps")
        x_loaded = [sem(f"x_loaded{k}") for k in range(2)]
        xres_loaded, x2_stored, xn2_stored, h_stored = sem("xres_loaded"), sem("x2_stored"), sem("xn2_stored"), sem("h_stored")
        pre_full, post_full = sem("pre_psum_full"), sem("post_psum_full")
        centred, squared, rstd_made, normed = sem("centred"), sem("squared"), sem("rstd_made"), sem("normed")
        upre_made, u_made, res_made, dbc_out = sem("upre_made"), sem("u_made"), sem("res_made"), sem("dbc_out")
        rest_made, mid_made, parts_made = sem("rest_made"), sem("mid_made"), sem("parts_made")
        abs_made, relu_made = sem("abs_made"), sem("relu_made")
        soft_made, delta_made, du_made = sem("soft_made"), sem("delta_made"), sem("du_made")
        bc_full, bc_made, da_made = sem("bc_psum_full"), sem("bc_made"), sem("da_made")
        dbu_made, scanned, carried, products = sem("dbu_made"), sem("scanned"), sem("carried"), sem("products")
        summed, y_read, gated = sem("summed"), sem("y_read"), sem("gated")
        x2_made, centred2, squared2, rstd2_made = sem("x2_made"), sem("centred2"), sem("squared2"), sem("rstd2_made")
        normed2, h_out = sem("normed2"), sem("h_out")
        idx_loaded, pos_made, scattered = sem("idx_loaded"), sem("pos_made"), sem("scattered")

        def order(pre, post):
            names = (POST if post else []) + (PRE if pre else [])
            return sorted(names, key=lambda n: PE_AT[n])

        class Body:

            def __init__(self, i, next_pair, par, scan=True, pre=True, post=True, first=0, before=()):
                self.i, self.next_pair, self.par, self.scan, self.pre, self.post = i, next_pair, par, scan, pre, post
                self.first, self.before, self.order = first, before, order(pre, post)

            def slot(self, name):
                return (self.order.index(name) + self.first) % 2

        def bodies(eng, run):
            a, last = len(PRE), PRE[-2:]
            run(Body(-1, 0, 1, scan=False, post=False))
            run(Body(0, 0, 0, post=False, first=a % 2, before=last))
            assert (len(PRE) + len(POST)) % 2 == 0
            with eng.Fori(0, (CHUNKS - 2) // 2) as j:
                run(Body(j * 2 + 1, j + 1, 1, before=last))
                run(Body(j * 2 + 2, j + 1, 0, before=last))
            run(Body(CHUNKS - 1, CHUNKS // 2, 1, pre=False, before=last))
            run(Body(CHUNKS, CHUNKS // 2, 0, scan=False, pre=False, first=len(POST) % 2, before=POST[-2:]))

        sp_passed, pool_passed = sem("m_sp_passed"), sem("m_pool_passed")
        with nc.Block() as block:
            @block.sync
            def _(sp):
                loads = [(w_in, w["in"], "(c p) e -> p c e"), (w_x, w["x"], "(c p) e -> p c e"),
                         (w_out, w["out"], "(c p) e -> p c e"), (w_conv, w["conv"], "(c p) e -> p c e")]
                for t, d, how in loads:
                    sp.dma_start(t[:, :, :], d.rearrange(how, p=P)).then_inc(w_loaded, 16)
                sp.dma_start(w_g[:, :, 0:16], w["gat"].rearrange("(c p) e -> p c e", p=P)).then_inc(w_loaded, 16)
                sp.dma_start(w_dt[:, :], w["dt"]).then_inc(w_loaded, 16)
                sp.dma_start(a_neg[:, :, :], w["a_log"].rearrange("(c p) e -> p c e", p=P)).then_inc(w_loaded, 16)
                for t, d in ((conv_b, w["conv_b"]), (dt_b, w["dt_b"]), (skip, w["skip"])):
                    sp.dma_start(t[:, :], d).then_inc(w_loaded, 16)
                for k in range(2):
                    sp.dma_start(att[:, k, :], w["att"][k:k + 1, :].to_broadcast([P, 16])).then_inc(w_loaded, 16)
                def run(b):
                    i = b.i
                    if b.pre:
                        if not (isinstance(i, int) and i < 1):
                            wait_alone(sp, centred, i, sp_passed)
                        sp.dma_start(xt[1 - b.par][:, :, :], x_dram[bass.ds(i + 1, 1)].rearrange("o p (c t) -> (o p) c t", c=CT)).then_inc(x_loaded[1 - b.par], 16)
                    if b.post:
                        wait_alone(sp, x2_made, i * 2, sp_passed)
                        sp.dma_start(tables["x2"][bass.ds(i - 1, 1)].rearrange("o p (c t) -> (o p) c t", c=CT), x2[:, :, :]).then_inc(x2_stored, 16)
                    if b.post:
                        wait_alone(sp, normed2, i, sp_passed)
                        sp.dma_start(tables["xn2"][bass.ds(i - 1, 1)].rearrange("o p (c t) -> (o p) c t", c=CT), xn2[:, :, :]).then_inc(xn2_stored, 16)
                        wait_alone(sp, h_out, i, sp_passed)
                        rows = bass.ds((i - 1) * T, T)
                        sp.dma_start(tables["src"][rows, :].rearrange("(k p) f -> p k f", p=P), hst[:, :, 0:SRC_F]).then_inc(h_stored, 16)
                        sp.dma_start(tables["dst"][rows, :].rearrange("(k p) f -> p k f", p=P), hst[:, :, SRC_F:H_F]).then_inc(h_stored, 16)
                    if b.scan:
                        if b.post:
                            wait_alone(sp, x2_stored, i * 16, sp_passed)
                            wait_alone(sp, centred2, i, sp_passed)
                        sp.dma_start(x2[:, :, :], x_dram[bass.ds(i, 1)].rearrange("o p (c t) -> (o p) c t", c=CT)).then_inc(xres_loaded, 16)
                bodies(sp, run)
                sp.wait_ge(x2_stored, CHUNKS * 16)
                sp.wait_ge(xn2_stored, CHUNKS * 16)
                sp.wait_ge(h_stored, CHUNKS * 32)

            @block.gpsimd
            def _(pool):
                g = nc.gpsimd
                g.memset(mean_w[:, :], 1.0 / (CT * P)).then_inc(const, 1)
                g.memset(eps[:, 0:1], 1e-6).then_inc(const, 1)
                g.memset(eps[:, 1:2], 1e-5).then_inc(const, 1)
                g.memset(eps[:, 2:3], 1.0).then_inc(const, 1)
                g.memset(carry[:, :, :], 0.0).then_inc(const, 1)
                g.memset(upre[:, :, 0:HALO], 0.0).then_inc(const, 1)
                g.memset(keep[:, :], 1.0).then_inc(const, 1)
                g.memset(ident[:, :], 0.0).then_inc(const, 1)
                g.memset(sel[:, :], 0.0).then_inc(const, 1)
                g.memset(chunk_step[:, :], CHUNK).then_inc(const, 1)
                pool.wait_ge(const, 10)
                g.memset(keep[:, 0:CHUNKS + 1:PER_BATCH], 0.0).then_inc(const, 1)
                g.affine_select(out=ident[:, :], in_=ident[:, :], compare_op=ALU.not_equal, fill=1.0, base=0,
                                pattern=[[-1, P]], channel_multiplier=1).then_inc(const, 1)
                for k in range(3):
                    g.affine_select(out=sel[:, :], in_=sel[:, :], compare_op=ALU.not_equal, fill=1.0, base=-32 * k,
                                    pattern=[[-1, 2 * NS]], channel_multiplier=1).then_inc(const, 1)
                    pool.wait_ge(const, 13 + k)
                g.iota(end_pos[:, :], pattern=[[1, CW]], base=1, channel_multiplier=CW).then_inc(pos_made, 1)
                n_chunks = pool.value_load(counts[0:1, 1:2], min_val=1, max_val=EDGES // CHUNK)
                with pool.Fori(0, n_chunks) as c:
                    g.dma_start(end_idx[:, :], ends_at_dram[bass.ds(c * CHUNK, CHUNK), :].rearrange("(p c) o -> p (c o)", p=P)).then_inc(idx_loaded, 16)
                    wait_alone(pool, idx_loaded, c * 16 + 16, pool_passed)
                    wait_alone(pool, pos_made, c + 1, pool_passed)
                    for k in range(CW):
                        g.indirect_dma_start(ends_dram, bass.IndirectOffsetOnAxis(ap=end_idx[:, k:k + 1].bitcast(U32), axis=0),
                                             end_pos[:, k:k + 1], None, bounds_check=GROUPS + OFF - 1, oob_is_err=False).then_inc(scattered, 16)
                    wait_alone(pool, scattered, c * (16 * CW) + 16 * CW, pool_passed)
                    g.tensor_tensor(end_pos[:, :], end_pos[:, :], chunk_step[:, :], ALU.add).then_inc(pos_made, 1)

            @block.vector
            def _(dve):
                v = nc.vector
                st = Steps(dve, setup)
                dve.wait_ge(w_loaded, 16 * 12)
                dve.wait_ge(const, 15)
                for d in range(DT):
                    for k in range(TAPS):
                        st(v.tensor_scalar(diag[:, d * TAPS + k, :], ident[:, :], w_conv[:, d, k:k + 1], None, ALU.mult))
                for c in range(CT):
                    for k in range(2):
                        st(v.tensor_tensor(w_att[:, c, k, :], w_g[:, c, 0:16], att[:, k, :], ALU.mult))
                st.settle()
                for c in range(CT):
                    (v.tensor_reduce(w_g[:, c, 16:24], w_att[:, c, :, :].rearrange("p k (h e) -> p (k h) e", e=4),
                                       mybir.AxisListType.X, ALU.add)).then_inc(weights_made, 1)
                dve.wait_ge(weights_made, 1 + CT)
                v.tensor_scalar(a_neg[:, :, :], a_neg[:, :, :], -1.0, None, ALU.mult).then_inc(weights_made, 1)

                def piece(b, name):
                    i, n, l = b.i, b.i + 1, b.i - 1
                    if name == "centre":
                        s = b.slot("mean")
                        dve.wait_ge(pre_full, n * 19 + 1)
                        v.tensor_tensor(xn[:, :, :], xt[1 - b.par][:, :, :], psg[s][:, None, :].to_broadcast([P, CT, T]), ALU.subtract).then_inc(centred, 1)
                    elif name == "norm":
                        dve.wait_ge(rstd_made, n * 2 + 2)
                        v.tensor_tensor(xn[:, :, :], xn[:, :, :], rs[:, None, :].to_broadcast([P, CT, T]), ALU.mult).then_inc(normed, 1)
                    elif name == "low_parts":
                        s = b.slot("dbc")
                        dve.wait_ge(dbc_out, n * 2 + 2)
                        v.tensor_tensor(rest[32:64, :], psg[s][32:64, :], parts[1 - b.par][32:64, :], ALU.subtract).then_inc(rest_made, 1)
                    elif name == "lowest_part":
                        dve.wait_ge(mid_made, n * 2 + 2)
                        v.tensor_tensor(parts[1 - b.par][0:32, :], rest[32:64, :], mid[32:64, :], ALU.subtract).then_inc(parts_made, 1)
                    elif name == "delta":
                        dve.wait_ge(soft_made, n + 1)
                        v.tensor_tensor(delta[:, :, :], delta[:, :, :], soft[:, :, :], ALU.add).then_inc(delta_made, 1)
                        dve.wait_ge(delta_made, n + 1)
                        v.tensor_tensor(du[:, :, :], delta[:, :, :], u[1 - b.par][:, :, :], ALU.mult).then_inc(du_made, 1)
                    elif name == "y":
                        for d in range(DT):
                            dve.wait_ge(summed, l * STEPS + STEPS - DT + d + 1)
                            v.scalar_tensor_tensor(yt[:, d, :], u[1 - b.par][:, d, :], skip[:, d:d + 1], psy[:, d, :],
                                                   ALU.mult, ALU.add).then_inc(y_read, 1)
                        dve.wait_ge(y_read, l * 4 + 4)
                        v.tensor_tensor(yt[:, :, :], yt[:, :, :], sres[1 - b.par][:, :, :], ALU.mult).then_inc(gated, 1)
                    elif name == "x2":
                        for c in range(CT):
                            s = b.slot(f"out{c}")
                            dve.wait_ge(post_full, l * 5 + c + 1)
                            if c == 0:
                                dve.wait_ge(xres_loaded, l * 16 + 16)
                            v.tensor_tensor(x2[:, c, :], psg[s][:, :], x2[:, c, :], ALU.add).then_inc(x2_made, 1)
                    elif name == "centre2":
                        s = b.slot("mean2")
                        dve.wait_ge(post_full, l * 5 + 3)
                        v.tensor_tensor(xn2[:, :, :], x2[:, :, :], psg[s][:, None, :].to_broadcast([P, CT, T]), ALU.subtract).then_inc(centred2, 1)
                    elif name == "norm2":
                        dve.wait_ge(rstd2_made, l * 2 + 2)
                        v.tensor_tensor(xn2[:, :, :], xn2[:, :, :], rs2[:, None, :].to_broadcast([P, CT, T]), ALU.mult).then_inc(normed2, 1)

                def inputs(i, s):
                    g, d = divmod(s, DT)
                    if s >= 4 or not (isinstance(i, int) and i == 0):
                        dve.wait_ge(summed, i * STEPS + s - 3)
                    dve.wait_ge(bc_made, i * 32 + 8 * g + GQ)
                    v.tensor_tensor(hb[s % 4][:, :, :], bb[g % 2][:, :, :], du[:, d:d + 1, :].to_broadcast([P, GQ, T]), ALU.mult).then_inc(dbu_made, 1)

                def scans(i, s):
                    g, d = divmod(s, DT)
                    dve.wait_ge(dbu_made, i * STEPS + s + 1)
                    if not (isinstance(i, int) and i == 0):
                        dve.wait_ge(carried, (i - 1) * STEPS + s + 1)
                    for q in range(GQ):
                        dve.wait_ge(da_made, i * 64 + GQ * s + q + 1)
                        v.tensor_tensor_scan(hb[s % 4][:, q, :], da[s % 2][:, q, :], hb[s % 4][:, q, :],
                                             carry[:, d, GQ * g + q:GQ * g + q + 1], ALU.mult, ALU.add).then_inc(scanned, 1)

                def carries(b, s):
                    g, d = divmod(s, DT)
                    i = b.i
                    dve.wait_ge(scanned, i * 64 + GQ * (s + 1))
                    v.tensor_scalar(carry[:, d, GQ * g:GQ * (g + 1)], hb[s % 4][:, :, T - 1], keep[:, bass.ds(i + 1, 1)], None,
                                    ALU.mult).then_inc(carried, 1)

                def outputs(i, s):
                    g, d = divmod(s, DT)
                    dve.wait_ge(carried, i * STEPS + s + 1)
                    dve.wait_ge(bc_made, i * 32 + 8 * (g + 1))
                    v.tensor_tensor(hb[s % 4][:, :, :], hb[s % 4][:, :, :], cb[g % 2][:, :, :], ALU.mult).then_inc(products, 1)

                def run(b):
                    at = lambda s: [n for n, k in VEC_AT.items() if k == s and (b.post if n.endswith("2") else b.pre)]
                    if b.post:
                        piece(b, "y")
                    if b.scan:
                        dve.wait_ge(du_made, b.i + 1)
                        inputs(b.i, 0)
                        scans(b.i, 0)
                        for s in range(STEPS):
                            if s + 1 < STEPS:
                                inputs(b.i, s + 1)
                            carries(b, s)
                            if s + 1 < STEPS:
                                scans(b.i, s + 1)
                            outputs(b.i, s)
                            for name in at(s):
                                piece(b, name)
                    else:
                        for s in range(STEPS):
                            for name in at(s):
                                piece(b, name)
                    if b.post:
                        dve.wait_ge(xn2_stored, b.i * 16)
                    if b.pre:
                        piece(b, "delta")
                bodies(dve, run)

            @block.tensor
            def _(pe):
                mm = nc.tensor.matmul
                pe.wait_ge(weights_made, 2 + CT)
                pe.wait_ge(const, 15)

                def read(name, n, l):
                    tile = int(name[-1]) if name[-1].isdigit() else 0
                    for prefix, made, value in (
                            ("mean2", centred2, l + 1), ("var2", rstd2_made, l * 2 + 1), ("h", h_out, l + 1),
                            ("out", x2_made, l * 2 + tile + 1), ("mean", centred, n + 1), ("var", rstd_made, n * 2 + 1),
                            ("u", upre_made, n * 5 + tile + 1), ("conv", u_made, n * 4 + tile + 1),
                            ("res", res_made, n * 4 + tile + 1), ("dbc", rest_made, n + 1),
                            ("dt", relu_made, n * 4 + tile + 1)):
                        if name.startswith(prefix):
                            pe.wait_ge(made, value)
                            if prefix == "dt":
                                pe.wait_ge(abs_made, n * 5 + tile + 1)
                            return

                def use(b, name):
                    i, n, l = b.i, b.i + 1, b.i - 1
                    k = b.order.index(name)
                    ps = psg[b.slot(name)]
                    nxt = 1 - b.par
                    if k >= 2:
                        read(b.order[k - 2], n, l)
                    elif b.before:
                        read(b.before[k], i, l - 1)
                    kind, d = (name[:-1], int(name[-1])) if name[-1].isdigit() and name not in ("mean2", "var2") else (name, 0)
                    if kind == "mean":
                        pe.wait_ge(x_loaded[nxt], b.next_pair * 16 + 16)
                        terms = [(mean_w[:, :], xt[nxt][:, c, :]) for c in range(CT)]
                    elif kind == "var":
                        pe.wait_ge(squared, n + 1)
                        terms = [(mean_w[:, :], sq[:, c, :]) for c in range(CT)]
                    elif kind == "u" or kind == "res":
                        pe.wait_ge(normed, n + 1)
                        e = (d + DT * (kind == "res")) * P
                        terms = [(w_in[:, c, e:e + P], xn[:, c, :]) for c in range(CT)]
                    elif kind == "conv":
                        pe.wait_ge(upre_made, n * 5 + d + 1)
                        terms = [(diag[:, d * TAPS + t, :], upre[:, d, t:t + T]) for t in range(TAPS)]
                    elif kind == "dbc":
                        pe.wait_ge(u_made, n * 4 + 4)
                        terms = [(w_x[:, c, :], u[nxt][:, c, :]) for c in range(DT)]
                        ps = ps[0:64, :]
                    elif kind == "dt":
                        pe.wait_ge(dbc_out, n * 2 + 1)
                        terms = [(w_dt[:, d * P:(d + 1) * P], dtr[:, :])]
                    elif kind == "out":
                        pe.wait_ge(gated, l + 1)
                        terms = [(w_out[:, c, d * P:(d + 1) * P], yt[:, c, :]) for c in range(DT)]
                    elif kind == "mean2":
                        pe.wait_ge(x2_made, l * 2 + 2)
                        terms = [(mean_w[:, :], x2[:, c, :]) for c in range(CT)]
                    elif kind == "var2":
                        pe.wait_ge(squared2, l + 1)
                        terms = [(mean_w[:, :], sq[:, c, :]) for c in range(CT)]
                    elif kind == "h":
                        pe.wait_ge(normed2, l + 1)
                        for t in range(T // P):
                            for c in range(CT):
                                last = mm(ps[:, t * H_F:(t + 1) * H_F], xn2[:, c, t * P:(t + 1) * P], w_g[:, c, :],
                                          start=(c == 0), stop=(c == CT - 1))
                        last.then_inc(post_full, 1)
                        return
                    out = ps if kind == "dbc" else ps[:, :]
                    for k, (a, x) in enumerate(terms):
                        last = mm(out, a, x, start=(k == 0), stop=(k == len(terms) - 1))
                    last.then_inc(pre_full if name in PRE else post_full, 1)

                def broadcast(b, g):
                    i = b.i
                    if g == 0:
                        pe.wait_ge(parts_made, i + 1)
                        pe.wait_ge(mid_made, i * 2 + 2)
                    for k in range(2 * GQ):
                        n = GQ * g + k if k < GQ else NS + GQ * g + k - GQ
                        t = 8 * g + k
                        if t >= 2 or not (isinstance(i, int) and i == 0):
                            pe.wait_ge(bc_made, i * 32 + t - 1)
                        mm(pst[t % 2][:, :], sel[:, n:n + 1].to_broadcast([96, P]), parts[b.par][:, :], start=True, stop=True).then_inc(bc_full, 1)

                def total(b, s):
                    g, d = divmod(s, DT)
                    i = b.i
                    pe.wait_ge(products, i * STEPS + s + 1)
                    if g == 0 and not (isinstance(i, int) and i == 0):
                        pe.wait_ge(y_read, (i - 1) * 4 + d + 1)
                    for q in range(GQ):
                        last = mm(psy[:, d, :], ident[:, :], hb[s % 4][:, q, :], start=(g == 0 and q == 0), stop=(g == NGR - 1 and q == GQ - 1))
                    last.then_inc(summed, 1)

                def run(b):
                    if b.scan:
                        broadcast(b, 0)
                    for s in range(STEPS):
                        if b.scan and s % DT == 1 and s // DT + 1 < NGR:
                            broadcast(b, s // DT + 1)
                        for name in b.order:
                            if PE_AT[name] == s:
                                use(b, name)
                        if b.scan:
                            total(b, s)
                bodies(pe, run)

            @block.scalar
            def _(act):
                f = nc.scalar.activation
                act.wait_ge(w_loaded, 16 * 12)
                act.wait_ge(const, 15)
                f(a_neg[:, :, :], a_neg[:, :, :], ACT.Exp).then_inc(weights_made, 1)
                act.wait_ge(weights_made, 2 + CT)

                def piece(b, name):
                    i, n, l = b.i, b.i + 1, b.i - 1
                    nxt = 1 - b.par
                    if name == "square":
                        act.wait_ge(centred, n + 1)
                        if b.post:
                            act.wait_ge(post_full, l * 5 + 4)
                        f(sq[:, :, :], xn[:, :, :], ACT.Square).then_inc(squared, 1)
                    elif name == "rstd":
                        s = b.slot("var")
                        act.wait_ge(pre_full, n * 19 + 2)
                        f(rs[:, :], psg[s][:, :], ACT.Ln, bias=eps[:, 0:1]).then_inc(rstd_made, 1)
                        act.wait_ge(rstd_made, n * 2 + 1)
                        f(rs[:, :], rs[:, :], ACT.Exp, scale=-0.5).then_inc(rstd_made, 1)
                    elif name == "u_out":
                        for d in range(DT):
                            s = b.slot(f"u{d}")
                            act.wait_ge(pre_full, n * 19 + 3 + d)
                            f(upre[:, d, HALO:HALO + T], psg[s][:, :], ACT.Copy).then_inc(upre_made, 1)
                    elif name == "u_silu":
                        for d in range(DT):
                            s = b.slot(f"conv{d}")
                            act.wait_ge(pre_full, n * 19 + 7 + d)
                            if b.post and d == 0:
                                act.wait_ge(gated, l + 1)
                            f(u[nxt][:, d, :], psg[s][:, :], ACT.Silu, bias=conv_b[:, d:d + 1]).then_inc(u_made, 1)
                        f(upre[:, :, 0:HALO], upre[:, :, T:T + HALO], ACT.Copy, scale=keep[:, bass.ds(n + 1, 1)] if not isinstance(n, int) or n + 1 <= CHUNKS else 0.0).then_inc(upre_made, 1)
                    elif name == "res_silu":
                        for d in range(DT):
                            s = b.slot(f"res{d}")
                            act.wait_ge(pre_full, n * 19 + 11 + d)
                            f(sres[nxt][:, d, :], psg[s][:, :], ACT.Silu).then_inc(res_made, 1)
                    elif name == "dbc_out":
                        s = b.slot("dbc")
                        act.wait_ge(pre_full, n * 19 + 15)
                        f(dtr[:, :], psg[s][0:32, :], ACT.Copy).then_inc(dbc_out, 1)
                        f(parts[nxt][32:64, :], psg[s][32:64, :], ACT.Copy).then_inc(dbc_out, 1)
                    elif name == "mid_part":
                        act.wait_ge(rest_made, n + 1)
                        f(mid[32:64, :], rest[32:64, :], ACT.Copy).then_inc(mid_made, 1)
                        act.wait_ge(mid_made, n * 2 + 1)
                        f(parts[nxt][64:96, :], mid[32:64, :], ACT.Copy).then_inc(mid_made, 1)
                    elif name == "soft":
                        for d in range(DT):
                            s = b.slot(f"dt{d}")
                            act.wait_ge(pre_full, n * 19 + 16 + d)
                            if b.post and d == 0:
                                act.wait_ge(post_full, l * 5 + 2)
                            f(soft[:, d, :], psg[s][:, :], ACT.Abs, bias=dt_b[:, d:d + 1]).then_inc(abs_made, 1)
                            f(delta[:, d, :], psg[s][:, :], ACT.Relu, bias=dt_b[:, d:d + 1]).then_inc(relu_made, 1)
                            act.wait_ge(relu_made, n * 4 + d + 1)
                        f(soft[:, :, :], soft[:, :, :], ACT.Exp, scale=-1.0).then_inc(abs_made, 1)
                        act.wait_ge(abs_made, n * 5 + 5)
                        f(soft[:, :, :], soft[:, :, :], ACT.Ln, bias=eps[:, 2:3]).then_inc(soft_made, 1)
                    elif name == "square2":
                        act.wait_ge(centred2, l + 1)
                        f(sq[:, :, :], xn2[:, :, :], ACT.Square).then_inc(squared2, 1)
                    elif name == "rstd2":
                        s = b.slot("var2")
                        act.wait_ge(post_full, l * 5 + 4)
                        f(rs2[:, :], psg[s][:, :], ACT.Ln, bias=eps[:, 1:2]).then_inc(rstd2_made, 1)
                        act.wait_ge(rstd2_made, l * 2 + 1)
                        f(rs2[:, :], rs2[:, :], ACT.Exp, scale=-0.5).then_inc(rstd2_made, 1)
                    elif name == "h_out":
                        s = b.slot("h")
                        act.wait_ge(post_full, l * 5 + 5)
                        f(hst[:, :, :], psg[s][:, 0:T // P * H_F], ACT.Copy).then_inc(h_out, 1)

                def spread(b, g, which):
                    i = b.i
                    if g >= 2:
                        act.wait_ge(products, i * STEPS + (g - 1) * DT)
                    elif not (isinstance(i, int) and i == 0):
                        act.wait_ge(products, (i - 1) * STEPS + (g + 3) * DT)
                    dst = (bb, cb)[which][g % 2]
                    for q in range(GQ):
                        t = 8 * g + GQ * which + q
                        act.wait_ge(bc_full, i * 32 + t + 1)
                        f(dst[:, q, :], pst[t % 2][:, :], ACT.Copy).then_inc(bc_made, 1)

                def decays(b, s):
                    g, d = divmod(s, DT)
                    i = b.i
                    if s >= 2:
                        act.wait_ge(scanned, i * 64 + GQ * (s - 1))
                    elif not (isinstance(i, int) and i == 0):
                        act.wait_ge(scanned, (i - 1) * 64 + GQ * (s + 15))
                    for q in range(GQ):
                        n = GQ * g + q
                        f(da[s % 2][:, q, :], delta[:, d, :], ACT.Exp, scale=a_neg[:, d, n:n + 1]).then_inc(da_made, 1)

                def run(b):
                    at = lambda s: [n for n, k in ACT_AT.items() if k == s and (b.post if n in ("square2", "rstd2", "h_out") else b.pre)]
                    if b.scan:
                        spread(b, 0, 0)
                        act.wait_ge(delta_made, b.i + 1)
                    for s in range(STEPS):
                        if b.scan:
                            decays(b, s)
                            if s == 0:
                                spread(b, 0, 1)
                            if s % DT == 2 and s // DT + 1 < NGR:
                                spread(b, s // DT + 1, 0)
                                spread(b, s // DT + 1, 1)
                        for name in at(s):
                            piece(b, name)
                    if b.post:
                        act.wait_ge(h_stored, b.i * 32)
                    if b.pre:
                        piece(b, "soft")
                bodies(act, run)

HEADS = 4
EXPERTS = 4
GH = HEADS * EXPERTS
SEG_F = GH + HEADS + HEADS
NT = NODES // P
BIG = 1e30
PEAKS_AT, PEAK_LANES_AT, SUMS_AT, SUM_LANES_AT, GRAPH_STEPS = 12, 14, 54, 56, 78
AX = mybir.AxisListType.X


def attention(nc, keys_dram, src_dram, dst_dram, ends_dram, tables, w, seg_dram, gates_dram, counts):
    with ExitStack() as ctx:
        sb = lambda name, shape, dt=F32: ctx.enter_context(nc.sbuf_tensor(name, shape, dt))
        sem = lambda name: ctx.enter_context(nc.semaphore(name))
        pair = lambda name, shape, dt=F32: [sb(f"{name}{k}", shape, dt) for k in range(2)]
        ident, ones = sb("g_ident", [P, P]), sb("g_ones", [P, P])
        zero_row, eps = sb("zero_row", [P, CW]), sb("g_eps", [P, 1])
        ends_i = sb("ends_i", [P, 2, NT], I32)
        ends = sb("ends_f", [P, 2, NT + 1])
        tail_row, last = sb("tail_row", [1, 2 * P]), sb("carry_row", [1, 2 * P + 1])
        node_q = sb("node_q", [P, 3, NT])
        end_idx = sb("g_end_idx", [P, NT], I32)
        has0, none0, none1 = sb("has0", [P, NT]), sb("none0", [P, NT]), sb("none1", [P, NT])
        count1 = sb("count1", [P, NT])
        s_idx, d_idx = pair("s_idx", [P, CW], I32), pair("d_idx", [P, CW], I32)
        keys, prev = pair("keys", [P, CW], I32), pair("prev_keys", [P, CW], I32)
        grow, arow = pair("src_rows", [P, CW, SRC_F]), pair("dst_rows", [P, CW, DST_F])
        start, fresh, same, seen = (sb(n, [P, CW]) for n in ("start", "fresh", "same", "seen"))
        peak = sb("peak", [P, HEADS, CW + 1])
        tails, tail_t, lanes = sb("tails", [P, 2 * HEADS]), sb("tails_t", [HEADS, 2 * P]), sb("lane_peaks", [HEADS, P + 1])
        score = sb("score", [P, 3, HEADS * CW])
        expo = sb("expo", [P, 2, HEADS * CW])
        vals, decay = sb("vals", [P, SRC_F, CW]), sb("decay", [P, HEADS, CW])
        prod = sb("prod", [P, HEADS, CW])
        seg = pair("seg", [P, CW, SEG_F])
        stails, stail_t = sb("stails", [P, 2 * SRC_F]), sb("stails_t", [SRC_F, 2 * P])
        slanes, scarry = sb("lane_sums", [SRC_F, P + 1]), sb("scarry", [P, SRC_F])
        psa = ctx.enter_context(nc.psum_tensor("ps_tails", [P, 512], F32))
        psb = ctx.enter_context(nc.psum_tensor("ps_back", [P, 512], F32))
        psc = [ctx.enter_context(nc.psum_tensor(f"ps_nodes{k}", [P, 512], F32)) for k in range(4)]

        const, ends_loaded = sem("g_const"), sem("ends_loaded")
        node_steps, graph_steps, node_t = sem("node_steps"), sem("graph_steps"), sem("node_transposed")
        idx_loaded, keys_loaded = [sem(f"g_idx_loaded{k}") for k in range(2)], [sem(f"keys_loaded{k}") for k in range(2)]
        gathered = [sem(f"gathered{k}") for k in range(2)]
        started, seg_made = sem("starts_made"), sem("seg_made")
        tails_t, weights = sem("tails_transposed"), sem("weights_exp")
        expo_made = sem("expo_made")
        seg_stored = [sem(f"seg_stored{k}") for k in range(2)]

        def chunks(eng, run):
            n = eng.value_load(counts[0:1, 0:1], min_val=3, max_val=EDGES // CHUNK)
            run(0, 0)
            run(1, 1)
            with eng.Fori(2, n, 2) as c:
                c = c.with_bounds(min_val=2, max_val=EDGES // CHUNK - 2)
                run(c, 0)
                run(c + 1, 1)

        sp_passed, pool_passed, pe_passed = sem("g_sp_passed"), sem("g_pool_passed"), sem("g_pe_passed")
        with nc.Block() as block:
            @block.gpsimd
            def _(pool):
                g = nc.gpsimd
                g.memset(ones[:, :], 1.0).then_inc(const, 1)
                g.memset(zero_row[:, :], 0.0).then_inc(const, 1)
                g.memset(last[:, 0:1], 0.0).then_inc(const, 1)
                g.memset(lanes[:, 0:1], -BIG).then_inc(const, 1)
                g.memset(slanes[:, 0:1], 0.0).then_inc(const, 1)
                pool.wait_ge(const, 1)
                g.affine_select(out=ident[:, :], in_=ones[:, :], compare_op=ALU.is_equal, fill=0.0, base=0,
                                pattern=[[-1, P]], channel_multiplier=1).then_inc(const, 1)

                def run(n, par):
                    first = isinstance(n, int)
                    wait_alone(pool, idx_loaded[par], 32 if first else (n - par) * 16 + 32, pool_passed)
                    if not first:
                        wait_alone(pool, seg_made, n - 1, pool_passed)
                    for k in range(CW):
                        g.indirect_dma_start(grow[par][:, k, :], None, tables["src"], bass.IndirectOffsetOnAxis(ap=s_idx[par][:, k:k + 1].bitcast(U32), axis=0)).then_inc(gathered[par], 16)
                        g.indirect_dma_start(arow[par][:, k, :], None, tables["dst"], bass.IndirectOffsetOnAxis(ap=d_idx[par][:, k:k + 1].bitcast(U32), axis=0)).then_inc(gathered[par], 16)
                chunks(pool, run)

            @block.sync
            def _(sp):
                sp.dma_start(ends_i[:, :, :], ends_dram[OFF:OFF + GROUPS, :].rearrange("(k q c) o -> q k (c o)", k=2, q=P)).then_inc(ends_loaded, 16)

                def run(n, par):
                    first = isinstance(n, int)
                    if not first:
                        wait_alone(sp, gathered[par], (n - par) * (16 * CW), sp_passed)
                        wait_alone(sp, started, n - 1, sp_passed)
                    at = lambda t, off: t[bass.ds(n * CHUNK + off, CHUNK), :].rearrange("(p c) o -> p (c o)", p=P)
                    sp.dma_start(s_idx[par][:, :], at(src_dram, 0)).then_inc(idx_loaded[par], 16)
                    sp.dma_start(d_idx[par][:, :], at(dst_dram, 0)).then_inc(idx_loaded[par], 16)
                    sp.dma_start(keys[par][:, :], at(keys_dram, 1)).then_inc(keys_loaded[par], 16)
                    sp.dma_start(prev[par][:, :], at(keys_dram, 0)).then_inc(keys_loaded[par], 16)
                chunks(sp, run)

            @block.vector
            def _(dve):
                v = nc.vector
                st = Steps(dve, node_steps)

                def do(instruction):
                    st(instruction)
                    st.settle()
                dve.wait_ge(ends_loaded, 16)
                dve.wait_ge(const, 6)
                do(v.tensor_copy(node_q[:, 0:2, :], ends_i[:, :, :]))
                for k in range(2):
                    do(v.tensor_tensor_scan(ends[:, k, 1:NT + 1], node_q[:, k, :], node_q[:, k, :], 0.0, ALU.max, ALU.max))
                ends_tail = st.n
                dve.wait_ge(node_t, 2)
                do(v.tensor_copy(tail_row[:, :], psa[0:1, 0:2 * P]))
                do(v.tensor_tensor_scan(last[:, 1:2 * P + 1], tail_row[:, :], tail_row[:, :], last[:, 0:1], ALU.max, ALU.max))
                dve.wait_ge(node_t, 4)
                do(v.tensor_copy(ends[:, :, 0], psb[:, 0:2]))
                for k in range(2):
                    do(v.tensor_scalar(ends[:, k, 1:NT + 1], ends[:, k, 1:NT + 1], ends[:, k, 0:1], None, ALU.max))
                do(v.tensor_tensor(node_q[:, 1:3, :], ends[:, :, 1:NT + 1], ends[:, :, 0:NT], ALU.subtract))
                do(v.tensor_scalar(node_q[:, 0, :], ends[:, 0, 1:NT + 1], -1.0, 0.0, ALU.add, ALU.max))
                dve.wait_ge(node_t, 7)
                do(v.tensor_copy(end_idx[:, :], psc[0][:, 0:NT]))
                do(v.tensor_scalar(has0[:, :], psc[1][:, 0:NT], 0.0, None, ALU.is_gt))
                do(v.tensor_copy(count1[:, :], psc[2][:, 0:NT]))
                do(v.tensor_scalar(none0[:, :], has0[:, :], -1.0, BIG, ALU.add, ALU.mult))
                do(v.tensor_scalar(none1[:, :], count1[:, :], 0.0, None, ALU.is_gt))
                do(v.tensor_scalar(none1[:, :], none1[:, :], -1.0, BIG, ALU.add, ALU.mult))

                def run(n, par):
                    st = Steps(dve, graph_steps, n * GRAPH_STEPS)
                    first = isinstance(n, int)
                    pairs = 0 if first else n - par

                    def do(instruction):
                        st(instruction)
                        st.settle()
                    gf = grow[par][:, :, :].rearrange("p c f -> p f c")
                    af = arow[par][:, :, :].rearrange("p c f -> p f c")
                    a_src = gf[:, GH:SRC_F, :]
                    out = seg[par][:, :, :].rearrange("p c f -> p f c")
                    heads = lambda t: t.rearrange("p (h c) -> p h c", h=HEADS)
                    dve.wait_ge(keys_loaded[par], pairs * 16 + 32)
                    st(v.tensor_scalar(keys[par][:, :], keys[par][:, :], SRC_BITS, None, ALU.logical_shift_right))
                    do(v.tensor_scalar(prev[par][:, :], prev[par][:, :], SRC_BITS, None, ALU.logical_shift_right))
                    v.tensor_tensor(start[:, :], keys[par][:, :], prev[par][:, :], ALU.not_equal).then_inc(started, 1)
                    dve.wait_ge(started, n + 1)
                    st(v.tensor_scalar(fresh[:, :], start[:, :], -BIG, None, ALU.mult))
                    st(v.tensor_scalar(same[:, :], start[:, :], -1.0, 1.0, ALU.mult, ALU.add))
                    do(v.tensor_tensor_scan(seen[:, :], start[:, :], start[:, :], 0.0, ALU.max, ALU.max))
                    do(v.tensor_scalar(seen[:, :], seen[:, :], -BIG, None, ALU.mult))
                    dve.wait_ge(gathered[par], pairs * (16 * CW) + 32 * CW)
                    for h in range(HEADS):
                        st(v.tensor_tensor_scan(peak[:, h, 1:CW + 1], fresh[:, :], a_src[:, h, :], -BIG, ALU.add, ALU.max))
                    st.settle()
                    st(v.tensor_copy(tails[:, 0:HEADS], peak[:, :, CW]))
                    st(v.tensor_copy(tails[:, HEADS:2 * HEADS], seen[:, CW - 1:CW].to_broadcast([P, HEADS])))
                    dve.wait_ge(tails_t, n * 6 + 2)
                    do(v.tensor_copy(tail_t[:, :], psa[0:HEADS, 0:2 * P]))
                    do(v.tensor_tensor_scan(lanes[:, 1:P + 1], tail_t[:, P:2 * P], tail_t[:, 0:P], lanes[:, 0:1], ALU.add, ALU.max))
                    dve.wait_ge(tails_t, n * 6 + 3)
                    st(v.tensor_copy(peak[:, :, 0], psb[:, 0:HEADS]))
                    do(v.tensor_copy(lanes[:, 0:1], lanes[:, P:P + 1]))
                    for h in range(HEADS):
                        st(v.scalar_tensor_tensor(peak[:, h, 1:CW + 1], seen[:, :], peak[:, h, 0:1], peak[:, h, 1:CW + 1], ALU.add, ALU.max))
                    st.settle()
                    st(v.tensor_tensor(heads(score[:, 0, :]), a_src, af, ALU.add))
                    st(v.tensor_tensor(heads(score[:, 1, :]), peak[:, :, 1:CW + 1], af, ALU.add))
                    do(v.tensor_tensor(heads(score[:, 2, :]), peak[:, :, 0:CW], af, ALU.add))
                    do(v.scalar_tensor_tensor(score[:, :, :], score[:, :, :], 0.2, score[:, :, :], ALU.mult, ALU.max))
                    do(v.tensor_tensor(expo[:, :, :], score[:, 0:3:2, :], score[:, 1:2, :].to_broadcast([P, 2, HEADS * CW]), ALU.subtract))
                    v.tensor_scalar(expo[:, :, :], expo[:, :, :], 0.0, None, ALU.min).then_inc(expo_made, 1)
                    dve.wait_ge(weights, n * 2 + 2)
                    st(v.tensor_tensor(decay[:, :, :], decay[:, :, :], same[:, None, :].to_broadcast([P, HEADS, CW]), ALU.mult))
                    per_expert = lambda t: t[:, :, None, :].to_broadcast([P, HEADS, EXPERTS, CW])
                    do(v.tensor_tensor(vals[:, 0:GH, :].rearrange("p (h e) c -> p h e c", h=HEADS), per_expert(vals[:, GH:SRC_F, :]),
                                       gf[:, 0:GH, :].rearrange("p (h e) c -> p h e c", h=HEADS), ALU.mult))
                    if not first:
                        dve.wait_ge(seg_stored[par], pairs * 8)
                    for f in range(SRC_F):
                        h = f // EXPERTS if f < GH else f - GH
                        st(v.tensor_tensor_scan(out[:, f, :], decay[:, h, :], vals[:, f, :], 0.0, ALU.mult, ALU.add))
                    for h in range(HEADS):
                        st(v.tensor_tensor_scan(prod[:, h, :], decay[:, h, :], zero_row[:, :], 1.0, ALU.mult, ALU.add))
                    st.settle()
                    st(v.tensor_copy(stails[:, 0:SRC_F], out[:, 0:SRC_F, CW - 1]))
                    st(v.tensor_copy(stails[:, SRC_F:SRC_F + GH].rearrange("p (h e) -> p h e", h=HEADS), prod[:, :, CW - 1:CW].to_broadcast([P, HEADS, EXPERTS])))
                    st(v.tensor_copy(stails[:, SRC_F + GH:2 * SRC_F], prod[:, :, CW - 1]))
                    dve.wait_ge(tails_t, n * 6 + 5)
                    do(v.tensor_copy(stail_t[:, :], psa[0:SRC_F, 0:2 * P]))
                    do(v.tensor_tensor_scan(slanes[:, 1:P + 1], stail_t[:, P:2 * P], stail_t[:, 0:P], slanes[:, 0:1], ALU.mult, ALU.add))
                    dve.wait_ge(tails_t, n * 6 + 6)
                    st(v.tensor_copy(scarry[:, :], psb[:, 0:SRC_F]))
                    do(v.tensor_copy(slanes[:, 0:1], slanes[:, P:P + 1]))
                    for f in range(SRC_F):
                        h = f // EXPERTS if f < GH else f - GH
                        st(v.scalar_tensor_tensor(out[:, f, :], prod[:, h, :], scarry[:, f:f + 1], out[:, f, :], ALU.mult, ALU.add))
                    st.settle()
                    v.tensor_copy(out[:, SRC_F:SEG_F, :], peak[:, :, 1:CW + 1]).then_inc(seg_made, 1)
                    dve.wait_ge(seg_made, n + 1)
                    assert st.n == GRAPH_STEPS, st.n
                chunks(dve, run)

            @block.tensor
            def _(pe):
                t = nc.tensor.transpose
                pe.wait_ge(const, 6)
                pe.wait_ge(node_steps, 3)
                for k in range(2):
                    t(psa[0:1, k * P:(k + 1) * P], ends[:, k, NT:NT + 1], ident[:, :]).then_inc(node_t, 1)
                pe.wait_ge(node_steps, 5)
                for k in range(2):
                    t(psb[:, k:k + 1], last[0:1, k * P:(k + 1) * P], ident[0:1, 0:1]).then_inc(node_t, 1)
                pe.wait_ge(node_steps, 10)
                for k in range(3):
                    t(psc[k][:, 0:NT], node_q[:, k, :], ident[:, :]).then_inc(node_t, 1)

                def run(n, par):
                    base = n * GRAPH_STEPS
                    pe.wait_ge(graph_steps, base + PEAKS_AT)
                    for k in range(2):
                        t(psa[0:HEADS, k * P:(k + 1) * P], tails[:, k * HEADS:(k + 1) * HEADS], ident[:, :]).then_inc(tails_t, 1)
                    wait_alone(pe, graph_steps, base + PEAK_LANES_AT, pe_passed)
                    t(psb[:, 0:HEADS], lanes[:, 0:P], ident[0:HEADS, 0:HEADS]).then_inc(tails_t, 1)
                    pe.wait_ge(graph_steps, base + SUMS_AT)
                    for k in range(2):
                        t(psa[0:SRC_F, k * P:(k + 1) * P], stails[:, k * SRC_F:(k + 1) * SRC_F], ident[:, :]).then_inc(tails_t, 1)
                    wait_alone(pe, graph_steps, base + SUM_LANES_AT, pe_passed)
                    t(psb[:, 0:SRC_F], slanes[:, 0:P], ident[0:SRC_F, 0:SRC_F]).then_inc(tails_t, 1)
                chunks(pe, run)

            @block.scalar
            def _(act):
                def run(n, par):
                    act.wait_ge(expo_made, n + 1)
                    if isinstance(n, int) and n == 0:
                        pass
                    for k, dst in enumerate((vals[:, GH:SRC_F, :], decay[:, :, :])):
                        nc.scalar.activation(dst, expo[:, k, :].rearrange("p (h c) -> p h c", h=HEADS), ACT.Exp).then_inc(weights, 1)
                    act.wait_ge(seg_made, n + 1)
                    act.dma_start(seg_dram[bass.ds(n * CHUNK, CHUNK), :].rearrange("(p c) f -> p (c f)", p=P),
                                  seg[par][:, :, :].rearrange("p c f -> p (c f)").bitcast(I32)).then_inc(seg_stored[par], 16)
                    if par == 1:
                        pairs = 0 if isinstance(n, int) else n - 1
                        for k in range(2):
                            act.wait_ge(seg_stored[k], pairs * 8 + 16)
                chunks(act, run)

        gate_nodes(nc, ctx, sb, sem, ident, eps, end_idx, has0, none0, none1, count1, psc, seg_dram, tables, w, gates_dram)


def gate_nodes(nc, ctx, sb, sem, ident, eps, end_idx, has0, none0, none1, count1, psc, seg_dram, tables, w, gates_dram):
    K4 = NT * HEADS
    last_row, gamma, beta, bias = sb("last_row", [P, SRC_F]), sb("gamma", [P, GH]), sb("beta", [P, GH]), sb("b_gat", [P, GH])
    rows, node, ad = sb("seg_rows", [P, NT, SEG_F]), sb("node_rows", [P, NT, SRC_F]), sb("node_dst", [P, NT, DST_F])
    a4 = sb("node_scores", [P, 4, K4])
    wts = sb("node_weights", [P, 3, K4])
    den, agg, tmp = sb("den", [P, K4]), sb("agg", [P, NT * GH]), sb("agg_tmp", [P, NT * GH])
    mean, var = sb("node_mean", [P, NT]), sb("node_var", [P, NT])
    sc, ties = sb("expert_scores", [P, K4]), sb("ties", [P, EXPERTS * EXPERTS])
    beats, even, rank, top = sb("beats", [P, NT * GH]), sb("even", [P, NT * GH]), sb("rank", [P, K4]), sb("top", [P, NT])
    gt = sb("gates_t", [EXPERTS, NODES])
    loaded, gathered, steps, exps = sem("node_loaded"), sem("seg_gathered"), sem("gate_steps"), sem("node_exps")
    var_made, gates_t, gates_out, stored = sem("var_made"), sem("gates_transposed"), sem("gates_out"), sem("gates_stored")
    tie_made, weights_ready, gates_made = sem("ties_made"), sem("node_exponents"), sem("gates_made")

    with nc.Block() as block:
        @block.sync
        def _(sp):
            sp.dma_start(node[:, :, :], tables["src"].rearrange("(k p) f -> p k f", p=P)).then_inc(loaded, 16)
            sp.dma_start(ad[:, :, :], tables["dst"].rearrange("(k p) f -> p k f", p=P)).then_inc(loaded, 16)
            sp.dma_start(last_row[:, :], tables["src"][NODES - 1:NODES, :].to_broadcast([P, SRC_F])).then_inc(loaded, 16)
            for t, d in ((gamma, w["gamma"]), (beta, w["beta"]), (bias, w["b_gat"])):
                sp.dma_start(t[:, :], d.to_broadcast([P, GH])).then_inc(loaded, 16)
            sp.wait_ge(gates_out, NT // 4)
            sp.dma_start(gates_dram, gt[:, :]).then_inc(stored, 16)
            sp.wait_ge(stored, 16)

        @block.gpsimd
        def _(pool):
            g = nc.gpsimd
            g.memset(eps[:, :], 1e-5).then_inc(tie_made, 1)
            g.memset(ties[:, :], 1.0).then_inc(tie_made, 1)
            pool.wait_ge(tie_made, 2)
            g.affine_select(out=ties[:, :].rearrange("p (e j) -> p e j", j=EXPERTS), in_=ties[:, :].rearrange("p (e j) -> p e j", j=EXPERTS),
                            compare_op=ALU.is_gt, fill=0.0, base=0, pattern=[[1, EXPERTS], [-1, EXPERTS]], channel_multiplier=0).then_inc(tie_made, 1)
            for k in range(NT):
                g.indirect_dma_start(rows[:, k, :].bitcast(I32), None, seg_dram, bass.IndirectOffsetOnAxis(ap=end_idx[:, k:k + 1].bitcast(U32), axis=0)).then_inc(gathered, 16)

        @block.vector
        def _(dve):
            v = nc.vector
            st = Steps(dve, steps)

            def do(instruction):
                st(instruction)
                st.settle()
            kh = lambda t: t.rearrange("p (k h) -> p k h", h=HEADS)
            khe = lambda t: t.rearrange("p (k h e) -> p k h e", h=HEADS, e=EXPERTS)
            over_h = lambda t: t[:, :, None].to_broadcast([P, NT, HEADS])
            over_e = lambda t: kh(t)[:, :, :, None].to_broadcast([P, NT, HEADS, EXPERTS])
            over_k = lambda t: t[:, None, :].to_broadcast([P, NT, HEADS])
            a_self, a_last = node[:, :, GH:SRC_F], over_k(last_row[:, GH:SRC_F])
            dve.wait_ge(loaded, 16 * 6)
            do(v.tensor_tensor(kh(a4[:, 1, :]), a_self, ad[:, :, :], ALU.add))
            do(v.tensor_tensor(kh(a4[:, 2, :]), a_last, ad[:, :, :], ALU.add))
            dve.wait_ge(gathered, 16 * NT)
            do(v.tensor_tensor(kh(a4[:, 0, :]), rows[:, :, SRC_F:SEG_F], ad[:, :, :], ALU.add))
            do(v.tensor_tensor(kh(den[:, :]), rows[:, :, SRC_F:SEG_F], over_h(none0[:, :]), ALU.add))
            do(v.tensor_tensor(kh(den[:, :]), kh(den[:, :]), a_self, ALU.max))
            do(v.tensor_tensor(kh(sc[:, :]), over_h(none1[:, :]), a_last, ALU.add))
            do(v.tensor_tensor(den[:, :], den[:, :], sc[:, :], ALU.max))
            do(v.tensor_tensor(kh(a4[:, 3, :]), kh(den[:, :]), ad[:, :, :], ALU.add))
            do(v.scalar_tensor_tensor(a4[:, :, :], a4[:, :, :], 0.2, a4[:, :, :], ALU.mult, ALU.max))
            do(v.tensor_tensor(wts[:, :, :], a4[:, 0:3, :], a4[:, 3:4, :].to_broadcast([P, 3, K4]), ALU.subtract))
            v.tensor_scalar(wts[:, :, :], wts[:, :, :], 0.0, None, ALU.min).then_inc(weights_ready, 1)
            dve.wait_ge(exps, 1)
            do(v.tensor_tensor(kh(wts[:, 0, :]), kh(wts[:, 0, :]), over_h(has0[:, :]), ALU.mult))
            do(v.tensor_tensor(kh(wts[:, 2, :]), kh(wts[:, 2, :]), over_h(count1[:, :]), ALU.mult))
            do(v.tensor_tensor(kh(den[:, :]), rows[:, :, GH:SRC_F], kh(wts[:, 0, :]), ALU.mult))
            do(v.tensor_tensor(den[:, :], den[:, :], wts[:, 1, :], ALU.add))
            do(v.tensor_tensor(den[:, :], den[:, :], wts[:, 2, :], ALU.add))
            do(v.tensor_scalar(den[:, :], den[:, :], 1e-16, None, ALU.add))
            do(v.reciprocal(den[:, :], den[:, :]))
            he = lambda t: t.rearrange("p k (h e) -> p k h e", h=HEADS)
            do(v.tensor_tensor(khe(agg[:, :]), he(rows[:, :, 0:GH]), over_e(wts[:, 0, :]), ALU.mult))
            do(v.tensor_tensor(khe(tmp[:, :]), he(node[:, :, 0:GH]), over_e(wts[:, 1, :]), ALU.mult))
            do(v.tensor_tensor(agg[:, :], agg[:, :], tmp[:, :], ALU.add))
            last_he = last_row[:, 0:GH].rearrange("p (h e) -> p h e", h=HEADS)
            for h in range(HEADS):
                do(v.tensor_tensor(khe(tmp[:, :])[:, :, h, :], last_he[:, h:h + 1, :].to_broadcast([P, NT, EXPERTS]), over_e(wts[:, 2, :])[:, :, h, :], ALU.mult))
            do(v.tensor_tensor(agg[:, :], agg[:, :], tmp[:, :], ALU.add))
            do(v.tensor_tensor(khe(agg[:, :]), khe(agg[:, :]), over_e(den[:, :]), ALU.mult))
            kf = lambda t: t.rearrange("p (k f) -> p k f", f=GH)
            f_over_k = lambda t: t[:, None, :].to_broadcast([P, NT, GH])
            over_f = lambda t: t[:, :, None].to_broadcast([P, NT, GH])
            do(v.tensor_tensor(kf(agg[:, :]), kf(agg[:, :]), f_over_k(bias[:, :]), ALU.add))
            do(v.tensor_reduce(mean[:, :], kf(agg[:, :]), AX, ALU.add))
            do(v.tensor_scalar(mean[:, :], mean[:, :], 1.0 / GH, None, ALU.mult))
            do(v.tensor_tensor(kf(agg[:, :]), kf(agg[:, :]), over_f(mean[:, :]), ALU.subtract))
            do(v.tensor_tensor(tmp[:, :], agg[:, :], agg[:, :], ALU.mult))
            v.tensor_reduce(var[:, :], kf(tmp[:, :]), AX, ALU.add).then_inc(var_made, 1)
            dve.wait_ge(exps, 3)
            do(v.tensor_tensor(kf(agg[:, :]), kf(agg[:, :]), over_f(var[:, :]), ALU.mult))
            do(v.tensor_tensor(kf(agg[:, :]), kf(agg[:, :]), f_over_k(gamma[:, :]), ALU.mult))
            do(v.tensor_tensor(kf(agg[:, :]), kf(agg[:, :]), f_over_k(beta[:, :]), ALU.add))
            do(v.tensor_reduce(kh(sc[:, :]), khe(agg[:, :]).rearrange("p k h e -> p k e h"), AX, ALU.add))
            do(v.tensor_scalar(sc[:, :], sc[:, :], 1.0 / HEADS, None, ALU.mult))
            mine = kh(sc[:, :])[:, :, :, None].to_broadcast([P, NT, EXPERTS, EXPERTS])
            theirs = kh(sc[:, :])[:, :, None, :].to_broadcast([P, NT, EXPERTS, EXPERTS])
            do(v.tensor_tensor(khe(beats[:, :]), theirs, mine, ALU.is_gt))
            do(v.tensor_tensor(khe(even[:, :]), theirs, mine, ALU.is_equal))
            dve.wait_ge(tie_made, 3)
            do(v.tensor_tensor(kf(even[:, :]), kf(even[:, :]), f_over_k(ties[:, :]), ALU.mult))
            do(v.tensor_tensor(beats[:, :], beats[:, :], even[:, :], ALU.add))
            do(v.tensor_reduce(kh(rank[:, :]), khe(beats[:, :]), AX, ALU.add))
            do(v.tensor_scalar(rank[:, :], rank[:, :], 2.0, None, ALU.is_lt))
            do(v.tensor_reduce(top[:, :], kh(sc[:, :]), AX, ALU.max))
            v.tensor_tensor(kh(sc[:, :]), kh(sc[:, :]), over_h(top[:, :]), ALU.subtract).then_inc(var_made, 1)
            dve.wait_ge(exps, 4)
            do(v.tensor_tensor(sc[:, :], sc[:, :], rank[:, :], ALU.mult))
            do(v.tensor_reduce(top[:, :], kh(sc[:, :]), AX, ALU.add))
            do(v.reciprocal(top[:, :], top[:, :]))
            v.tensor_tensor(kh(sc[:, :]), kh(sc[:, :]), over_h(top[:, :]), ALU.mult).then_inc(gates_made, 1)
            for k in range(NT // 4):
                dve.wait_ge(gates_t, 4 * k + 4)
                v.tensor_copy(gt[:, k * 512:(k + 1) * 512], psc[k % 4][0:EXPERTS, :]).then_inc(gates_out, 1)

        @block.scalar
        def _(act):
            f = nc.scalar.activation
            act.wait_ge(tie_made, 1)
            act.wait_ge(weights_ready, 1)
            f(wts[:, :, :], wts[:, :, :], ACT.Exp).then_inc(exps, 1)
            act.wait_ge(var_made, 1)
            f(var[:, :], var[:, :], ACT.Ln, scale=1.0 / GH, bias=eps[:, 0:1]).then_inc(exps, 1)
            act.wait_ge(exps, 2)
            f(var[:, :], var[:, :], ACT.Exp, scale=-0.5).then_inc(exps, 1)
            act.wait_ge(var_made, 2)
            f(sc[:, :], sc[:, :], ACT.Exp).then_inc(exps, 1)

        @block.tensor
        def _(pe):
            pe.wait_ge(gates_made, 1)
            for k in range(NT):
                if k % 4 == 0 and k >= 16:
                    pe.wait_ge(gates_out, k // 4 - 3)
                nc.tensor.transpose(psc[k // 4 % 4][0:EXPERTS, (k % 4) * P:(k % 4 + 1) * P], sc[:, k * EXPERTS:(k + 1) * EXPERTS], ident[:, :]).then_inc(gates_t, 1)

FF = 512
FT = FF // P
UNITS = EXPERTS * FT
RING = 4
LAG = 3


def experts(nc, tables, gates_dram, w, out_dram):
    with ExitStack() as ctx:
        sb = lambda name, shape, dt=F32: ctx.enter_context(nc.sbuf_tensor(name, shape, dt))
        sem = lambda name: ctx.enter_context(nc.semaphore(name))
        pair = lambda name, shape: [sb(f"{name}{k}", shape) for k in range(2)]
        w1, w2 = sb("w1", [P, EXPERTS, CT, FF]), sb("w2", [P, UNITS, CT * P])
        b1, b2, sel = sb("b1", [P, UNITS]), sb("b2", [EXPERTS, CT * P]), sb("gate_sel", [EXPERTS, EXPERTS, P])
        xn, res, gate, out = pair("f_xn", [P, CT, T]), pair("f_x2", [P, CT, T]), pair("f_gates", [EXPERTS, T]), pair("f_out", [P, CT, T])
        hid = [sb(f"hid{k}", [P, T]) for k in range(RING)]
        ps_up = [ctx.enter_context(nc.psum_tensor(f"ps_up{k}", [P, T], F32)) for k in range(RING)]
        ps_gate = [ctx.enter_context(nc.psum_tensor(f"ps_gate{k}", [P, T], F32)) for k in range(2)]
        ps_down = [ctx.enter_context(nc.psum_tensor(f"ps_down{k}", [P, T], F32)) for k in range(CT)]
        w_loaded, const = sem("f_w_loaded"), sem("f_const")
        loaded, stored = [sem(f"f_loaded{k}") for k in range(2)], [sem(f"f_stored{k}") for k in range(2)]
        up, gates_up, gelu, gated, down, added = sem("up_full"), sem("gate_full"), sem("gelu_made"), sem("f_gated"), sem("down_done"), sem("f_added")

        def bodies(eng, run):
            run(0, 0, 0)
            run(1, 0, 1)
            with eng.Fori(1, CHUNKS // 2) as j:
                run(j * 2, j, 0)
                run(j * 2 + 1, j, 1)

        chunk_of = lambda t, i: t[bass.ds(i, 1)].rearrange("o p (c t) -> (o p) c t", c=CT)
        sp_passed, pool_passed = sem("f_sp_passed"), sem("f_pool_passed")
        with nc.Block() as block:
            @block.sync
            def _(sp):
                sp.dma_start(w1[:, :, :, :], w["w1"].rearrange("e (c p) f -> p (e c) f", p=P)).then_inc(w_loaded, 16)
                sp.dma_start(w2[:, :, :], w["w2"].rearrange("e (c p) d -> p (e c) d", p=P)).then_inc(w_loaded, 16)
                sp.dma_start(b1[:, :], w["b1"]).then_inc(w_loaded, 16)
                sp.dma_start(b2[:, :], w["b2"]).then_inc(w_loaded, 16)

                def run(i, j, par):
                    if not isinstance(i, int):
                        wait_alone(sp, added, i * 2 - 2, sp_passed)
                        wait_alone(sp, gelu, i * UNITS - UNITS, sp_passed)
                        wait_alone(sp, gated, i * UNITS - UNITS, sp_passed)
                    sp.dma_start(xn[par][:, :, :], chunk_of(tables["xn2"], i)).then_inc(loaded[par], 16)
                    sp.dma_start(res[par][:, :, :], chunk_of(tables["x2"], i)).then_inc(loaded[par], 16)
                    sp.dma_start(gate[par][:, :], gates_dram[:, bass.ds(i * T, T)]).then_inc(loaded[par], 16)
                bodies(sp, run)

            @block.gpsimd
            def _(pool):
                nc.gpsimd.memset(sel[:, :, :], 0.0).then_inc(const, 1)
                pool.wait_ge(const, 1)
                nc.gpsimd.affine_select(out=sel[:, :, :], in_=sel[:, :, :], compare_op=ALU.not_equal, fill=1.0, base=0,
                                        pattern=[[-1, EXPERTS], [0, P]], channel_multiplier=1).then_inc(const, 1)

                def run(i, j, par):
                    wait_alone(pool, added, i * 2 + 2, pool_passed)
                    pool.dma_start(chunk_of(out_dram, i), out[par][:, :, :]).then_inc(stored[par], 16)
                bodies(pool, run)
                for k in range(2):
                    pool.wait_ge(stored[k], CHUNKS // 2 * 16)

            @block.tensor
            def _(pe):
                mm = nc.tensor.matmul
                pe.wait_ge(w_loaded, 64)
                pe.wait_ge(const, 2)

                def run(i, j, par):
                    pe.wait_ge(loaded[par], j * 48 + 48)
                    later = not isinstance(i, int) or i > 0
                    for k in range(UNITS + LAG):
                        if k < UNITS:
                            e, ft = divmod(k, FT)
                            if ft == 0:
                                if e >= 2 or later:
                                    pe.wait_ge(gated, i * UNITS + (e - 1) * FT)
                                mm(ps_gate[e % 2][:, :], sel[:, e, :], gate[par][:, :], start=True, stop=True).then_inc(gates_up, 1)
                            if k >= RING or later:
                                pe.wait_ge(gelu, i * UNITS + k - RING + 1)
                            for c in range(CT):
                                last = mm(ps_up[k % RING][:, :], w1[:, e, c, ft * P:(ft + 1) * P], xn[par][:, c, :], start=(c == 0), stop=(c == CT - 1))
                            last.then_inc(up, 1)
                        if k == LAG:
                            if later:
                                pe.wait_ge(added, i * 2)
                            for c in range(CT):
                                mm(ps_down[c][:, :], b2[:, c * P:(c + 1) * P], gate[par][:, :], start=True, stop=False)
                        if k >= LAG:
                            q = k - LAG
                            pe.wait_ge(gated, i * UNITS + q + 1)
                            for c in range(CT):
                                last = mm(ps_down[c][:, :], w2[:, q, c * P:(c + 1) * P], hid[q % RING][:, :], start=False, stop=(q == UNITS - 1))
                            last.then_inc(down, 1)
                bodies(pe, run)

            @block.scalar
            def _(act):
                act.wait_ge(w_loaded, 64)

                def run(i, j, par):
                    later = not isinstance(i, int) or i > 0
                    for k in range(UNITS):
                        act.wait_ge(up, i * UNITS + k + 1)
                        if k >= RING or later:
                            act.wait_ge(down, i * UNITS + k - RING + 1)
                        nc.scalar.activation(hid[k % RING][:, :], ps_up[k % RING][:, :], ACT.Gelu, bias=b1[:, k:k + 1]).then_inc(gelu, 1)
                bodies(act, run)

            @block.vector
            def _(dve):
                v = nc.vector

                def run(i, j, par):
                    for k in range(UNITS):
                        e = k // FT
                        dve.wait_ge(gates_up, i * EXPERTS + e + 1)
                        dve.wait_ge(gelu, i * UNITS + k + 1)
                        v.tensor_tensor(hid[k % RING][:, :], hid[k % RING][:, :], ps_gate[e % 2][:, :], ALU.mult).then_inc(gated, 1)
                    dve.wait_ge(down, i * UNITS + UNITS)
                    dve.wait_ge(loaded[par], j * 48 + 48)
                    if not isinstance(i, int):
                        dve.wait_ge(stored[par], j * 16)
                    for c in range(CT):
                        v.tensor_tensor(out[par][:, c, :], ps_down[c][:, :], res[par][:, c, :], ALU.add).then_inc(added, 1)
                bodies(dve, run)


INPUTS = ["x", "in", "x_proj", "dt", "out_proj", "conv", "conv_b", "dt_b", "skip", "a_log", "gat", "att", "b_gat",
          "gamma", "beta", "w1", "b1", "w2", "b2", "edge_src", "edge_dst"]


def metaformer_block(nc, a, out):
    dram = lambda name, shape, dt=F32: nc.dram_tensor(name, shape, dt, kind="Internal").ap()
    keys, ends_at = dram("keys_sorted", [EDGES + 2, 1], I32), dram("ends_at", [EDGES, 1], I32)
    ends = dram("ends", [GROUPS + OFF, 1], I32)
    src, dst = dram("edge_src_sorted", [EDGES, 1], I32), dram("edge_dst_sorted", [EDGES, 1], I32)
    seg = dram("segments", [EDGES, SEG_F], I32)
    gates = dram("gates", [EXPERTS, NODES])
    tables = {"x2": dram("x_after_mamba", [CHUNKS, P, CT * T]), "xn2": dram("x_normed", [CHUNKS, P, CT * T]),
              "src": dram("node_src", [NODES, SRC_F]), "dst": dram("node_dst_scores", [NODES, DST_F])}
    w = {"in": a["in"], "x": a["x_proj"], "dt": a["dt"], "out": a["out_proj"], "conv": a["conv"], "conv_b": a["conv_b"],
         "dt_b": a["dt_b"], "skip": a["skip"], "a_log": a["a_log"], "gat": a["gat"], "att": a["att"]}
    with nc.sbuf_tensor("chunk_counts", [P, 2], I32) as counts:
        sort_edges(nc, a["edge_src"], a["edge_dst"], keys, ends_at, ends, src, dst, counts)
        mamba(nc, a["x"], w, tables, ends_at, ends, counts)
        attention(nc, keys, src, dst, ends, tables, a, seg, gates, counts)
        experts(nc, tables, gates, a, out)


def kernel(x, L0_conv_in_proj_w, L0_conv_conv_w, L0_conv_conv_b, L0_conv_x_proj_w, L0_conv_dt_proj_w, L0_conv_dt_proj_b,
           L0_conv_A_log, L0_conv_D, L0_conv_out_proj_w, L0_ffn_W_gat, L0_ffn_att_src, L0_ffn_att_dst, L0_ffn_b_gat,
           L0_ffn_ln_gamma, L0_ffn_ln_beta, L0_ffn_W1, L0_ffn_b1, L0_ffn_W2, L0_ffn_b2, L0_ffn_edge_index):
    import concourse.bacc as bacc
    from concourse.bass_utils import run_bass_kernel_spmd

    lay = np.ascontiguousarray
    arr = np.asarray
    column = lambda v: lay(arr(v).reshape(-1, P).T)
    xs = lay(arr(x).reshape(4, CT, P, PER_BATCH, T).transpose(0, 3, 2, 1, 4)).reshape(CHUNKS, P, CT * T)
    xp, dtw = arr(L0_conv_x_proj_w).T, arr(L0_conv_dt_proj_w).T
    x_proj = np.zeros((xp.shape[0], 64), xp.dtype)
    x_proj[:, 0:16], x_proj[:, 32:64] = xp[:, 0:16], xp[:, 16:48]
    dt = np.zeros((32, dtw.shape[1]), dtw.dtype)
    dt[0:16] = dtw
    edges = arr(L0_ffn_edge_index)
    inputs = {
        "x": xs, "in": lay(arr(L0_conv_in_proj_w).T), "x_proj": x_proj, "dt": dt, "out_proj": lay(arr(L0_conv_out_proj_w).T),
        "conv": lay(arr(L0_conv_conv_w).reshape(-1, TAPS)), "conv_b": column(L0_conv_conv_b), "dt_b": column(L0_conv_dt_proj_b),
        "skip": column(L0_conv_D), "a_log": lay(arr(L0_conv_A_log)), "gat": lay(arr(L0_ffn_W_gat)),
        "att": lay(np.stack([arr(L0_ffn_att_src).reshape(-1), arr(L0_ffn_att_dst).reshape(-1)])),
        "b_gat": lay(arr(L0_ffn_b_gat).reshape(1, -1)), "gamma": lay(arr(L0_ffn_ln_gamma).reshape(1, -1)),
        "beta": lay(arr(L0_ffn_ln_beta).reshape(1, -1)), "w1": lay(arr(L0_ffn_W1)), "b1": column(L0_ffn_b1),
        "w2": lay(arr(L0_ffn_W2)), "b2": lay(arr(L0_ffn_b2)),
        "edge_src": lay(edges[0].reshape(P, EC)), "edge_dst": lay(edges[1].reshape(P, EC)),
    }
    nc = bacc.Bacc("TRN2", target_bir_lowering=False, num_devices=1)
    arrays, args = {}, {}
    for name in INPUTS:
        arrays[f"in_{name}"] = inputs[name]
        args[name] = nc.dram_tensor(f"in_{name}", inputs[name].shape, mybir.dt.from_np(inputs[name].dtype), kind="ExternalInput").ap()
    out = nc.dram_tensor("out", [CHUNKS, P, CT * T], F32, kind="ExternalOutput").ap()
    metaformer_block(nc, args, out)
    got = run_bass_kernel_spmd(nc, [arrays], core_ids=[0]).results[0]["out"]
    return lay(got.reshape(4, PER_BATCH, P, CT, T).transpose(0, 3, 2, 1, 4)).reshape(4, CT * P, 64, 64)
```

```python
import numpy as np
import concourse.bass as bass
from concourse import mybir
from contextlib import ExitStack

ALU = mybir.AluOpType
ACT = mybir.ActivationFunctionType
F32 = mybir.dt.float32
BF16 = mybir.dt.bfloat16
I32 = mybir.dt.int32
U32 = mybir.dt.uint32

P = 128
NODES = 16384
EDGES = 1048576
EC = EDGES // P
LB = EC.bit_length() - 1
PB = 7
SRC_BITS = 14
SRC_MASK = NODES - 1
OFF = 1024
GROUPS = 2 * NODES
CHUNK = 8192
CW = CHUNK // P


def float_of(bits):
    return float(np.array([bits], np.uint32).view(np.float32)[0])


class Steps:

    def __init__(self, engine, sem, base=0):
        self.engine, self.sem, self.base, self.n = engine, sem, base, 0

    def __call__(self, instruction):
        instruction.then_inc(self.sem, 1)
        self.n += 1

    def settle(self, back=0):
        self.engine.wait_ge(self.sem, self.base + (self.n - back))


def wait_alone(engine, sem, value, passed):
    engine.wait_ge(sem, value)
    if not isinstance(value, int):
        engine.sem_inc(passed, 1)


def sort_edges(nc, edge_src, edge_dst, keys_dram, ends_at_dram, ends_dram, src_dram, dst_dram, counts):
    with ExitStack() as ctx:
        sb = lambda name, shape, dt: ctx.enter_context(nc.sbuf_tensor(name, shape, dt))
        sem = lambda name: ctx.enter_context(nc.semaphore(name))
        x = sb("sort_x", [P, EC], F32)
        y = sb("sort_y", [P, EC], F32)
        z = sb("sort_z", [P, EC], F32)
        ident = sb("sort_ident", [P, P], F32)
        lane = sb("lane", [P, 1], I32)
        lane_bit = sb("lane_bit", [P, PB], I32)
        sign = sb("sign", [P, PB + 1], F32)
        ones = sb("sort_ones", [P, P], F32)
        below = sb("below", [P, 2], F32)
        sentinel = sb("sentinel", [1, 1], I32)
        zeros = sb("zero_rows", [P, (GROUPS + OFF) // P], I32)
        ps = [ctx.enter_context(nc.psum_tensor(f"sort_ps{k}", [P, 1024], F32)) for k in range(4)]
        loaded, const, lanes, keys_made = sem("edges_loaded"), sem("const_ready"), sem("lane_iota"), sem("keys_made")
        dve_steps, act_steps = sem("dve_steps"), sem("act_steps")
        run_sorted, transposed = sem("run_sorted"), sem("transposed")
        out = sem("evacuated_by_scalar"), sem("evacuated_by_vector")
        stored, reloaded, counted = sem("keys_stored"), sem("next_loaded"), sem("lane_counts_summed")
        counted_dve, idx_made, idx_stored, zeroed = sem("lane_counts"), sem("ends_at_made"), sem("ends_at_stored"), sem("ends_zeroed")
        src_made, dst_made, src_stored, dst_stored = sem("src_made"), sem("dst_made"), sem("src_stored"), sem("dst_stored")
        xi, yi, zi = (t[:, :].bitcast(I32) for t in (x, y, z))
        TILES = EC // P
        GROUP = 8
        NG = TILES // GROUP
        upper = range(LB + 1, LB + PB + 1)
        sides, at = [], LB * (LB + 1) // 2 + 1
        for level in upper:
            for stages in (level - LB, LB):
                sides.append(((y, x) if at % 2 == 0 else (x, y)))
                at += 1 + stages

        def halves(n, k):
            src, dst = ps[(n * NG + k) % 4][:, :], sides[n][1][:, k * GROUP * P:(k + 1) * GROUP * P]
            if n % 2 == 0:
                view = lambda w, d: w.rearrange("p (h d l) -> p h d l", d=2, l=1 << (n // 2))[:, :, d]
                return [(view(dst, 0), view(src, 0), 1.0), (view(dst, 1), view(src, 1), -1.0)]
            half = GROUP * P // 2
            return [(dst[:, c:c + half], src[:, c:c + half], sign[:, n // 2 + 1:n // 2 + 2]) for c in (0, half)]

        with nc.Block() as block:
            @block.sync
            def _(sp):
                sp.dma_start(xi, edge_src).then_inc(loaded, 16)
                sp.dma_start(yi, edge_dst).then_inc(loaded, 16)
                sp.wait_ge(const, 4)
                sp.dma_start(keys_dram[0:1, :], sentinel[:, :]).then_inc(zeroed, 16)
                sp.dma_start(keys_dram[EDGES + 1:EDGES + 2, :], sentinel[:, :]).then_inc(zeroed, 16)
                sp.dma_start(ends_dram.rearrange("(p c) o -> p (c o)", p=P), zeros[:, :]).then_inc(zeroed, 16)
                sp.wait_ge(keys_made, 1)
                body = keys_dram[1:EDGES + 1, :].rearrange("(p c) o -> p (c o)", p=P)
                sp.dma_start(body, xi).then_inc(stored, 16)
                sp.wait_ge(stored, 16)
                sp.wait_ge(zeroed, 48)
                shifted = keys_dram[2:EDGES + 2, :].rearrange("(p c) o -> p (c o)", p=P)
                sp.dma_start(yi, shifted).then_inc(reloaded, 16)
                lanes_of = lambda t: t.rearrange("(p c) o -> p (c o)", p=P)
                sp.wait_ge(src_made, 1)
                sp.dma_start(lanes_of(src_dram), zi).then_inc(src_stored, 16)
                sp.wait_ge(idx_made, 1)
                sp.dma_start(ends_at_dram.rearrange("(p c) o -> p (c o)", p=P), zi).then_inc(idx_stored, 16)
                sp.wait_ge(dst_made, 1)
                sp.dma_start(lanes_of(dst_dram), yi).then_inc(dst_stored, 16)
                sp.wait_ge(src_stored, 16)
                sp.wait_ge(dst_stored, 16)
                sp.wait_ge(idx_stored, 16)

            @block.gpsimd
            def _(pool):
                nc.gpsimd.iota(lane[:, :], pattern=[[0, 1]], base=0, channel_multiplier=1).then_inc(lanes, 1)
                nc.gpsimd.memset(ones[:, :], 1.0).then_inc(const, 1)
                nc.gpsimd.memset(sentinel[:, :], 0).then_inc(const, 1)
                nc.gpsimd.memset(zeros[:, :], 0).then_inc(const, 1)
                pool.wait_ge(const, 1)
                nc.gpsimd.affine_select(out=ident[:, :], in_=ones[:, :], compare_op=ALU.is_equal, fill=0.0, base=0,
                                        pattern=[[-1, P]], channel_multiplier=1).then_inc(const, 1)

            @block.vector
            def _(dve):
                step = Steps(dve, dve_steps)
                v = nc.vector
                dve.wait_ge(lanes, 1)
                for b in range(PB):
                    step(v.tensor_scalar(lane_bit[:, b:b + 1], lane[:, :], b, 1, ALU.logical_shift_right, ALU.bitwise_and))
                step.settle()
                step(v.tensor_scalar(sign[:, 0:PB], lane_bit[:, :], -2, 1, ALU.mult, ALU.add))
                step(v.memset(sign[:, PB:PB + 1], 1.0))
                dve.wait_ge(loaded, 32)
                def one(out, in_, a, b, op0, op1):
                    step(v.tensor_scalar(out, in_, a, b, op0, op1)); step.settle()
                def two(out, a, b, op):
                    step(v.tensor_tensor(out, a, b, op)); step.settle()
                one(zi, xi, 0, NODES, ALU.is_lt, ALU.mult)
                two(xi, xi, zi, ALU.add)
                one(xi, xi, 0, NODES - 1, ALU.max, ALU.min)
                one(yi, yi, -1, NODES, ALU.max, ALU.min)
                one(yi, yi, 0x1FFFF, None, ALU.bitwise_and, ALU.bypass)
                one(zi, xi, NODES - 1, NODES, ALU.is_equal, ALU.mult)
                two(zi, zi, yi, ALU.add)
                one(yi, yi, NODES, 4 * NODES, ALU.is_ge, ALU.mult)
                two(yi, yi, zi, ALU.add)
                one(yi, yi, GROUPS, OFF, ALU.min, ALU.add)
                one(yi, yi, SRC_BITS, None, ALU.logical_shift_left, ALU.bypass)
                two(yi, xi, yi, ALU.bitwise_or)

                cur, nxt = y, x

                def stage(bit, direction):
                    nonlocal cur, nxt
                    lo = 1 << bit
                    if direction is None:
                        a, o = (t[:, :].rearrange("p (m t l) -> p m t l", t=2, l=lo) for t in (cur, nxt))
                        step.settle()
                        step(v.tensor_tensor(o[:, :, 0], a[:, :, 0], a[:, :, 1], ALU.min))
                        step(v.tensor_tensor(o[:, :, 1], a[:, :, 0], a[:, :, 1], ALU.max))
                    else:
                        a, o = (t[:, :].rearrange("p (h d m t l) -> p h d m t l", d=2, m=1 << (direction - 1 - bit), t=2, l=lo)
                                for t in (cur, nxt))
                        for d in range(2):
                            step.settle(0 if bit == direction - 1 and d == 0 else 2)
                            low, high = (ALU.min, ALU.max) if d == 0 else (ALU.max, ALU.min)
                            step(v.tensor_tensor(o[:, :, d, :, 0], a[:, :, d, :, 0], a[:, :, d, :, 1], low))
                            step(v.tensor_tensor(o[:, :, d, :, 1], a[:, :, d, :, 0], a[:, :, d, :, 1], high))
                    cur, nxt = nxt, cur

                for level in range(1, LB):
                    for bit in reversed(range(level)):
                        stage(bit, level)
                step.settle()
                step(v.tensor_scalar(nxt[:, :], cur[:, :], sign[:, 0:1], None, ALU.mult))
                cur, nxt = nxt, cur
                for bit in reversed(range(LB)):
                    stage(bit, None)
                for n, (_, other) in enumerate(sides):
                    step.settle()
                    dve.sem_inc(run_sorted, 1)
                    for k in range(1, NG, 2):
                        dve.wait_ge(transposed, n * NG + k + 1)
                        for dst, src, factor in halves(n, k):
                            v.tensor_scalar(dst, src, factor, None, ALU.mult).then_inc(out[1], 1)
                    dve.wait_ge(out[0], (n + 1) * NG)
                    dve.wait_ge(out[1], (n + 1) * NG)
                    cur, nxt = nxt, cur
                    level = upper[n // 2]
                    bits, direction = (level - LB, level - LB) if n % 2 == 0 else (LB, None)
                    for bit in reversed(range(bits)):
                        stage(bit, direction if level < LB + PB else None)
                step.settle()
                assert cur is x, "the network ends in x"
                dve.sem_inc(keys_made, 1)
                for n, top in enumerate((NODES, GROUPS)):
                    step(v.tensor_scalar(z[:, :], x[:, :], float_of((top + OFF) << SRC_BITS), 0.0, ALU.is_lt, ALU.add,
                                         accum_out=below[:, n:n + 1]))
                    step.settle()
                dve.sem_inc(counted_dve, 1)
                dve.wait_ge(counted, 1)
                one(counts[:, :], ps[0][:, 0:2], float(CHUNK - 1), None, ALU.add, ALU.bypass)
                one(counts[:, :], counts[:, :], CHUNK.bit_length() - 1, None, ALU.logical_shift_right, ALU.bypass)
                one(counts[:, 0:1], counts[:, 0:1], 7, None, ALU.max, ALU.bypass)
                one(counts[:, 1:2], counts[:, 1:2], float(NODES // 512), None, ALU.subtract, ALU.bypass)
                one(counts[:, 1:2], counts[:, 1:2], 1, None, ALU.max, ALU.bypass)
                dve.wait_ge(reloaded, 16)
                one(yi, yi, SRC_BITS, None, ALU.logical_shift_right, ALU.bypass)
                v.tensor_scalar(zi, xi, SRC_MASK, None, ALU.bitwise_and).then_inc(src_made, 1)
                dve.wait_ge(stored, 16)
                dve.wait_ge(src_made, 1)
                one(xi, xi, SRC_BITS, None, ALU.logical_shift_right, ALU.bypass)
                two(yi, yi, xi, ALU.is_equal)
                dve.wait_ge(src_stored, 16)
                v.scalar_tensor_tensor(zi, yi, float(4 * GROUPS), xi, ALU.mult, ALU.add).then_inc(idx_made, 1)
                dve.wait_ge(idx_made, 1)
                v.tensor_scalar(yi, xi, OFF, NODES - 1, ALU.subtract, ALU.min).then_inc(dst_made, 1)

            @block.tensor
            def _(pe):
                pe.wait_ge(const, 4)
                for n, (src, _) in enumerate(sides):
                    pe.wait_ge(run_sorted, n + 1)
                    for k in range(NG):
                        g = n * NG + k
                        if g >= 4:
                            pe.wait_ge(out[g % 2], 2 * ((g - 4) // 2 + 1))
                        for q in range(GROUP):
                            t = k * GROUP + q
                            last = nc.tensor.transpose(ps[g % 4][:, q * P:(q + 1) * P], src[:, t * P:(t + 1) * P], ident[:, :])
                        last.then_inc(transposed, 1)
                pe.wait_ge(counted_dve, 1)
                pe.wait_ge(out[0], len(sides) * NG)
                nc.tensor.matmul(ps[0][:, 0:2], ones[:, :], below[:, :], start=True, stop=True).then_inc(counted, 1)

            @block.scalar
            def _(act):
                for n in range(len(sides)):
                    for k in range(0, NG, 2):
                        act.wait_ge(transposed, n * NG + k + 1)
                        for dst, src, factor in halves(n, k):
                            nc.scalar.activation(dst, src, ACT.Copy, scale=factor).then_inc(out[0], 1)

T = 512
CHUNKS = NODES // T
PER_BATCH = 4096 // T
CT = 2
DT = 4
NS = 16
GQ = 4
NGR = NS // GQ
STEPS = NGR * DT
POOL_STEPS = (3, 7, 11, 15)
OWN_STEPS = [s for s in range(STEPS) if s not in POOL_STEPS]
SOFT_AT = (14, 15, 16, 17)
DELTA_AT = (14, 15, 16, 17)
HALO = 3
LOG_EXP = "natural_log_exp_and_others"
TAPS = 4
SRC_F = 20
DST_F = 4
H_F = SRC_F + DST_F

PRE = ["mean", "var"] + [f"u{d}" for d in range(DT)] + [f"conv{d}" for d in range(DT)] + [f"res{d}" for d in range(DT)] \
    + ["dbc"] + [f"dt{d}" for d in range(DT)]
POST = ["out0", "out1", "mean2", "var2", "h"]
PE_AT = {"out0": 0, "out1": 0, "mean2": 1, "mean": 2, "var2": 3, "var": 4, "h": 6, "dbc": 12,
         **{f"u{d}": 7 for d in range(DT)}, **{f"conv{d}": 9 for d in range(DT)},
         **{f"res{d}": 10 for d in range(DT)}, **{f"dt{d}": 13 for d in range(DT)}}
VEC_AT = {"x2": 0, "centre2": 1, "centre": 2, "norm2": 5, "norm": 6, "low_parts": 12, "lowest_part": 14}
ACT_AT = {"square2": 3, "square": 4, "rstd2": 5, "rstd": 7, "h_out": 8, "u_out": 9, "u_silu": 10, "res_silu": 11,
          "dbc_out": 13, "mid_part": 14}


def mamba(nc, x_dram, w, tables, ends_at_dram, ends_dram, counts):
    with ExitStack() as ctx:
        sb = lambda name, shape, dt=F32: ctx.enter_context(nc.sbuf_tensor(name, shape, dt))
        sem = lambda name: ctx.enter_context(nc.semaphore(name))
        xt = [sb(f"x_in{k}", [P, CT, T]) for k in range(2)]
        xn, sq, rs, rs2 = sb("xn", [P, CT, T]), sb("sq", [P, CT, T]), sb("rs", [P, T]), sb("rs2", [P, T])
        upre = sb("upre", [P, DT, HALO + T])
        u = [sb(f"u{k}", [P, DT, T]) for k in range(2)]
        sres = [sb(f"sres{k}", [P, DT, T]) for k in range(2)]
        delta, du, yt = sb("delta", [P, DT, T]), sb("du", [P, DT, T]), sb("yt", [P, DT, T])
        soft = [xn[:, 0, :], xn[:, 1, :], sq[:, 0, :], sq[:, 1, :]]
        hb = [sb(f"hb{k}", [P, GQ, T]) for k in range(4)]
        da = [sb(f"da{k}", [P, GQ, T]) for k in range(2)]
        bb = [sb(f"bb{k}", [P, GQ, T]) for k in range(2)]
        cb = [sb(f"cb{k}", [P, GQ, T]) for k in range(2)]
        x2, xn2, hst = sb("x2", [P, CT, T]), sb("xn2", [P, CT, T]), sb("hst", [P, T // P, H_F])
        parts = [sb(f"bc_parts{k}", [96, T], BF16) for k in range(2)]
        rest, mid, dtr = sb("bc_rest", [64, T]), sb("bc_mid", [64, T], BF16), sb("dtr", [32, T])
        carry, keep = sb("carry", [P, DT, NS]), sb("keep", [P, CHUNKS + 1])
        w_in, w_x = sb("w_in", [P, CT, 2 * DT * P]), sb("w_x", [P, DT, 64])
        w_dt, w_out = sb("w_dt", [32, DT * P]), sb("w_out", [P, DT, CT * P])
        w_g, att = sb("w_g", [P, CT, H_F]), sb("att", [P, 2, 16])
        w_att = sb("w_att", [P, CT, 2, 16])
        w_conv, diag = sb("w_conv", [P, DT, TAPS]), sb("diag", [P, DT * TAPS, P])
        conv_b, dt_b, skip = sb("conv_b", [P, DT]), sb("dt_b", [P, DT]), sb("skip", [P, DT])
        a_neg, eps = sb("a_neg", [P, DT, NS]), sb("eps", [P, 3])
        ident, mean_w, sel = sb("ident", [P, P]), sb("mean_w", [P, P]), sb("sel", [96, 2 * NS], BF16)
        end_idx, end_pos = sb("end_idx", [P, CW], I32), sb("end_pos", [P, CW], I32)
        chunk_step = sb("chunk_step", [P, CW], I32)
        psy = ctx.enter_context(nc.psum_tensor("psy", [P, DT, T], F32))
        pst = [ctx.enter_context(nc.psum_tensor(f"pst{k}", [P, T], F32)) for k in range(2)]
        psg = [ctx.enter_context(nc.psum_tensor(f"psg{k}", [P, T], F32)) for k in range(2)]

        w_loaded, const, weights_made, setup = sem("w_loaded"), sem("mamba_const"), sem("weights_made"), sem("setup_steps")
        x_loaded = [sem(f"x_loaded{k}") for k in range(2)]
        xres_loaded, x2_stored, xn2_stored, h_stored = sem("xres_loaded"), sem("x2_stored"), sem("xn2_stored"), sem("h_stored")
        pre_full, post_full = sem("pre_psum_full"), sem("post_psum_full")
        centred, squared, rstd_made, normed = sem("centred"), sem("squared"), sem("rstd_made"), sem("normed")
        upre_made, u_made, res_made, dbc_out = sem("upre_made"), sem("u_made"), sem("res_made"), sem("dbc_out")
        rest_made, mid_made, parts_made = sem("rest_made"), sem("mid_made"), sem("parts_made")
        abs_made, relu_made = sem("abs_made"), sem("relu_made")
        soft_made, delta_made, du_made = sem("soft_made"), sem("delta_made"), sem("du_made")
        bc_full, bc_made, da_made = sem("bc_psum_full"), sem("bc_made"), sem("da_made")
        dbu_made, pool_dbu_made, scanned, carried, products = sem("dbu_made"), sem("pool_dbu_made"), sem("scanned"), sem("carried"), sem("products")
        summed, y_read, gated = sem("summed"), sem("y_read"), sem("gated")
        x2_made, centred2, squared2, rstd2_made = sem("x2_made"), sem("centred2"), sem("squared2"), sem("rstd2_made")
        normed2, h_out = sem("normed2"), sem("h_out")
        idx_loaded, pos_made, scattered = sem("idx_loaded"), sem("pos_made"), sem("scattered")

        def order(pre, post):
            names = (POST if post else []) + (PRE if pre else [])
            return sorted(names, key=lambda n: PE_AT[n])

        class Body:

            def __init__(self, i, next_pair, par, scan=True, pre=True, post=True, first=0, before=()):
                self.i, self.next_pair, self.par, self.scan, self.pre, self.post = i, next_pair, par, scan, pre, post
                self.first, self.before, self.order = first, before, order(pre, post)

            def slot(self, name):
                return (self.order.index(name) + self.first) % 2

        def bodies(eng, run):
            a, last = len(PRE), PRE[-2:]
            run(Body(-1, 0, 1, scan=False, post=False))
            run(Body(0, 0, 0, post=False, first=a % 2, before=last))
            assert (len(PRE) + len(POST)) % 2 == 0
            with eng.Fori(0, (CHUNKS - 2) // 2) as j:
                run(Body(j * 2 + 1, j + 1, 1, before=last))
                run(Body(j * 2 + 2, j + 1, 0, before=last))
            run(Body(CHUNKS - 1, CHUNKS // 2, 1, pre=False, before=last))
            run(Body(CHUNKS, CHUNKS // 2, 0, scan=False, pre=False, first=len(POST) % 2, before=POST[-2:]))

        sp_passed, pool_passed = sem("m_sp_passed"), sem("m_pool_passed")
        with nc.Block() as block:
            @block.sync
            def _(sp):
                loads = [(w_in, w["in"], "(c p) e -> p c e"), (w_x, w["x"], "(c p) e -> p c e"),
                         (w_out, w["out"], "(c p) e -> p c e"), (w_conv, w["conv"], "(c p) e -> p c e")]
                for t, d, how in loads:
                    sp.dma_start(t[:, :, :], d.rearrange(how, p=P)).then_inc(w_loaded, 16)
                sp.dma_start(w_g[:, :, 0:16], w["gat"].rearrange("(c p) e -> p c e", p=P)).then_inc(w_loaded, 16)
                sp.dma_start(w_dt[:, :], w["dt"]).then_inc(w_loaded, 16)
                sp.dma_start(a_neg[:, :, :], w["a_log"].rearrange("(c p) e -> p c e", p=P)).then_inc(w_loaded, 16)
                for t, d in ((conv_b, w["conv_b"]), (dt_b, w["dt_b"]), (skip, w["skip"])):
                    sp.dma_start(t[:, :], d).then_inc(w_loaded, 16)
                for k in range(2):
                    sp.dma_start(att[:, k, :], w["att"][k:k + 1, :].to_broadcast([P, 16])).then_inc(w_loaded, 16)
                def run(b):
                    i = b.i
                    if b.pre:
                        if not (isinstance(i, int) and i < 1):
                            wait_alone(sp, centred, i, sp_passed)
                        sp.dma_start(xt[1 - b.par][:, :, :], x_dram[bass.ds(i + 1, 1)].rearrange("o p (c t) -> (o p) c t", c=CT)).then_inc(x_loaded[1 - b.par], 16)
                    if b.post:
                        wait_alone(sp, x2_made, i * 2, sp_passed)
                        sp.dma_start(tables["x2"][bass.ds(i - 1, 1)].rearrange("o p (c t) -> (o p) c t", c=CT), x2[:, :, :]).then_inc(x2_stored, 16)
                    if b.post:
                        wait_alone(sp, normed2, i, sp_passed)
                        sp.dma_start(tables["xn2"][bass.ds(i - 1, 1)].rearrange("o p (c t) -> (o p) c t", c=CT), xn2[:, :, :]).then_inc(xn2_stored, 16)
                        wait_alone(sp, h_out, i, sp_passed)
                        rows = bass.ds((i - 1) * T, T)
                        sp.dma_start(tables["src"][rows, :].rearrange("(k p) f -> p k f", p=P), hst[:, :, 0:SRC_F]).then_inc(h_stored, 16)
                        sp.dma_start(tables["dst"][rows, :].rearrange("(k p) f -> p k f", p=P), hst[:, :, SRC_F:H_F]).then_inc(h_stored, 16)
                    if b.scan:
                        if b.post:
                            wait_alone(sp, x2_stored, i * 16, sp_passed)
                            wait_alone(sp, centred2, i, sp_passed)
                        sp.dma_start(x2[:, :, :], x_dram[bass.ds(i, 1)].rearrange("o p (c t) -> (o p) c t", c=CT)).then_inc(xres_loaded, 16)
                bodies(sp, run)
                sp.wait_ge(x2_stored, CHUNKS * 16)
                sp.wait_ge(xn2_stored, CHUNKS * 16)
                sp.wait_ge(h_stored, CHUNKS * 32)

            @block.gpsimd
            def _(pool):
                g = nc.gpsimd
                g.memset(mean_w[:, :], 1.0 / (CT * P)).then_inc(const, 1)
                g.memset(eps[:, 0:1], 1e-6).then_inc(const, 1)
                g.memset(eps[:, 1:2], 1e-5).then_inc(const, 1)
                g.memset(eps[:, 2:3], 1.0).then_inc(const, 1)
                g.memset(carry[:, :, :], 0.0).then_inc(const, 1)
                g.memset(upre[:, :, 0:HALO], 0.0).then_inc(const, 1)
                g.memset(keep[:, :], 1.0).then_inc(const, 1)
                g.memset(ident[:, :], 0.0).then_inc(const, 1)
                g.memset(sel[:, :], 0.0).then_inc(const, 1)
                g.memset(chunk_step[:, :], CHUNK).then_inc(const, 1)
                pool.wait_ge(const, 10)
                g.memset(keep[:, 0:CHUNKS + 1:PER_BATCH], 0.0).then_inc(const, 1)
                g.affine_select(out=ident[:, :], in_=ident[:, :], compare_op=ALU.not_equal, fill=1.0, base=0,
                                pattern=[[-1, P]], channel_multiplier=1).then_inc(const, 1)
                for k in range(3):
                    g.affine_select(out=sel[:, :], in_=sel[:, :], compare_op=ALU.not_equal, fill=1.0, base=-32 * k,
                                    pattern=[[-1, 2 * NS]], channel_multiplier=1).then_inc(const, 1)
                    pool.wait_ge(const, 13 + k)
                def load_ends(c):
                    g.dma_start(end_idx[:, :], ends_at_dram[bass.ds(c * CHUNK, CHUNK), :].rearrange("(p c) o -> p (c o)", p=P)).then_inc(idx_loaded, 16)

                def scatter(k):
                    g.indirect_dma_start(ends_dram, bass.IndirectOffsetOnAxis(ap=end_idx[:, k:k + 1].bitcast(U32), axis=0),
                                         end_pos[:, k:k + 1], None, bounds_check=GROUPS + OFF - 1, oob_is_err=False).then_inc(scattered, 16)

                g.iota(end_pos[:, :], pattern=[[1, CW]], base=1 + CHUNKS * CHUNK, channel_multiplier=CW).then_inc(pos_made, 1)
                beyond = pool.value_load(counts[0:1, 1:2], min_val=1, max_val=EDGES // CHUNK - CHUNKS)
                with pool.Fori(0, beyond) as done:
                    load_ends(done + CHUNKS)
                    wait_alone(pool, idx_loaded, done * 16 + 16, pool_passed)
                    wait_alone(pool, pos_made, done + 1, pool_passed)
                    for k in range(CW):
                        scatter(k)
                    wait_alone(pool, scattered, done * (16 * CW) + 16 * CW, pool_passed)
                    g.tensor_tensor(end_pos[:, :], end_pos[:, :], chunk_step[:, :], ALU.add).then_inc(pos_made, 1)
                wait_alone(pool, pos_made, beyond + 1, pool_passed)
                g.iota(end_pos[:, :], pattern=[[1, CW]], base=1, channel_multiplier=CW).then_inc(pos_made, 1)

                def run(b):
                    if not b.scan:
                        return
                    i = b.i
                    done = beyond + i
                    load_ends(i)
                    wait_alone(pool, idx_loaded, done * 16 + 16, pool_passed)
                    wait_alone(pool, pos_made, done + 2, pool_passed)
                    scatters = iter(range(CW))
                    for s in range(STEPS):
                        if s in POOL_STEPS:
                            group, d = divmod(s, DT)
                            if s >= 4 or not (isinstance(i, int) and i == 0):
                                wait_alone(pool, summed, i * STEPS + s - 3, pool_passed)
                            wait_alone(pool, du_made, i * 4 + d + 1, pool_passed)
                            wait_alone(pool, bc_made, i * 32 + 8 * group + GQ, pool_passed)
                            g.tensor_tensor(hb[s % 4][:, :, :], bb[group % 2][:, :, :], du[:, d:d + 1, :].to_broadcast([P, GQ, T]), ALU.mult).then_inc(pool_dbu_made, 1)
                            for k in range(CW // len(POOL_STEPS)):
                                scatter(next(scatters))
                    wait_alone(pool, scattered, done * (16 * CW) + 16 * CW, pool_passed)
                    g.tensor_tensor(end_pos[:, :], end_pos[:, :], chunk_step[:, :], ALU.add).then_inc(pos_made, 1)
                bodies(pool, run)

            @block.vector
            def _(dve):
                v = nc.vector
                st = Steps(dve, setup)
                dve.wait_ge(w_loaded, 16 * 12)
                dve.wait_ge(const, 15)
                for d in range(DT):
                    for k in range(TAPS):
                        st(v.tensor_scalar(diag[:, d * TAPS + k, :], ident[:, :], w_conv[:, d, k:k + 1], None, ALU.mult))
                for c in range(CT):
                    for k in range(2):
                        st(v.tensor_tensor(w_att[:, c, k, :], w_g[:, c, 0:16], att[:, k, :], ALU.mult))
                st.settle()
                for c in range(CT):
                    (v.tensor_reduce(w_g[:, c, 16:24], w_att[:, c, :, :].rearrange("p k (h e) -> p (k h) e", e=4),
                                       mybir.AxisListType.X, ALU.add)).then_inc(weights_made, 1)
                dve.wait_ge(weights_made, 1 + CT)
                v.tensor_scalar(a_neg[:, :, :], a_neg[:, :, :], -1.0, None, ALU.mult).then_inc(weights_made, 1)

                def piece(b, name):
                    i, n, l = b.i, b.i + 1, b.i - 1
                    if name == "centre":
                        s = b.slot("mean")
                        dve.wait_ge(pre_full, n * 19 + 1)
                        if b.scan:
                            dve.wait_ge(delta_made, b.i * 4 + 2)
                        v.tensor_tensor(xn[:, :, :], xt[1 - b.par][:, :, :], psg[s][:, None, :].to_broadcast([P, CT, T]), ALU.subtract).then_inc(centred, 1)
                    elif name == "norm":
                        dve.wait_ge(rstd_made, n * 2 + 2)
                        v.tensor_tensor(xn[:, :, :], xn[:, :, :], rs[:, None, :].to_broadcast([P, CT, T]), ALU.mult).then_inc(normed, 1)
                    elif name == "low_parts":
                        s = b.slot("dbc")
                        dve.wait_ge(dbc_out, n * 2 + 2)
                        v.tensor_tensor(rest[32:64, :], psg[s][32:64, :], parts[1 - b.par][32:64, :], ALU.subtract).then_inc(rest_made, 1)
                    elif name == "lowest_part":
                        dve.wait_ge(mid_made, n * 2 + 2)
                        v.tensor_tensor(parts[1 - b.par][0:32, :], rest[32:64, :], mid[32:64, :], ALU.subtract).then_inc(parts_made, 1)
                    elif name == "y":
                        for d in range(DT):
                            dve.wait_ge(summed, l * STEPS + STEPS - DT + d + 1)
                            v.scalar_tensor_tensor(yt[:, d, :], u[1 - b.par][:, d, :], skip[:, d:d + 1], psy[:, d, :],
                                                   ALU.mult, ALU.add).then_inc(y_read, 1)
                        dve.wait_ge(y_read, l * 4 + 4)
                        v.tensor_tensor(yt[:, :, :], yt[:, :, :], sres[1 - b.par][:, :, :], ALU.mult).then_inc(gated, 1)
                    elif name == "x2":
                        for c in range(CT):
                            s = b.slot(f"out{c}")
                            dve.wait_ge(post_full, l * 5 + c + 1)
                            if c == 0:
                                dve.wait_ge(xres_loaded, l * 16 + 16)
                            v.tensor_tensor(x2[:, c, :], psg[s][:, :], x2[:, c, :], ALU.add).then_inc(x2_made, 1)
                    elif name == "centre2":
                        s = b.slot("mean2")
                        dve.wait_ge(post_full, l * 5 + 3)
                        v.tensor_tensor(xn2[:, :, :], x2[:, :, :], psg[s][:, None, :].to_broadcast([P, CT, T]), ALU.subtract).then_inc(centred2, 1)
                    elif name == "norm2":
                        dve.wait_ge(rstd2_made, l * 2 + 2)
                        v.tensor_tensor(xn2[:, :, :], xn2[:, :, :], rs2[:, None, :].to_broadcast([P, CT, T]), ALU.mult).then_inc(normed2, 1)

                def deltas(c, par, d):
                    dve.wait_ge(soft_made, c * 4 + d + 1)
                    v.tensor_tensor(delta[:, d, :], delta[:, d, :], soft[d], ALU.add).then_inc(delta_made, 1)
                    dve.wait_ge(delta_made, c * 4 + d + 1)
                    if not (isinstance(c, int) and c == 0):
                        if STEPS - DT + d in POOL_STEPS:
                            dve.wait_ge(pool_dbu_made, c * len(POOL_STEPS))
                        else:
                            dve.wait_ge(dbu_made, (c - 1) * len(OWN_STEPS) + OWN_STEPS.index(STEPS - DT + d) + 1)
                    v.tensor_tensor(du[:, d, :], delta[:, d, :], u[par][:, d, :], ALU.mult).then_inc(du_made, 1)

                def inputs(i, s):
                    if s in POOL_STEPS:
                        return
                    g, d = divmod(s, DT)
                    if s >= 4 or not (isinstance(i, int) and i == 0):
                        dve.wait_ge(summed, i * STEPS + s - 3)
                    if g == 0:
                        dve.wait_ge(du_made, i * 4 + d + 1)
                    dve.wait_ge(bc_made, i * 32 + 8 * g + GQ)
                    v.tensor_tensor(hb[s % 4][:, :, :], bb[g % 2][:, :, :], du[:, d:d + 1, :].to_broadcast([P, GQ, T]), ALU.mult).then_inc(dbu_made, 1)

                def scans(i, s):
                    g, d = divmod(s, DT)
                    if s in POOL_STEPS:
                        dve.wait_ge(pool_dbu_made, i * len(POOL_STEPS) + POOL_STEPS.index(s) + 1)
                    else:
                        dve.wait_ge(dbu_made, i * len(OWN_STEPS) + OWN_STEPS.index(s) + 1)
                    if not (isinstance(i, int) and i == 0):
                        dve.wait_ge(carried, (i - 1) * STEPS + s + 1)
                    for q in range(GQ):
                        dve.wait_ge(da_made, i * 64 + GQ * s + q + 1)
                        v.tensor_tensor_scan(hb[s % 4][:, q, :], da[s % 2][:, q, :], hb[s % 4][:, q, :],
                                             carry[:, d, GQ * g + q:GQ * g + q + 1], ALU.mult, ALU.add).then_inc(scanned, 1)

                def carries(b, s):
                    g, d = divmod(s, DT)
                    i = b.i
                    dve.wait_ge(scanned, i * 64 + GQ * (s + 1))
                    v.tensor_scalar(carry[:, d, GQ * g:GQ * (g + 1)], hb[s % 4][:, :, T - 1], keep[:, bass.ds(i + 1, 1)], None,
                                    ALU.mult).then_inc(carried, 1)

                def outputs(i, s):
                    g, d = divmod(s, DT)
                    dve.wait_ge(carried, i * STEPS + s + 1)
                    dve.wait_ge(bc_made, i * 32 + 8 * (g + 1))
                    v.tensor_tensor(hb[s % 4][:, :, :], hb[s % 4][:, :, :], cb[g % 2][:, :, :], ALU.mult).then_inc(products, 1)

                def run(b):
                    at = lambda s: [n for n, k in VEC_AT.items() if k == s and (b.post if n.endswith("2") else b.pre)]

                    def made(s):
                        for d in range(DT):
                            if DELTA_AT[d] == s and b.pre:
                                deltas(b.i + 1, 1 - b.par, d)
                            if DELTA_AT[d] == s + STEPS and b.scan:
                                deltas(b.i, b.par, d)
                    if b.post:
                        piece(b, "y")
                    if b.scan:
                        inputs(b.i, 0)
                        scans(b.i, 0)
                        for s in range(STEPS):
                            if s + 1 < STEPS:
                                inputs(b.i, s + 1)
                            carries(b, s)
                            if s + 1 < STEPS:
                                scans(b.i, s + 1)
                            outputs(b.i, s)
                            made(s)
                            for name in at(s):
                                piece(b, name)
                    else:
                        for s in range(STEPS):
                            made(s)
                            for name in at(s):
                                piece(b, name)
                    if b.post:
                        dve.wait_ge(xn2_stored, b.i * 16)
                bodies(dve, run)

            @block.tensor
            def _(pe):
                mm = nc.tensor.matmul
                pe.wait_ge(weights_made, 2 + CT)
                pe.wait_ge(const, 15)

                def read(name, n, l):
                    tile = int(name[-1]) if name[-1].isdigit() else 0
                    for prefix, made, value in (
                            ("mean2", centred2, l + 1), ("var2", rstd2_made, l * 2 + 1), ("h", h_out, l + 1),
                            ("out", x2_made, l * 2 + tile + 1), ("mean", centred, n + 1), ("var", rstd_made, n * 2 + 1),
                            ("u", upre_made, n * 5 + tile + 1), ("conv", u_made, n * 4 + tile + 1),
                            ("res", res_made, n * 4 + tile + 1), ("dbc", rest_made, n + 1),
                            ("dt", relu_made, n * 4 + tile + 1)):
                        if name.startswith(prefix):
                            pe.wait_ge(made, value)
                            if prefix == "dt":
                                pe.wait_ge(abs_made, n * 8 + 2 * tile + 1)
                            return

                def use(b, name):
                    i, n, l = b.i, b.i + 1, b.i - 1
                    k = b.order.index(name)
                    ps = psg[b.slot(name)]
                    nxt = 1 - b.par
                    if k >= 2:
                        read(b.order[k - 2], n, l)
                    elif b.before:
                        read(b.before[k], i, l - 1)
                    kind, d = (name[:-1], int(name[-1])) if name[-1].isdigit() and name not in ("mean2", "var2") else (name, 0)
                    if kind == "mean":
                        pe.wait_ge(x_loaded[nxt], b.next_pair * 16 + 16)
                        terms = [(mean_w[:, :], xt[nxt][:, c, :]) for c in range(CT)]
                    elif kind == "var":
                        pe.wait_ge(squared, n + 1)
                        terms = [(mean_w[:, :], sq[:, c, :]) for c in range(CT)]
                    elif kind == "u" or kind == "res":
                        pe.wait_ge(normed, n + 1)
                        e = (d + DT * (kind == "res")) * P
                        terms = [(w_in[:, c, e:e + P], xn[:, c, :]) for c in range(CT)]
                    elif kind == "conv":
                        pe.wait_ge(upre_made, n * 5 + d + 1)
                        terms = [(diag[:, d * TAPS + t, :], upre[:, d, t:t + T]) for t in range(TAPS)]
                    elif kind == "dbc":
                        pe.wait_ge(u_made, n * 4 + 4)
                        terms = [(w_x[:, c, :], u[nxt][:, c, :]) for c in range(DT)]
                        ps = ps[0:64, :]
                    elif kind == "dt":
                        pe.wait_ge(dbc_out, n * 2 + 1)
                        terms = [(w_dt[:, d * P:(d + 1) * P], dtr[:, :])]
                    elif kind == "out":
                        pe.wait_ge(gated, l + 1)
                        terms = [(w_out[:, c, d * P:(d + 1) * P], yt[:, c, :]) for c in range(DT)]
                    elif kind == "mean2":
                        pe.wait_ge(x2_made, l * 2 + 2)
                        terms = [(mean_w[:, :], x2[:, c, :]) for c in range(CT)]
                    elif kind == "var2":
                        pe.wait_ge(squared2, l + 1)
                        terms = [(mean_w[:, :], sq[:, c, :]) for c in range(CT)]
                    elif kind == "h":
                        pe.wait_ge(normed2, l + 1)
                        for t in range(T // P):
                            for c in range(CT):
                                last = mm(ps[:, t * H_F:(t + 1) * H_F], xn2[:, c, t * P:(t + 1) * P], w_g[:, c, :],
                                          start=(c == 0), stop=(c == CT - 1))
                        last.then_inc(post_full, 1)
                        return
                    out = ps if kind == "dbc" else ps[:, :]
                    for k, (a, x) in enumerate(terms):
                        last = mm(out, a, x, start=(k == 0), stop=(k == len(terms) - 1))
                    last.then_inc(pre_full if name in PRE else post_full, 1)

                def broadcast(b, g):
                    i = b.i
                    if g == 0:
                        pe.wait_ge(parts_made, i + 1)
                        pe.wait_ge(mid_made, i * 2 + 2)
                    for k in range(2 * GQ):
                        n = GQ * g + k if k < GQ else NS + GQ * g + k - GQ
                        t = 8 * g + k
                        if t >= 2 or not (isinstance(i, int) and i == 0):
                            pe.wait_ge(bc_made, i * 32 + t - 1)
                        mm(pst[t % 2][:, :], sel[:, n:n + 1].to_broadcast([96, P]), parts[b.par][:, :], start=True, stop=True).then_inc(bc_full, 1)

                def total(b, s):
                    g, d = divmod(s, DT)
                    i = b.i
                    pe.wait_ge(products, i * STEPS + s + 1)
                    if g == 0 and not (isinstance(i, int) and i == 0):
                        pe.wait_ge(y_read, (i - 1) * 4 + d + 1)
                    for q in range(GQ):
                        last = mm(psy[:, d, :], ident[:, :], hb[s % 4][:, q, :], start=(g == 0 and q == 0), stop=(g == NGR - 1 and q == GQ - 1))
                    last.then_inc(summed, 1)

                def run(b):
                    if b.scan:
                        broadcast(b, 0)
                    for s in range(STEPS):
                        if b.scan and s % DT == 1 and s // DT + 1 < NGR:
                            broadcast(b, s // DT + 1)
                        for name in b.order:
                            if PE_AT[name] == s:
                                use(b, name)
                        if b.scan:
                            total(b, s)
                bodies(pe, run)

            @block.scalar
            def _(act):
                f = nc.scalar.activation
                act.wait_ge(w_loaded, 16 * 12)
                act.wait_ge(const, 15)
                nc.scalar.preload_act_table_set(LOG_EXP)
                f(a_neg[:, :, :], a_neg[:, :, :], ACT.Exp).then_inc(weights_made, 1)
                act.wait_ge(weights_made, 2 + CT)

                def piece(b, name):
                    i, n, l = b.i, b.i + 1, b.i - 1
                    nxt = 1 - b.par
                    if name == "square":
                        act.wait_ge(centred, n + 1)
                        if b.scan:
                            act.wait_ge(delta_made, b.i * 4 + 4)
                        if b.post:
                            act.wait_ge(post_full, l * 5 + 4)
                        f(sq[:, :, :], xn[:, :, :], ACT.Square).then_inc(squared, 1)
                    elif name == "rstd":
                        s = b.slot("var")
                        act.wait_ge(pre_full, n * 19 + 2)
                        f(rs[:, :], psg[s][:, :], ACT.Ln, bias=eps[:, 0:1]).then_inc(rstd_made, 1)
                        act.wait_ge(rstd_made, n * 2 + 1)
                        f(rs[:, :], rs[:, :], ACT.Exp, scale=-0.5).then_inc(rstd_made, 1)
                    elif name == "u_out":
                        for d in range(DT):
                            s = b.slot(f"u{d}")
                            act.wait_ge(pre_full, n * 19 + 3 + d)
                            f(upre[:, d, HALO:HALO + T], psg[s][:, :], ACT.Copy).then_inc(upre_made, 1)
                    elif name == "u_silu":
                        for d in range(DT):
                            s = b.slot(f"conv{d}")
                            act.wait_ge(pre_full, n * 19 + 7 + d)
                            if b.post and d == 0:
                                act.wait_ge(gated, l + 1)
                            f(u[nxt][:, d, :], psg[s][:, :], ACT.Silu, bias=conv_b[:, d:d + 1]).then_inc(u_made, 1)
                        nc.scalar.preload_act_table_set(LOG_EXP)
                        f(upre[:, :, 0:HALO], upre[:, :, T:T + HALO], ACT.Copy, scale=keep[:, bass.ds(n + 1, 1)] if not isinstance(n, int) or n + 1 <= CHUNKS else 0.0).then_inc(upre_made, 1)
                    elif name == "res_silu":
                        for d in range(DT):
                            s = b.slot(f"res{d}")
                            act.wait_ge(pre_full, n * 19 + 11 + d)
                            f(sres[nxt][:, d, :], psg[s][:, :], ACT.Silu).then_inc(res_made, 1)
                        nc.scalar.preload_act_table_set(LOG_EXP)
                    elif name == "dbc_out":
                        s = b.slot("dbc")
                        act.wait_ge(pre_full, n * 19 + 15)
                        f(dtr[:, :], psg[s][0:32, :], ACT.Copy).then_inc(dbc_out, 1)
                        f(parts[nxt][32:64, :], psg[s][32:64, :], ACT.Copy).then_inc(dbc_out, 1)
                    elif name == "mid_part":
                        act.wait_ge(rest_made, n + 1)
                        f(mid[32:64, :], rest[32:64, :], ACT.Copy).then_inc(mid_made, 1)
                        act.wait_ge(mid_made, n * 2 + 1)
                        f(parts[nxt][64:96, :], mid[32:64, :], ACT.Copy).then_inc(mid_made, 1)
                    elif name == "square2":
                        act.wait_ge(centred2, l + 1)
                        if b.scan:
                            act.wait_ge(delta_made, b.i * 4 + 4)
                        f(sq[:, :, :], xn2[:, :, :], ACT.Square).then_inc(squared2, 1)
                    elif name == "rstd2":
                        s = b.slot("var2")
                        act.wait_ge(post_full, l * 5 + 4)
                        f(rs2[:, :], psg[s][:, :], ACT.Ln, bias=eps[:, 1:2]).then_inc(rstd2_made, 1)
                        act.wait_ge(rstd2_made, l * 2 + 1)
                        f(rs2[:, :], rs2[:, :], ACT.Exp, scale=-0.5).then_inc(rstd2_made, 1)
                    elif name == "h_out":
                        s = b.slot("h")
                        act.wait_ge(post_full, l * 5 + 5)
                        f(hst[:, :, :], psg[s][:, 0:T // P * H_F], ACT.Copy).then_inc(h_out, 1)

                def softs(c, bank, d):
                    act.wait_ge(pre_full, c * 19 + 16 + d)
                    if not (isinstance(c, int) and c == 0):
                        act.wait_ge(da_made, (c - 1) * 64 + GQ * (STEPS - DT + d + 1))
                    f(soft[d], psg[bank][:, :], ACT.Abs, bias=dt_b[:, d:d + 1]).then_inc(abs_made, 1)
                    f(delta[:, d, :], psg[bank][:, :], ACT.Relu, bias=dt_b[:, d:d + 1]).then_inc(relu_made, 1)
                    act.wait_ge(relu_made, c * 4 + d + 1)
                    f(soft[d], soft[d], ACT.Exp, scale=-1.0).then_inc(abs_made, 1)
                    act.wait_ge(abs_made, c * 8 + 2 * d + 2)
                    f(soft[d], soft[d], ACT.Ln, bias=eps[:, 2:3]).then_inc(soft_made, 1)

                def spread(b, g, which):
                    i = b.i
                    if g >= 2:
                        act.wait_ge(products, i * STEPS + (g - 1) * DT)
                    elif not (isinstance(i, int) and i == 0):
                        act.wait_ge(products, (i - 1) * STEPS + (g + 3) * DT)
                    dst = (bb, cb)[which][g % 2]
                    for q in range(GQ):
                        t = 8 * g + GQ * which + q
                        act.wait_ge(bc_full, i * 32 + t + 1)
                        f(dst[:, q, :], pst[t % 2][:, :], ACT.Copy).then_inc(bc_made, 1)

                def decays(b, s):
                    g, d = divmod(s, DT)
                    i = b.i
                    if g == 0:
                        act.wait_ge(delta_made, i * 4 + d + 1)
                    if s >= 2:
                        act.wait_ge(scanned, i * 64 + GQ * (s - 1))
                    elif not (isinstance(i, int) and i == 0):
                        act.wait_ge(scanned, (i - 1) * 64 + GQ * (s + 15))
                    for q in range(GQ):
                        n = GQ * g + q
                        f(da[s % 2][:, q, :], delta[:, d, :], ACT.Exp, scale=a_neg[:, d, n:n + 1]).then_inc(da_made, 1)

                def run(b):
                    at = lambda s: [n for n, k in ACT_AT.items() if k == s and (b.post if n in ("square2", "rstd2", "h_out") else b.pre)]
                    if b.scan:
                        spread(b, 0, 0)
                    for s in range(STEPS):
                        if b.scan:
                            decays(b, s)
                            if s == 0:
                                spread(b, 0, 1)
                            if s % DT == 2 and s // DT + 1 < NGR:
                                spread(b, s // DT + 1, 0)
                                spread(b, s // DT + 1, 1)
                        for d in range(DT):
                            if SOFT_AT[d] == s and b.pre:
                                softs(b.i + 1, b.slot(f"dt{d}"), d)
                            if SOFT_AT[d] == s + STEPS and b.scan:
                                softs(b.i, (b.first + d) % 2, d)
                        for name in at(s):
                            piece(b, name)
                    if b.post:
                        act.wait_ge(h_stored, b.i * 32)
                bodies(act, run)

HEADS = 4
EXPERTS = 4
GH = HEADS * EXPERTS
SEG_F = GH + HEADS + HEADS
NT = NODES // P
BIG = 1e30
PEAKS_AT, PEAK_LANES_AT, SUMS_AT, SUM_LANES_AT, GRAPH_STEPS = 12, 14, 54, 56, 78
AX = mybir.AxisListType.X

FF = 512
FT = FF // P
UNITS = EXPERTS * FT
RING = 4
LAG = 3
BESIDE_EDGES, BESIDE_GATES = 6, 2
EARLY = 2 * (BESIDE_EDGES + BESIDE_GATES)
PE_UNIT = {"peaks": 2, "peak_lanes": 3, "sums": 9, "sum_lanes": 10}
ACT_UNIT = {"exps": 5, "store": 15}


class EarlyExperts:

    def __init__(self, nc, sb, sem, weights, xn2_dram, y_dram, ps_up, ps_down):
        self.nc, self.xn2_dram, self.y_dram, self.ps_up, self.ps_down = nc, xn2_dram, y_dram, ps_up, ps_down
        self.w1, self.w2, self.b1, self.b2, self.w_loaded = weights
        self.xn = [sb(f"e_xn{k}", [P, CT, T]) for k in range(2)]
        self.hid = [sb(f"e_hid{k}", [P, T]) for k in range(RING)]
        self.y = [sb(f"e_y{e}", [P, CT, T]) for e in range(EXPERTS)]
        self.loaded = [sem(f"e_xn_loaded{k}") for k in range(2)]
        self.y_stored = [sem(f"e_y_stored{e}") for e in range(EXPERTS)]
        self.up, self.gelu, self.down, self.y_out = sem("e_up_full"), sem("e_gelu_made"), sem("e_down_done"), sem("e_y_out")

    def load(self, sp, n, par, passed):
        if not (isinstance(n, int) and n == 0):
            wait_alone(sp, self.gelu, (n * 2 + (par - 1)) * UNITS, passed)
        sp.dma_start(self.xn[par][:, :, :], self.xn2_dram[bass.ds(n * 2 + par, 1)].rearrange("o p (c t) -> (o p) c t", c=CT)).then_inc(self.loaded[par], 16)

    def products(self, pe, n, par, beside=lambda k: None):
        mm = self.nc.tensor.matmul
        c = n * 2 + par
        later = not (isinstance(c, int) and c == 0)
        pe.wait_ge(self.loaded[par], n * 16 + 16)
        for k in range(UNITS + LAG):
            beside(k)
            if k < UNITS:
                e, ft = divmod(k, FT)
                if k >= RING or later:
                    pe.wait_ge(self.gelu, c * UNITS + (k - RING + 1))
                for t in range(CT):
                    last = mm(self.ps_up[k % RING][:, :], self.w1[:, e, t, ft * P:(ft + 1) * P], self.xn[par][:, t, :], start=(t == 0), stop=(t == CT - 1))
                last.then_inc(self.up, 1)
            if k >= LAG:
                q = k - LAG
                e, ft = divmod(q, FT)
                pe.wait_ge(self.gelu, c * UNITS + (q + 1))
                if ft == 0 and (e > 0 or later):
                    pe.wait_ge(self.y_out, c * (CT * EXPERTS) + CT * e)
                for t in range(CT):
                    last = mm(self.ps_down[t][:, :], self.w2[:, q, t * P:(t + 1) * P], self.hid[q % RING][:, :], start=(ft == 0), stop=(ft == FT - 1))
                last.then_inc(self.down, 1)

    def gelus(self, act, n, par, beside=lambda k: None):
        f = self.nc.scalar.activation
        c = n * 2 + par
        later = not (isinstance(c, int) and c == 0)
        for k in range(UNITS + LAG):
            beside(k)
            if k < UNITS:
                act.wait_ge(self.up, c * UNITS + (k + 1))
                if k >= RING or later:
                    act.wait_ge(self.down, c * UNITS + (k - RING + 1))
                f(self.hid[k % RING][:, :], self.ps_up[k % RING][:, :], ACT.Gelu, bias=self.b1[:, k:k + 1]).then_inc(self.gelu, 1)
            if k >= LAG and (k - LAG) % FT == FT - 1:
                e = (k - LAG) // FT
                act.wait_ge(self.down, c * UNITS + (e + 1) * FT)
                if later:
                    act.wait_ge(self.y_stored[e], c * 16)
                for t in range(CT):
                    f(self.y[e][:, t, :], self.ps_down[t][:, :], ACT.Identity, bias=self.b2[:, e * CT + t:e * CT + t + 1]).then_inc(self.y_out, 1)
                act.wait_ge(self.y_out, c * (CT * EXPERTS) + CT * (e + 1))
                act.dma_start(self.y_dram[bass.ds(c, 1), :, e * CT * T:(e + 1) * CT * T].rearrange("o p (c t) -> (o p) c t", c=CT), self.y[e][:, :, :]).then_inc(self.y_stored[e], 16)


def attention(nc, keys_dram, src_dram, dst_dram, ends_dram, tables, w, seg_dram, gates_dram, counts, weights, y_dram):
    with ExitStack() as ctx:
        sb = lambda name, shape, dt=F32: ctx.enter_context(nc.sbuf_tensor(name, shape, dt))
        sem = lambda name: ctx.enter_context(nc.semaphore(name))
        pair = lambda name, shape, dt=F32: [sb(f"{name}{k}", shape, dt) for k in range(2)]
        ident, ones = sb("g_ident", [P, P]), sb("g_ones", [P, P])
        zero_row, eps = sb("zero_row", [P, CW]), sb("g_eps", [P, 1])
        ends_i = sb("ends_i", [P, 2, NT], I32)
        ends = sb("ends_f", [P, 2, NT + 1])
        tail_row, last = sb("tail_row", [1, 2 * P]), sb("carry_row", [1, 2 * P + 1])
        node_q = sb("node_q", [P, 3, NT])
        end_idx = sb("g_end_idx", [P, NT], I32)
        has0, none0, none1 = sb("has0", [P, NT]), sb("none0", [P, NT]), sb("none1", [P, NT])
        count1 = sb("count1", [P, NT])
        s_idx, d_idx = pair("s_idx", [P, CW], I32), pair("d_idx", [P, CW], I32)
        keys, prev = pair("keys", [P, CW], I32), pair("prev_keys", [P, CW], I32)
        grow, arow = pair("src_rows", [P, CW, SRC_F]), pair("dst_rows", [P, CW, DST_F])
        start, fresh, same, seen = (sb(n, [P, CW]) for n in ("start", "fresh", "same", "seen"))
        peak = sb("peak", [P, HEADS, CW + 1])
        tails, tail_t, lanes = sb("tails", [P, 2 * HEADS]), sb("tails_t", [HEADS, 2 * P]), sb("lane_peaks", [HEADS, P + 1])
        score = sb("score", [P, 3, HEADS * CW])
        expo = sb("expo", [P, 2, HEADS * CW])
        vals, decay = sb("vals", [P, SRC_F, CW]), sb("decay", [P, HEADS, CW])
        prod = sb("prod", [P, HEADS, CW])
        seg = pair("seg", [P, CW, SEG_F])
        stails, stail_t = sb("stails", [P, 2 * SRC_F]), sb("stails_t", [SRC_F, 2 * P])
        slanes, scarry = sb("lane_sums", [SRC_F, P + 1]), sb("scarry", [P, SRC_F])
        psa = ctx.enter_context(nc.psum_tensor("ps_tails", [P, 512], F32))
        psb = ctx.enter_context(nc.psum_tensor("ps_back", [P, 512], F32))
        ps_down = [ctx.enter_context(nc.psum_tensor(f"ps_early_down{k}", [P, 512], F32)) for k in range(CT)]
        psc = [ctx.enter_context(nc.psum_tensor(f"ps_nodes{k}", [P, 512], F32)) for k in range(4)]

        const, ends_loaded = sem("g_const"), sem("ends_loaded")
        node_steps, graph_steps, node_t = sem("node_steps"), sem("graph_steps"), sem("node_transposed")
        idx_loaded, keys_loaded = [sem(f"g_idx_loaded{k}") for k in range(2)], [sem(f"keys_loaded{k}") for k in range(2)]
        gathered = [sem(f"gathered{k}") for k in range(2)]
        started, seg_made = sem("starts_made"), sem("seg_made")
        tails_t, weights_made = sem("tails_transposed"), sem("weights_exp")
        expo_made = sem("expo_made")
        seg_stored = [sem(f"seg_stored{k}") for k in range(2)]

        early = EarlyExperts(nc, sb, sem, weights, tables["xn2"], y_dram, psc, ps_down)

        def chunks(eng, run):
            n = eng.value_load(counts[0:1, 0:1], min_val=BESIDE_EDGES + 1, max_val=EDGES // CHUNK)
            run(0, 0, True)
            run(1, 1, True)
            with eng.Fori(1, BESIDE_EDGES // 2) as j:
                run(j * 2, 0, True)
                run(j * 2 + 1, 1, True)
            with eng.Fori(BESIDE_EDGES, n, 2) as c:
                c = c.with_bounds(min_val=BESIDE_EDGES, max_val=EDGES // CHUNK - 2)
                run(c, 0, False)
                run(c + 1, 1, False)

        sp_passed, pool_passed, pe_passed = sem("g_sp_passed"), sem("g_pool_passed"), sem("g_pe_passed")
        with nc.Block() as block:
            @block.gpsimd
            def _(pool):
                g = nc.gpsimd
                g.memset(ones[:, :], 1.0).then_inc(const, 1)
                g.memset(zero_row[:, :], 0.0).then_inc(const, 1)
                g.memset(last[:, 0:1], 0.0).then_inc(const, 1)
                g.memset(lanes[:, 0:1], -BIG).then_inc(const, 1)
                g.memset(slanes[:, 0:1], 0.0).then_inc(const, 1)
                pool.wait_ge(const, 1)
                g.affine_select(out=ident[:, :], in_=ones[:, :], compare_op=ALU.is_equal, fill=0.0, base=0,
                                pattern=[[-1, P]], channel_multiplier=1).then_inc(const, 1)

                def run(n, par, experts):
                    first = isinstance(n, int)
                    wait_alone(pool, idx_loaded[par], 32 if first else (n - par) * 16 + 32, pool_passed)
                    if not first:
                        wait_alone(pool, seg_made, n - 1, pool_passed)
                    for k in range(CW):
                        g.indirect_dma_start(grow[par][:, k, :], None, tables["src"], bass.IndirectOffsetOnAxis(ap=s_idx[par][:, k:k + 1].bitcast(U32), axis=0)).then_inc(gathered[par], 16)
                        g.indirect_dma_start(arow[par][:, k, :], None, tables["dst"], bass.IndirectOffsetOnAxis(ap=d_idx[par][:, k:k + 1].bitcast(U32), axis=0)).then_inc(gathered[par], 16)
                chunks(pool, run)

            @block.sync
            def _(sp):
                w1, w2, b1, b2, w_loaded = weights
                sp.dma_start(ends_i[:, :, :], ends_dram[OFF:OFF + GROUPS, :].rearrange("(k q c) o -> q k (c o)", k=2, q=P)).then_inc(ends_loaded, 16)
                for t, d in ((w1[:, :, :, :], w["w1"].rearrange("e (c p) f -> p (e c) f", p=P)), (w2[:, :, :], w["w2"].rearrange("e (c p) d -> p (e c) d", p=P)),
                             (b1[:, :], w["b1"]), (b2[:, :], w["b2_lanes"])):
                    sp.dma_start(t, d).then_inc(w_loaded, 16)

                def run(n, par, experts):
                    first = isinstance(n, int)
                    if not first:
                        wait_alone(sp, gathered[par], (n - par) * (16 * CW), sp_passed)
                        wait_alone(sp, started, n - 1, sp_passed)
                    at = lambda t, off: t[bass.ds(n * CHUNK + off, CHUNK), :].rearrange("(p c) o -> p (c o)", p=P)
                    sp.dma_start(s_idx[par][:, :], at(src_dram, 0)).then_inc(idx_loaded[par], 16)
                    sp.dma_start(d_idx[par][:, :], at(dst_dram, 0)).then_inc(idx_loaded[par], 16)
                    sp.dma_start(keys[par][:, :], at(keys_dram, 1)).then_inc(keys_loaded[par], 16)
                    sp.dma_start(prev[par][:, :], at(keys_dram, 0)).then_inc(keys_loaded[par], 16)
                    if experts:
                        early.load(sp, n, 0, sp_passed)
                        early.load(sp, n, 1, sp_passed)
                chunks(sp, run)

            @block.vector
            def _(dve):
                v = nc.vector
                st = Steps(dve, node_steps)

                def do(instruction):
                    st(instruction)
                    st.settle()
                dve.wait_ge(ends_loaded, 16)
                dve.wait_ge(const, 6)
                do(v.tensor_copy(node_q[:, 0:2, :], ends_i[:, :, :]))
                for k in range(2):
                    do(v.tensor_tensor_scan(ends[:, k, 1:NT + 1], node_q[:, k, :], node_q[:, k, :], 0.0, ALU.max, ALU.max))
                ends_tail = st.n
                dve.wait_ge(node_t, 2)
                do(v.tensor_copy(tail_row[:, :], psa[0:1, 0:2 * P]))
                do(v.tensor_tensor_scan(last[:, 1:2 * P + 1], tail_row[:, :], tail_row[:, :], last[:, 0:1], ALU.max, ALU.max))
                dve.wait_ge(node_t, 4)
                do(v.tensor_copy(ends[:, :, 0], psb[:, 0:2]))
                for k in range(2):
                    do(v.tensor_scalar(ends[:, k, 1:NT + 1], ends[:, k, 1:NT + 1], ends[:, k, 0:1], None, ALU.max))
                do(v.tensor_tensor(node_q[:, 1:3, :], ends[:, :, 1:NT + 1], ends[:, :, 0:NT], ALU.subtract))
                do(v.tensor_scalar(node_q[:, 0, :], ends[:, 0, 1:NT + 1], -1.0, 0.0, ALU.add, ALU.max))
                dve.wait_ge(node_t, 7)
                do(v.tensor_copy(end_idx[:, :], psc[0][:, 0:NT]))
                do(v.tensor_scalar(has0[:, :], psc[1][:, 0:NT], 0.0, None, ALU.is_gt))
                do(v.tensor_copy(count1[:, :], psc[2][:, 0:NT]))
                do(v.tensor_scalar(none0[:, :], has0[:, :], -1.0, BIG, ALU.add, ALU.mult))
                do(v.tensor_scalar(none1[:, :], count1[:, :], 0.0, None, ALU.is_gt))
                do(v.tensor_scalar(none1[:, :], none1[:, :], -1.0, BIG, ALU.add, ALU.mult))

                def run(n, par, experts):
                    st = Steps(dve, graph_steps, n * GRAPH_STEPS)
                    first = isinstance(n, int)
                    pairs = 0 if first else n - par

                    def do(instruction):
                        st(instruction)
                        st.settle()
                    gf = grow[par][:, :, :].rearrange("p c f -> p f c")
                    af = arow[par][:, :, :].rearrange("p c f -> p f c")
                    a_src = gf[:, GH:SRC_F, :]
                    out = seg[par][:, :, :].rearrange("p c f -> p f c")
                    heads = lambda t: t.rearrange("p (h c) -> p h c", h=HEADS)
                    dve.wait_ge(keys_loaded[par], pairs * 16 + 32)
                    st(v.tensor_scalar(keys[par][:, :], keys[par][:, :], SRC_BITS, None, ALU.logical_shift_right))
                    do(v.tensor_scalar(prev[par][:, :], prev[par][:, :], SRC_BITS, None, ALU.logical_shift_right))
                    v.tensor_tensor(start[:, :], keys[par][:, :], prev[par][:, :], ALU.not_equal).then_inc(started, 1)
                    dve.wait_ge(started, n + 1)
                    st(v.tensor_scalar(fresh[:, :], start[:, :], -BIG, None, ALU.mult))
                    st(v.tensor_scalar(same[:, :], start[:, :], -1.0, 1.0, ALU.mult, ALU.add))
                    do(v.tensor_tensor_scan(seen[:, :], start[:, :], start[:, :], 0.0, ALU.max, ALU.max))
                    do(v.tensor_scalar(seen[:, :], seen[:, :], -BIG, None, ALU.mult))
                    dve.wait_ge(gathered[par], pairs * (16 * CW) + 32 * CW)
                    for h in range(HEADS):
                        st(v.tensor_tensor_scan(peak[:, h, 1:CW + 1], fresh[:, :], a_src[:, h, :], -BIG, ALU.add, ALU.max))
                    st.settle()
                    st(v.tensor_copy(tails[:, 0:HEADS], peak[:, :, CW]))
                    st(v.tensor_copy(tails[:, HEADS:2 * HEADS], seen[:, CW - 1:CW].to_broadcast([P, HEADS])))
                    dve.wait_ge(tails_t, n * 6 + 2)
                    do(v.tensor_copy(tail_t[:, :], psa[0:HEADS, 0:2 * P]))
                    do(v.tensor_tensor_scan(lanes[:, 1:P + 1], tail_t[:, P:2 * P], tail_t[:, 0:P], lanes[:, 0:1], ALU.add, ALU.max))
                    dve.wait_ge(tails_t, n * 6 + 3)
                    st(v.tensor_copy(peak[:, :, 0], psb[:, 0:HEADS]))
                    do(v.tensor_copy(lanes[:, 0:1], lanes[:, P:P + 1]))
                    for h in range(HEADS):
                        st(v.scalar_tensor_tensor(peak[:, h, 1:CW + 1], seen[:, :], peak[:, h, 0:1], peak[:, h, 1:CW + 1], ALU.add, ALU.max))
                    st.settle()
                    st(v.tensor_tensor(heads(score[:, 0, :]), a_src, af, ALU.add))
                    st(v.tensor_tensor(heads(score[:, 1, :]), peak[:, :, 1:CW + 1], af, ALU.add))
                    do(v.tensor_tensor(heads(score[:, 2, :]), peak[:, :, 0:CW], af, ALU.add))
                    do(v.scalar_tensor_tensor(score[:, :, :], score[:, :, :], 0.2, score[:, :, :], ALU.mult, ALU.max))
                    do(v.tensor_tensor(expo[:, :, :], score[:, 0:3:2, :], score[:, 1:2, :].to_broadcast([P, 2, HEADS * CW]), ALU.subtract))
                    v.tensor_scalar(expo[:, :, :], expo[:, :, :], 0.0, None, ALU.min).then_inc(expo_made, 1)
                    dve.wait_ge(weights_made, n * 2 + 2)
                    st(v.tensor_tensor(decay[:, :, :], decay[:, :, :], same[:, None, :].to_broadcast([P, HEADS, CW]), ALU.mult))
                    per_expert = lambda t: t[:, :, None, :].to_broadcast([P, HEADS, EXPERTS, CW])
                    do(v.tensor_tensor(vals[:, 0:GH, :].rearrange("p (h e) c -> p h e c", h=HEADS), per_expert(vals[:, GH:SRC_F, :]),
                                       gf[:, 0:GH, :].rearrange("p (h e) c -> p h e c", h=HEADS), ALU.mult))
                    if not first:
                        dve.wait_ge(seg_stored[par], pairs * 8)
                    for f in range(SRC_F):
                        h = f // EXPERTS if f < GH else f - GH
                        st(v.tensor_tensor_scan(out[:, f, :], decay[:, h, :], vals[:, f, :], 0.0, ALU.mult, ALU.add))
                    for h in range(HEADS):
                        st(v.tensor_tensor_scan(prod[:, h, :], decay[:, h, :], zero_row[:, :], 1.0, ALU.mult, ALU.add))
                    st.settle()
                    st(v.tensor_copy(stails[:, 0:SRC_F], out[:, 0:SRC_F, CW - 1]))
                    st(v.tensor_copy(stails[:, SRC_F:SRC_F + GH].rearrange("p (h e) -> p h e", h=HEADS), prod[:, :, CW - 1:CW].to_broadcast([P, HEADS, EXPERTS])))
                    st(v.tensor_copy(stails[:, SRC_F + GH:2 * SRC_F], prod[:, :, CW - 1]))
                    dve.wait_ge(tails_t, n * 6 + 5)
                    do(v.tensor_copy(stail_t[:, :], psa[0:SRC_F, 0:2 * P]))
                    do(v.tensor_tensor_scan(slanes[:, 1:P + 1], stail_t[:, P:2 * P], stail_t[:, 0:P], slanes[:, 0:1], ALU.mult, ALU.add))
                    dve.wait_ge(tails_t, n * 6 + 6)
                    st(v.tensor_copy(scarry[:, :], psb[:, 0:SRC_F]))
                    do(v.tensor_copy(slanes[:, 0:1], slanes[:, P:P + 1]))
                    for f in range(SRC_F):
                        h = f // EXPERTS if f < GH else f - GH
                        st(v.scalar_tensor_tensor(out[:, f, :], prod[:, h, :], scarry[:, f:f + 1], out[:, f, :], ALU.mult, ALU.add))
                    st.settle()
                    v.tensor_copy(out[:, SRC_F:SEG_F, :], peak[:, :, 1:CW + 1]).then_inc(seg_made, 1)
                    dve.wait_ge(seg_made, n + 1)
                    assert st.n == GRAPH_STEPS, st.n
                chunks(dve, run)

            @block.tensor
            def _(pe):
                t = nc.tensor.transpose
                pe.wait_ge(const, 6)
                pe.wait_ge(node_steps, 3)
                for k in range(2):
                    t(psa[0:1, k * P:(k + 1) * P], ends[:, k, NT:NT + 1], ident[:, :]).then_inc(node_t, 1)
                pe.wait_ge(node_steps, 5)
                for k in range(2):
                    t(psb[:, k:k + 1], last[0:1, k * P:(k + 1) * P], ident[0:1, 0:1]).then_inc(node_t, 1)
                pe.wait_ge(node_steps, 10)
                for k in range(3):
                    t(psc[k][:, 0:NT], node_q[:, k, :], ident[:, :]).then_inc(node_t, 1)

                def run(n, par, experts):
                    base = n * GRAPH_STEPS

                    def step(name):
                        if name == "peaks":
                            pe.wait_ge(graph_steps, base + PEAKS_AT)
                            for k in range(2):
                                t(psa[0:HEADS, k * P:(k + 1) * P], tails[:, k * HEADS:(k + 1) * HEADS], ident[:, :]).then_inc(tails_t, 1)
                        elif name == "peak_lanes":
                            wait_alone(pe, graph_steps, base + PEAK_LANES_AT, pe_passed)
                            t(psb[:, 0:HEADS], lanes[:, 0:P], ident[0:HEADS, 0:HEADS]).then_inc(tails_t, 1)
                        elif name == "sums":
                            pe.wait_ge(graph_steps, base + SUMS_AT)
                            for k in range(2):
                                t(psa[0:SRC_F, k * P:(k + 1) * P], stails[:, k * SRC_F:(k + 1) * SRC_F], ident[:, :]).then_inc(tails_t, 1)
                        elif name == "sum_lanes":
                            wait_alone(pe, graph_steps, base + SUM_LANES_AT, pe_passed)
                            t(psb[:, 0:SRC_F], slanes[:, 0:P], ident[0:SRC_F, 0:SRC_F]).then_inc(tails_t, 1)

                    def beside(k):
                        for name, unit in PE_UNIT.items():
                            if unit == k:
                                step(name)
                    if experts:
                        early.products(pe, n, 0)
                        early.products(pe, n, 1, beside)
                    else:
                        for name in PE_UNIT:
                            step(name)
                pe.wait_ge(weights[-1], 64)
                pe.wait_ge(node_steps, 13)
                chunks(pe, run)

            @block.scalar
            def _(act):
                act.wait_ge(weights[-1], 64)

                def run(n, par, experts):
                    def step(name):
                        if name == "exps":
                            act.wait_ge(expo_made, n + 1)
                            for k, dst in enumerate((vals[:, GH:SRC_F, :], decay[:, :, :])):
                                nc.scalar.activation(dst, expo[:, k, :].rearrange("p (h c) -> p h c", h=HEADS), ACT.Exp).then_inc(weights_made, 1)
                        else:
                            act.wait_ge(seg_made, n + 1)
                            act.dma_start(seg_dram[bass.ds(n * CHUNK, CHUNK), :].rearrange("(p c) f -> p (c f)", p=P),
                                          seg[par][:, :, :].rearrange("p c f -> p (c f)").bitcast(I32)).then_inc(seg_stored[par], 16)

                    def beside(k):
                        for name, unit in ACT_UNIT.items():
                            if unit == k:
                                step(name)
                    if experts:
                        early.gelus(act, n, 0)
                        early.gelus(act, n, 1, beside)
                    else:
                        step("exps")
                        step("store")
                        if par == 1:
                            for k in range(2):
                                act.wait_ge(seg_stored[k], n * 8 + 8)
                chunks(act, run)

        gate_nodes(nc, ctx, sb, sem, ident, eps, end_idx, has0, none0, none1, count1, psc, seg_dram, tables, w, gates_dram, early)


def gate_nodes(nc, ctx, sb, sem, ident, eps, end_idx, has0, none0, none1, count1, psc, seg_dram, tables, w, gates_dram, early):
    K4 = NT * HEADS
    last_row, gamma, beta, bias = sb("last_row", [P, SRC_F]), sb("gamma", [P, GH]), sb("beta", [P, GH]), sb("b_gat", [P, GH])
    rows, node, ad = sb("seg_rows", [P, NT, SEG_F]), sb("node_rows", [P, NT, SRC_F]), sb("node_dst", [P, NT, DST_F])
    a4 = sb("node_scores", [P, 4, K4])
    wts = sb("node_weights", [P, 3, K4])
    den, agg, tmp = sb("den", [P, K4]), sb("agg", [P, NT * GH]), sb("agg_tmp", [P, NT * GH])
    mean, var = sb("node_mean", [P, NT]), sb("node_var", [P, NT])
    sc, ties = sb("expert_scores", [P, K4]), sb("ties", [P, EXPERTS * EXPERTS])
    beats, even, rank, top = sb("beats", [P, NT * GH]), sb("even", [P, NT * GH]), sb("rank", [P, K4]), sb("top", [P, NT])
    gt = [sb(f"gates_t{k}", [EXPERTS, 512]) for k in range(4)]
    loaded, gathered, steps, exps = sem("node_loaded"), sem("seg_gathered"), sem("gate_steps"), sem("node_exps")
    var_made, gates_t, gates_out = sem("var_made"), sem("gates_transposed"), sem("gates_out")
    stored = [sem(f"gates_stored{k}") for k in range(4)]
    passed = sem("n_sp_passed")
    rest = range(BESIDE_EDGES, BESIDE_EDGES + BESIDE_GATES)
    tie_made, weights_ready, gates_made = sem("ties_made"), sem("node_exponents"), sem("gates_made")

    with nc.Block() as block:
        @block.sync
        def _(sp):
            sp.dma_start(node[:, :, :], tables["src"].rearrange("(k p) f -> p k f", p=P)).then_inc(loaded, 16)
            sp.dma_start(ad[:, :, :], tables["dst"].rearrange("(k p) f -> p k f", p=P)).then_inc(loaded, 16)
            sp.dma_start(last_row[:, :], tables["src"][NODES - 1:NODES, :].to_broadcast([P, SRC_F])).then_inc(loaded, 16)
            for t, d in ((gamma, w["gamma"]), (beta, w["beta"]), (bias, w["b_gat"])):
                sp.dma_start(t[:, :], d.to_broadcast([P, GH])).then_inc(loaded, 16)
            for n in rest:
                early.load(sp, n, 0, passed)
                early.load(sp, n, 1, passed)
            for k in range(NT // 4):
                sp.wait_ge(gates_out, k + 1)
                sp.dma_start(gates_dram[:, k * 512:(k + 1) * 512], gt[k % 4][:, :]).then_inc(stored[k % 4], 16)
            for k in range(4):
                sp.wait_ge(stored[k], NT // 16 * 16)

        @block.gpsimd
        def _(pool):
            g = nc.gpsimd
            g.memset(eps[:, :], 1e-5).then_inc(tie_made, 1)
            g.memset(ties[:, :], 1.0).then_inc(tie_made, 1)
            pool.wait_ge(tie_made, 2)
            g.affine_select(out=ties[:, :].rearrange("p (e j) -> p e j", j=EXPERTS), in_=ties[:, :].rearrange("p (e j) -> p e j", j=EXPERTS),
                            compare_op=ALU.is_gt, fill=0.0, base=0, pattern=[[1, EXPERTS], [-1, EXPERTS]], channel_multiplier=0).then_inc(tie_made, 1)
            for k in range(NT):
                g.indirect_dma_start(rows[:, k, :].bitcast(I32), None, seg_dram, bass.IndirectOffsetOnAxis(ap=end_idx[:, k:k + 1].bitcast(U32), axis=0)).then_inc(gathered, 16)

        @block.vector
        def _(dve):
            v = nc.vector
            st = Steps(dve, steps)

            def do(instruction):
                st(instruction)
                st.settle()
            kh = lambda t: t.rearrange("p (k h) -> p k h", h=HEADS)
            khe = lambda t: t.rearrange("p (k h e) -> p k h e", h=HEADS, e=EXPERTS)
            over_h = lambda t: t[:, :, None].to_broadcast([P, NT, HEADS])
            over_e = lambda t: kh(t)[:, :, :, None].to_broadcast([P, NT, HEADS, EXPERTS])
            over_k = lambda t: t[:, None, :].to_broadcast([P, NT, HEADS])
            a_self, a_last = node[:, :, GH:SRC_F], over_k(last_row[:, GH:SRC_F])
            dve.wait_ge(loaded, 16 * 6)
            do(v.tensor_tensor(kh(a4[:, 1, :]), a_self, ad[:, :, :], ALU.add))
            do(v.tensor_tensor(kh(a4[:, 2, :]), a_last, ad[:, :, :], ALU.add))
            dve.wait_ge(gathered, 16 * NT)
            do(v.tensor_tensor(kh(a4[:, 0, :]), rows[:, :, SRC_F:SEG_F], ad[:, :, :], ALU.add))
            do(v.tensor_tensor(kh(den[:, :]), rows[:, :, SRC_F:SEG_F], over_h(none0[:, :]), ALU.add))
            do(v.tensor_tensor(kh(den[:, :]), kh(den[:, :]), a_self, ALU.max))
            do(v.tensor_tensor(kh(sc[:, :]), over_h(none1[:, :]), a_last, ALU.add))
            do(v.tensor_tensor(den[:, :], den[:, :], sc[:, :], ALU.max))
            do(v.tensor_tensor(kh(a4[:, 3, :]), kh(den[:, :]), ad[:, :, :], ALU.add))
            do(v.scalar_tensor_tensor(a4[:, :, :], a4[:, :, :], 0.2, a4[:, :, :], ALU.mult, ALU.max))
            do(v.tensor_tensor(wts[:, :, :], a4[:, 0:3, :], a4[:, 3:4, :].to_broadcast([P, 3, K4]), ALU.subtract))
            v.tensor_scalar(wts[:, :, :], wts[:, :, :], 0.0, None, ALU.min).then_inc(weights_ready, 1)
            dve.wait_ge(exps, 1)
            do(v.tensor_tensor(kh(wts[:, 0, :]), kh(wts[:, 0, :]), over_h(has0[:, :]), ALU.mult))
            do(v.tensor_tensor(kh(wts[:, 2, :]), kh(wts[:, 2, :]), over_h(count1[:, :]), ALU.mult))
            do(v.tensor_tensor(kh(den[:, :]), rows[:, :, GH:SRC_F], kh(wts[:, 0, :]), ALU.mult))
            do(v.tensor_tensor(den[:, :], den[:, :], wts[:, 1, :], ALU.add))
            do(v.tensor_tensor(den[:, :], den[:, :], wts[:, 2, :], ALU.add))
            do(v.tensor_scalar(den[:, :], den[:, :], 1e-16, None, ALU.add))
            do(v.reciprocal(den[:, :], den[:, :]))
            he = lambda t: t.rearrange("p k (h e) -> p k h e", h=HEADS)
            do(v.tensor_tensor(khe(agg[:, :]), he(rows[:, :, 0:GH]), over_e(wts[:, 0, :]), ALU.mult))
            do(v.tensor_tensor(khe(tmp[:, :]), he(node[:, :, 0:GH]), over_e(wts[:, 1, :]), ALU.mult))
            do(v.tensor_tensor(agg[:, :], agg[:, :], tmp[:, :], ALU.add))
            last_he = last_row[:, 0:GH].rearrange("p (h e) -> p h e", h=HEADS)
            for h in range(HEADS):
                do(v.tensor_tensor(khe(tmp[:, :])[:, :, h, :], last_he[:, h:h + 1, :].to_broadcast([P, NT, EXPERTS]), over_e(wts[:, 2, :])[:, :, h, :], ALU.mult))
            do(v.tensor_tensor(agg[:, :], agg[:, :], tmp[:, :], ALU.add))
            do(v.tensor_tensor(khe(agg[:, :]), khe(agg[:, :]), over_e(den[:, :]), ALU.mult))
            kf = lambda t: t.rearrange("p (k f) -> p k f", f=GH)
            f_over_k = lambda t: t[:, None, :].to_broadcast([P, NT, GH])
            over_f = lambda t: t[:, :, None].to_broadcast([P, NT, GH])
            do(v.tensor_tensor(kf(agg[:, :]), kf(agg[:, :]), f_over_k(bias[:, :]), ALU.add))
            do(v.tensor_reduce(mean[:, :], kf(agg[:, :]), AX, ALU.add))
            do(v.tensor_scalar(mean[:, :], mean[:, :], 1.0 / GH, None, ALU.mult))
            do(v.tensor_tensor(kf(agg[:, :]), kf(agg[:, :]), over_f(mean[:, :]), ALU.subtract))
            do(v.tensor_tensor(tmp[:, :], agg[:, :], agg[:, :], ALU.mult))
            v.tensor_reduce(var[:, :], kf(tmp[:, :]), AX, ALU.add).then_inc(var_made, 1)
            dve.wait_ge(exps, 3)
            do(v.tensor_tensor(kf(agg[:, :]), kf(agg[:, :]), over_f(var[:, :]), ALU.mult))
            do(v.tensor_tensor(kf(agg[:, :]), kf(agg[:, :]), f_over_k(gamma[:, :]), ALU.mult))
            do(v.tensor_tensor(kf(agg[:, :]), kf(agg[:, :]), f_over_k(beta[:, :]), ALU.add))
            do(v.tensor_reduce(kh(sc[:, :]), khe(agg[:, :]).rearrange("p k h e -> p k e h"), AX, ALU.add))
            do(v.tensor_scalar(sc[:, :], sc[:, :], 1.0 / HEADS, None, ALU.mult))
            mine = kh(sc[:, :])[:, :, :, None].to_broadcast([P, NT, EXPERTS, EXPERTS])
            theirs = kh(sc[:, :])[:, :, None, :].to_broadcast([P, NT, EXPERTS, EXPERTS])
            do(v.tensor_tensor(khe(beats[:, :]), theirs, mine, ALU.is_gt))
            do(v.tensor_tensor(khe(even[:, :]), theirs, mine, ALU.is_equal))
            dve.wait_ge(tie_made, 3)
            do(v.tensor_tensor(kf(even[:, :]), kf(even[:, :]), f_over_k(ties[:, :]), ALU.mult))
            do(v.tensor_tensor(beats[:, :], beats[:, :], even[:, :], ALU.add))
            do(v.tensor_reduce(kh(rank[:, :]), khe(beats[:, :]), AX, ALU.add))
            do(v.tensor_scalar(rank[:, :], rank[:, :], 2.0, None, ALU.is_lt))
            do(v.tensor_reduce(top[:, :], kh(sc[:, :]), AX, ALU.max))
            v.tensor_tensor(kh(sc[:, :]), kh(sc[:, :]), over_h(top[:, :]), ALU.subtract).then_inc(var_made, 1)
            dve.wait_ge(exps, 4)
            do(v.tensor_tensor(sc[:, :], sc[:, :], rank[:, :], ALU.mult))
            do(v.tensor_reduce(top[:, :], kh(sc[:, :]), AX, ALU.add))
            do(v.reciprocal(top[:, :], top[:, :]))
            v.tensor_tensor(kh(sc[:, :]), kh(sc[:, :]), over_h(top[:, :]), ALU.mult).then_inc(gates_made, 1)
            for k in range(NT // 4):
                dve.wait_ge(gates_t, 4 * k + 4)
                if k >= 4:
                    dve.wait_ge(stored[k % 4], k // 4 * 16)
                v.tensor_copy(gt[k % 4][:, :], psc[k % 4][0:EXPERTS, :]).then_inc(gates_out, 1)

        @block.scalar
        def _(act):
            f = nc.scalar.activation
            for n in rest:
                early.gelus(act, n, 0)
                early.gelus(act, n, 1)
            act.wait_ge(tie_made, 1)
            act.wait_ge(weights_ready, 1)
            f(wts[:, :, :], wts[:, :, :], ACT.Exp).then_inc(exps, 1)
            act.wait_ge(var_made, 1)
            f(var[:, :], var[:, :], ACT.Ln, scale=1.0 / GH, bias=eps[:, 0:1]).then_inc(exps, 1)
            act.wait_ge(exps, 2)
            f(var[:, :], var[:, :], ACT.Exp, scale=-0.5).then_inc(exps, 1)
            act.wait_ge(var_made, 2)
            f(sc[:, :], sc[:, :], ACT.Exp).then_inc(exps, 1)
            for e in range(EXPERTS):
                act.wait_ge(early.y_stored[e], EARLY * 16)

        @block.tensor
        def _(pe):
            for n in rest:
                early.products(pe, n, 0)
                early.products(pe, n, 1)
            pe.wait_ge(early.gelu, EARLY * UNITS)
            pe.wait_ge(gates_made, 1)
            for k in range(NT):
                if k % 4 == 0 and k >= 16:
                    pe.wait_ge(gates_out, k // 4 - 3)
                nc.tensor.transpose(psc[k // 4 % 4][0:EXPERTS, (k % 4) * P:(k % 4 + 1) * P], sc[:, k * EXPERTS:(k + 1) * EXPERTS], ident[:, :]).then_inc(gates_t, 1)

LATE = CHUNKS - EARLY


def experts(nc, tables, gates_dram, y_dram, w, weights, out_dram):
    assert LATE == EARLY
    with ExitStack() as ctx:
        sb = lambda name, shape, dt=F32: ctx.enter_context(nc.sbuf_tensor(name, shape, dt))
        sem = lambda name: ctx.enter_context(nc.semaphore(name))
        pair = lambda name, shape: [sb(f"{name}{k}", shape) for k in range(2)]
        w1, w2, b1, _, _ = weights
        b2 = sb("b2", [EXPERTS, CT * P])
        xn, res, gate, out = pair("f_xn", [P, CT, T]), pair("f_x2", [P, CT, T]), pair("f_gates", [EXPERTS, T]), pair("f_out", [P, CT, T])
        spread = pair("f_gates_spread", [P, EXPERTS, T])
        y, y_spread, y_sum = pair("y_in", [P, EXPERTS, CT, T]), pair("y_gates_spread", [P, EXPERTS, T]), pair("y_sum", [P, CT, T])
        hid = [sb(f"hid{k}", [P, T]) for k in range(RING)]
        ps_up = [ctx.enter_context(nc.psum_tensor(f"ps_up{k}", [P, T], F32)) for k in range(RING)]
        ps_down = [ctx.enter_context(nc.psum_tensor(f"ps_down{k}", [P, T], F32)) for k in range(2 * CT)]
        b2_loaded = sem("f_b2_loaded")
        loaded, stored = [sem(f"f_loaded{k}") for k in range(2)], [sem(f"f_stored{k}") for k in range(2)]
        y_loaded, y_stored = [sem(f"y_loaded{k}") for k in range(2)], [sem(f"y_stored{k}") for k in range(2)]
        up, gelu, gated, down, added = sem("up_full"), sem("gelu_made"), sem("f_gated"), sem("down_done"), sem("f_added")
        y_gated, y_added = sem("y_gated"), sem("y_added")

        def bodies(eng, run):
            run(0, 0, 0)
            run(1, 0, 1)
            with eng.Fori(1, LATE // 2) as j:
                run(j * 2, j, 0)
                run(j * 2 + 1, j, 1)

        chunk_of = lambda t, i: t[bass.ds(i, 1)].rearrange("o p (c t) -> (o p) c t", c=CT)
        gates_of = lambda i: gates_dram[:, bass.ds(i * T, T)]
        sp_passed, pool_passed = sem("f_sp_passed"), sem("f_pool_passed")
        with nc.Block() as block:
            @block.sync
            def _(sp):
                sp.dma_start(b2[:, :], w["b2"]).then_inc(b2_loaded, 16)

                def run(i, j, par):
                    if not isinstance(i, int):
                        wait_alone(sp, added, i * 2 - 2, sp_passed)
                        wait_alone(sp, gelu, i * UNITS - UNITS, sp_passed)
                        wait_alone(sp, gated, i * UNITS - UNITS, sp_passed)
                    sp.dma_start(xn[par][:, :, :], chunk_of(tables["xn2"], i + EARLY)).then_inc(loaded[par], 16)
                    sp.dma_start(gate[par][:, :], gates_of(i + EARLY)).then_inc(loaded[par], 16)
                    sp.dma_start(spread[par][:, :, :], gates_of(i + EARLY)[None, :, :].to_broadcast([P, EXPERTS, T])).then_inc(loaded[par], 16)
                    sp.dma_start(res[par][:, :, :], chunk_of(tables["x2"], i + EARLY)).then_inc(loaded[par], 16)
                    if not isinstance(i, int):
                        wait_alone(sp, y_stored[par], j * 16, sp_passed)
                        wait_alone(sp, y_added, (i - 1) * EXPERTS, sp_passed)
                    sp.dma_start(y[par][:, :, :, :], y_dram[bass.ds(i, 1)].rearrange("o p (e c t) -> (o p) e c t", e=EXPERTS, c=CT)).then_inc(y_loaded[par], 16)
                    sp.dma_start(y_spread[par][:, :, :], gates_of(i)[None, :, :].to_broadcast([P, EXPERTS, T])).then_inc(y_loaded[par], 16)
                    sp.dma_start(y_sum[par][:, :, :], chunk_of(tables["x2"], i)).then_inc(y_loaded[par], 16)
                bodies(sp, run)

            @block.gpsimd
            def _(pool):
                def run(i, j, par):
                    wait_alone(pool, y_added, i * EXPERTS + EXPERTS, pool_passed)
                    pool.dma_start(chunk_of(out_dram, i), y_sum[par][:, :, :]).then_inc(y_stored[par], 16)
                    wait_alone(pool, added, i * 2 + 2, pool_passed)
                    pool.dma_start(chunk_of(out_dram, i + EARLY), out[par][:, :, :]).then_inc(stored[par], 16)
                bodies(pool, run)
                for k in range(2):
                    pool.wait_ge(stored[k], LATE // 2 * 16)
                    pool.wait_ge(y_stored[k], LATE // 2 * 16)

            @block.tensor
            def _(pe):
                mm = nc.tensor.matmul
                pe.wait_ge(b2_loaded, 16)

                def run(i, j, par):
                    pe.wait_ge(loaded[par], j * 64 + 64)
                    later = not isinstance(i, int) or i > 0
                    sums = ps_down[CT * par:CT * (par + 1)]
                    for k in range(UNITS + LAG):
                        if k < UNITS:
                            e, ft = divmod(k, FT)
                            if k >= RING or later:
                                pe.wait_ge(gelu, i * UNITS + k - RING + 1)
                            for c in range(CT):
                                last = mm(ps_up[k % RING][:, :], w1[:, e, c, ft * P:(ft + 1) * P], xn[par][:, c, :], start=(c == 0), stop=(c == CT - 1))
                            last.then_inc(up, 1)
                        if k == LAG:
                            if not isinstance(i, int):
                                pe.wait_ge(added, i * 2 - 2)
                            for c in range(CT):
                                mm(sums[c][:, :], b2[:, c * P:(c + 1) * P], gate[par][:, :], start=True, stop=False)
                        if k >= LAG:
                            q = k - LAG
                            pe.wait_ge(gated, i * UNITS + q + 1)
                            for c in range(CT):
                                last = mm(sums[c][:, :], w2[:, q, c * P:(c + 1) * P], hid[q % RING][:, :], start=False, stop=(q == UNITS - 1))
                            last.then_inc(down, 1)
                bodies(pe, run)

            @block.scalar
            def _(act):
                def run(i, j, par):
                    later = not isinstance(i, int) or i > 0
                    for k in range(UNITS):
                        act.wait_ge(up, i * UNITS + k + 1)
                        if k >= RING or later:
                            act.wait_ge(down, i * UNITS + k - RING + 1)
                        nc.scalar.activation(hid[k % RING][:, :], ps_up[k % RING][:, :], ACT.Gelu, bias=b1[:, k:k + 1]).then_inc(gelu, 1)
                bodies(act, run)

            @block.vector
            def _(dve):
                v = nc.vector

                def merge(i, j, par, k):
                    e = k // 2
                    if k == 0:
                        dve.wait_ge(y_loaded[par], j * 48 + 48)
                    if k % 2 == 0:
                        v.tensor_tensor(y[par][:, e, :, :], y[par][:, e, :, :], y_spread[par][:, e:e + 1, :].to_broadcast([P, CT, T]), ALU.mult).then_inc(y_gated, 1)
                    else:
                        dve.wait_ge(y_gated, i * EXPERTS + e + 1)
                        if e:
                            dve.wait_ge(y_added, i * EXPERTS + e)
                        v.tensor_tensor(y_sum[par][:, :, :], y_sum[par][:, :, :], y[par][:, e, :, :], ALU.add).then_inc(y_added, 1)

                def run(i, j, par):
                    dve.wait_ge(loaded[par], j * 64 + 64)
                    for k in range(UNITS):
                        dve.wait_ge(gelu, i * UNITS + k + 1)
                        v.tensor_tensor(hid[k % RING][:, :], hid[k % RING][:, :], spread[par][:, k // FT, :], ALU.mult).then_inc(gated, 1)
                        if k % 2 == 1:
                            merge(i, j, par, k // 2)
                    dve.wait_ge(down, i * UNITS + UNITS)
                    if not isinstance(i, int):
                        dve.wait_ge(stored[par], j * 16)
                    for c in range(CT):
                        v.tensor_tensor(out[par][:, c, :], ps_down[CT * par + c][:, :], res[par][:, c, :], ALU.add).then_inc(added, 1)
                bodies(dve, run)


INPUTS = ["x", "in", "x_proj", "dt", "out_proj", "conv", "conv_b", "dt_b", "skip", "a_log", "gat", "att", "b_gat",
          "gamma", "beta", "w1", "b1", "w2", "b2", "b2_lanes", "edge_src", "edge_dst"]


def metaformer_block(nc, a, out):
    dram = lambda name, shape, dt=F32: nc.dram_tensor(name, shape, dt, kind="Internal").ap()
    keys, ends_at = dram("keys_sorted", [EDGES + 2, 1], I32), dram("ends_at", [EDGES, 1], I32)
    ends = dram("ends", [GROUPS + OFF, 1], I32)
    src, dst = dram("edge_src_sorted", [EDGES, 1], I32), dram("edge_dst_sorted", [EDGES, 1], I32)
    seg = dram("segments", [EDGES, SEG_F], I32)
    gates = dram("gates", [EXPERTS, NODES])
    y = dram("early_expert_outputs", [EARLY, P, EXPERTS * CT * T])
    tables = {"x2": dram("x_after_mamba", [CHUNKS, P, CT * T]), "xn2": dram("x_normed", [CHUNKS, P, CT * T]),
              "src": dram("node_src", [NODES, SRC_F]), "dst": dram("node_dst_scores", [NODES, DST_F])}
    w = {"in": a["in"], "x": a["x_proj"], "dt": a["dt"], "out": a["out_proj"], "conv": a["conv"], "conv_b": a["conv_b"],
         "dt_b": a["dt_b"], "skip": a["skip"], "a_log": a["a_log"], "gat": a["gat"], "att": a["att"]}
    with nc.sbuf_tensor("chunk_counts", [P, 2], I32) as counts:
        sort_edges(nc, a["edge_src"], a["edge_dst"], keys, ends_at, ends, src, dst, counts)
        mamba(nc, a["x"], w, tables, ends_at, ends, counts)
        with (nc.sbuf_tensor("w1", [P, EXPERTS, CT, FF], F32) as w1, nc.sbuf_tensor("w2", [P, UNITS, CT * P], F32) as w2,
              nc.sbuf_tensor("b1", [P, UNITS], F32) as b1, nc.sbuf_tensor("b2_lanes", [P, EXPERTS * CT], F32) as b2,
              nc.semaphore("expert_weights_loaded") as w_loaded):
            weights = (w1, w2, b1, b2, w_loaded)
            attention(nc, keys, src, dst, ends, tables, a, seg, gates, counts, weights, y)
            experts(nc, tables, gates, y, a, weights, out)


def kernel(x, L0_conv_in_proj_w, L0_conv_conv_w, L0_conv_conv_b, L0_conv_x_proj_w, L0_conv_dt_proj_w, L0_conv_dt_proj_b,
           L0_conv_A_log, L0_conv_D, L0_conv_out_proj_w, L0_ffn_W_gat, L0_ffn_att_src, L0_ffn_att_dst, L0_ffn_b_gat,
           L0_ffn_ln_gamma, L0_ffn_ln_beta, L0_ffn_W1, L0_ffn_b1, L0_ffn_W2, L0_ffn_b2, L0_ffn_edge_index):
    import concourse.bacc as bacc
    from concourse.bass_utils import run_bass_kernel_spmd

    lay = np.ascontiguousarray
    arr = np.asarray
    column = lambda v: lay(arr(v).reshape(-1, P).T)
    xs = lay(arr(x).reshape(4, CT, P, PER_BATCH, T).transpose(0, 3, 2, 1, 4)).reshape(CHUNKS, P, CT * T)
    xp, dtw = arr(L0_conv_x_proj_w).T, arr(L0_conv_dt_proj_w).T
    x_proj = np.zeros((xp.shape[0], 64), xp.dtype)
    x_proj[:, 0:16], x_proj[:, 32:64] = xp[:, 0:16], xp[:, 16:48]
    dt = np.zeros((32, dtw.shape[1]), dtw.dtype)
    dt[0:16] = dtw
    edges = arr(L0_ffn_edge_index)
    inputs = {
        "x": xs, "in": lay(arr(L0_conv_in_proj_w).T), "x_proj": x_proj, "dt": dt, "out_proj": lay(arr(L0_conv_out_proj_w).T),
        "conv": lay(arr(L0_conv_conv_w).reshape(-1, TAPS)), "conv_b": column(L0_conv_conv_b), "dt_b": column(L0_conv_dt_proj_b),
        "skip": column(L0_conv_D), "a_log": lay(arr(L0_conv_A_log)), "gat": lay(arr(L0_ffn_W_gat)),
        "att": lay(np.stack([arr(L0_ffn_att_src).reshape(-1), arr(L0_ffn_att_dst).reshape(-1)])),
        "b_gat": lay(arr(L0_ffn_b_gat).reshape(1, -1)), "gamma": lay(arr(L0_ffn_ln_gamma).reshape(1, -1)),
        "beta": lay(arr(L0_ffn_ln_beta).reshape(1, -1)), "w1": lay(arr(L0_ffn_W1)), "b1": column(L0_ffn_b1),
        "w2": lay(arr(L0_ffn_W2)), "b2": lay(arr(L0_ffn_b2)), "b2_lanes": column(L0_ffn_b2),
        "edge_src": lay(edges[0].reshape(P, EC)), "edge_dst": lay(edges[1].reshape(P, EC)),
    }
    nc = bacc.Bacc("TRN2", target_bir_lowering=False, num_devices=1)
    arrays, args = {}, {}
    for name in INPUTS:
        arrays[f"in_{name}"] = inputs[name]
        args[name] = nc.dram_tensor(f"in_{name}", inputs[name].shape, mybir.dt.from_np(inputs[name].dtype), kind="ExternalInput").ap()
    out = nc.dram_tensor("out", [CHUNKS, P, CT * T], F32, kind="ExternalOutput").ap()
    metaformer_block(nc, args, out)
    got = run_bass_kernel_spmd(nc, [arrays], core_ids=[0]).results[0]["out"]
    return lay(got.reshape(4, PER_BATCH, P, CT, T).transpose(0, 3, 2, 1, 4)).reshape(4, CT * P, 64, 64)
```

```python
import numpy as np
import concourse.bass as bass
from concourse import mybir
from contextlib import ExitStack

ALU = mybir.AluOpType
ACT = mybir.ActivationFunctionType
F32 = mybir.dt.float32
BF16 = mybir.dt.bfloat16
I32 = mybir.dt.int32
U32 = mybir.dt.uint32

P = 128
NODES = 16384
EDGES = 1048576
EC = EDGES // P
LB = EC.bit_length() - 1
PB = 7
SRC_BITS = 14
SRC_MASK = NODES - 1
OFF = 1024
GROUPS = 2 * NODES
CHUNK = 8192
CW = CHUNK // P
ZERO_W = 8192
KEPT_LEVEL = 7


def float_of(bits):
    return float(np.array([bits], np.uint32).view(np.float32)[0])


class Steps:

    def __init__(self, engine, sem, base=0):
        self.engine, self.sem, self.base, self.n = engine, sem, base, 0

    def __call__(self, instruction):
        instruction.then_inc(self.sem, 1)
        self.n += 1

    def settle(self, back=0):
        self.engine.wait_ge(self.sem, self.base + (self.n - back))


def wait_alone(engine, sem, value, passed):
    engine.wait_ge(sem, value)
    if not isinstance(value, int):
        engine.sem_inc(passed, 1)


def sort_edges(nc, edge_src, edge_dst, keys_dram, ends_at_dram, ends_dram, src_dram, dst_dram, placed_dram, counts):
    with ExitStack() as ctx:
        sb = lambda name, shape, dt: ctx.enter_context(nc.sbuf_tensor(name, shape, dt))
        sem = lambda name: ctx.enter_context(nc.semaphore(name))
        x = sb("sort_x", [P, EC], F32)
        y = sb("sort_y", [P, EC], F32)
        z = sb("sort_z", [P, EC], F32)
        ident = sb("sort_ident", [P, P], F32)
        lane = sb("lane", [P, 1], I32)
        lane_bit = sb("lane_bit", [P, PB], I32)
        sign = sb("sign", [P, PB + 1], F32)
        ones = sb("sort_ones", [P, P], F32)
        below = sb("below", [P, 2], F32)
        sentinel = sb("sentinel", [1, 1], I32)
        crowded = sb("crowded_runs", [P, 1], I32)
        zeros = sb("zero_rows", [P, ZERO_W], I32)
        ps = [ctx.enter_context(nc.psum_tensor(f"sort_ps{k}", [P, 1024], F32)) for k in range(4)]
        loaded, const, lanes, keys_made = sem("edges_loaded"), sem("const_ready"), sem("lane_iota"), sem("keys_made")
        dve_steps, act_steps = sem("dve_steps"), sem("act_steps")
        run_sorted, transposed = sem("run_sorted"), sem("transposed")
        out = sem("evacuated_by_scalar"), sem("evacuated_by_vector")
        placed_zeroed = sem("placed_zeroed")
        full_runs, flagged = sem("full_runs_counted"), sem("crowded_made")
        stored, reloaded, counted = sem("keys_stored"), sem("next_loaded"), sem("lane_counts_summed")
        counted_dve, idx_made, idx_stored, zeroed = sem("lane_counts"), sem("ends_at_made"), sem("ends_at_stored"), sem("ends_zeroed")
        src_made, dst_made, src_stored, dst_stored = sem("src_made"), sem("dst_made"), sem("src_stored"), sem("dst_stored")
        xi, yi, zi = (t[:, :].bitcast(I32) for t in (x, y, z))
        GROUP = 8

        class Network:

            def __init__(self, lane_bits, first_level, crossed):
                self.lane_bits, self.first_level, self.width = lane_bits, first_level, 1 << lane_bits
                self.groups = self.width // P // GROUP
                self.upper = range(lane_bits + 1, lane_bits + PB + 1)
                self.sides = []
                at = crossed + sum(range(first_level, lane_bits + 1)) + 1
                for level in self.upper:
                    for stages in (level - lane_bits, lane_bits):
                        self.sides.append(((y, x) if at % 2 == 0 else (x, y)))
                        at += 1 + stages
                self.ends_in_x = at % 2 == 1
                self.sorted, self.spare = (t[:, 0:self.width] for t in ((x, y) if self.ends_in_x else (y, x)))

            def halves(self, n, k):
                src, dst = ps[(n * self.groups + k) % 4][:, :], self.sides[n][1][:, k * GROUP * P:(k + 1) * GROUP * P]
                if n % 2 == 0:
                    view = lambda w, d: w.rearrange("p (h d l) -> p h d l", d=2, l=1 << (n // 2))[:, :, d]
                    return [(view(dst, 0), view(src, 0), 1.0), (view(dst, 1), view(src, 1), -1.0)]
                half = GROUP * P // 2
                return [(dst[:, c:c + half], src[:, c:c + half], sign[:, n // 2 + 1:n // 2 + 2]) for c in (0, half)]

        common = KEPT_LEVEL * (KEPT_LEVEL + 1) // 2
        whole, half_net = Network(LB, KEPT_LEVEL + 1, common), Network(LB - 1, KEPT_LEVEL, common)

        def either(eng, run):
            eng.wait_ge(flagged, 1)
            n = eng.value_load(crowded[0:1, 0:1], min_val=0, max_val=EDGES)
            with eng.If(n > 0):
                run(whole)
            with eng.Else():
                run(half_net)

        with nc.Block() as block:
            @block.sync
            def _(sp):
                sp.dma_start(xi, edge_src).then_inc(loaded, 16)
                sp.dma_start(yi, edge_dst).then_inc(loaded, 16)
                sp.wait_ge(const, 4)
                sp.dma_start(keys_dram[0:1, :], sentinel[:, :]).then_inc(zeroed, 16)
                sp.dma_start(ends_dram.rearrange("(p c) o -> p (c o)", p=P), zeros[:, 0:(GROUPS + OFF) // P]).then_inc(zeroed, 16)
                per_lane = placed_dram.rearrange("(p c) f -> p (c f)", p=P)
                for c in range(0, per_lane.shape[1], ZERO_W):
                    sp.dma_start(per_lane[:, c:c + ZERO_W], zeros[:, :]).then_inc(placed_zeroed, 16)

                def run(net):
                    edges, w = net.width * P, net.width
                    sorted_keys, spare = net.sorted.bitcast(I32), net.spare.bitcast(I32)
                    rows_of = lambda t, first=0: t[first:first + edges, :].rearrange("(p c) o -> p (c o)", p=P)
                    sp.dma_start(keys_dram[edges + 1:edges + 2, :], sentinel[:, :]).then_inc(zeroed, 16)
                    sp.wait_ge(keys_made, 1)
                    sp.dma_start(rows_of(keys_dram, 1), sorted_keys).then_inc(stored, 16)
                    sp.wait_ge(stored, 16)
                    sp.wait_ge(zeroed, 48)
                    sp.dma_start(spare, rows_of(keys_dram, 2)).then_inc(reloaded, 16)
                    sp.wait_ge(src_made, 1)
                    sp.dma_start(rows_of(src_dram), zi[:, 0:w]).then_inc(src_stored, 16)
                    sp.wait_ge(idx_made, 1)
                    sp.dma_start(rows_of(ends_at_dram), zi[:, 0:w]).then_inc(idx_stored, 16)
                    sp.wait_ge(dst_made, 1)
                    sp.dma_start(rows_of(dst_dram), spare).then_inc(dst_stored, 16)
                    sp.wait_ge(src_stored, 16)
                    sp.wait_ge(dst_stored, 16)
                    sp.wait_ge(idx_stored, 16)
                    sp.wait_ge(placed_zeroed, placed_dram.shape[0] // P * placed_dram.shape[1] // ZERO_W * 16)
                either(sp, run)

            @block.gpsimd
            def _(pool):
                nc.gpsimd.iota(lane[:, :], pattern=[[0, 1]], base=0, channel_multiplier=1).then_inc(lanes, 1)
                nc.gpsimd.memset(ones[:, :], 1.0).then_inc(const, 1)
                nc.gpsimd.memset(sentinel[:, :], 0).then_inc(const, 1)
                nc.gpsimd.memset(zeros[:, :], 0).then_inc(const, 1)
                pool.wait_ge(const, 1)
                nc.gpsimd.affine_select(out=ident[:, :], in_=ones[:, :], compare_op=ALU.is_equal, fill=0.0, base=0,
                                        pattern=[[-1, P]], channel_multiplier=1).then_inc(const, 1)

            @block.vector
            def _(dve):
                step = Steps(dve, dve_steps)
                v = nc.vector
                dve.wait_ge(lanes, 1)
                for b in range(PB):
                    step(v.tensor_scalar(lane_bit[:, b:b + 1], lane[:, :], b, 1, ALU.logical_shift_right, ALU.bitwise_and))
                step.settle()
                step(v.tensor_scalar(sign[:, 0:PB], lane_bit[:, :], -2, 1, ALU.mult, ALU.add))
                step(v.memset(sign[:, PB:PB + 1], 1.0))
                dve.wait_ge(loaded, 32)
                def one(out, in_, a, b, op0, op1):
                    step(v.tensor_scalar(out, in_, a, b, op0, op1)); step.settle()
                def two(out, a, b, op):
                    step(v.tensor_tensor(out, a, b, op)); step.settle()
                one(zi, xi, 0, NODES, ALU.is_lt, ALU.mult)
                two(xi, xi, zi, ALU.add)
                one(xi, xi, 0, NODES - 1, ALU.max, ALU.min)
                one(yi, yi, -1, NODES, ALU.max, ALU.min)
                one(yi, yi, 0x1FFFF, None, ALU.bitwise_and, ALU.bypass)
                one(zi, xi, NODES - 1, NODES, ALU.is_equal, ALU.mult)
                two(zi, zi, yi, ALU.add)
                one(yi, yi, NODES, 4 * NODES, ALU.is_ge, ALU.mult)
                two(yi, yi, zi, ALU.add)
                one(yi, yi, GROUPS, OFF, ALU.min, ALU.add)
                one(yi, yi, SRC_BITS, None, ALU.logical_shift_left, ALU.bypass)
                two(yi, xi, yi, ALU.bitwise_or)

                def stage(width, cur, nxt, bit, direction):
                    lo = 1 << bit
                    if direction is None:
                        a, o = (t[:, 0:width].rearrange("p (m t l) -> p m t l", t=2, l=lo) for t in (cur, nxt))
                        step.settle()
                        step(v.tensor_tensor(o[:, :, 0], a[:, :, 0], a[:, :, 1], ALU.min))
                        step(v.tensor_tensor(o[:, :, 1], a[:, :, 0], a[:, :, 1], ALU.max))
                    else:
                        a, o = (t[:, 0:width].rearrange("p (h d m t l) -> p h d m t l", d=2, m=1 << (direction - 1 - bit), t=2, l=lo)
                                for t in (cur, nxt))
                        for d in range(2):
                            step.settle(0 if bit == direction - 1 and d == 0 else 2)
                            low, high = (ALU.min, ALU.max) if d == 0 else (ALU.max, ALU.min)
                            step(v.tensor_tensor(o[:, :, d, :, 0], a[:, :, d, :, 0], a[:, :, d, :, 1], low))
                            step(v.tensor_tensor(o[:, :, d, :, 1], a[:, :, d, :, 0], a[:, :, d, :, 1], high))
                    return nxt, cur

                cur, nxt = y, x
                for level in range(1, KEPT_LEVEL + 1):
                    for bit in reversed(range(level)):
                        cur, nxt = stage(EC, cur, nxt, bit, level)
                step.settle()
                run = 1 << KEPT_LEVEL
                pairs = cur[:, :].rearrange("p (h d l) -> p h d l", d=2, l=run)
                for d, middle in enumerate((run // 2, run // 2 - 1)):
                    step(v.tensor_scalar(z[:, 0:EC // run // 2], pairs[:, :, d, middle], float_of((GROUPS + OFF) << SRC_BITS), 0.0,
                                         ALU.is_lt, ALU.add, accum_out=below[:, d:d + 1]))
                    step.settle()
                step(v.tensor_tensor(below[:, 0:1], below[:, 0:1], below[:, 1:2], ALU.add))
                step.settle()
                dve.sem_inc(counted_dve, 1)
                dve.wait_ge(full_runs, 1)
                v.tensor_copy(crowded[:, :], ps[0][:, 0:1]).then_inc(flagged, 1)
                before, start = step.n, (cur, nxt)

                def rest(net):
                    nonlocal step
                    step = Steps(dve, dve_steps)
                    step.n = before
                    w = net.width
                    cur, nxt = start
                    first = net.first_level
                    if first == KEPT_LEVEL:
                        a = cur[:, :].rearrange("p (h d l) -> p h d l", d=2, l=run)
                        a = a[:, :, 0, 0:run // 2], a[:, :, 1, run // 2:run]
                        o = nxt[:, 0:w].rearrange("p (h t l) -> p h t l", t=2, l=run // 2)
                        for d in range(2):
                            low, high = (ALU.min, ALU.max) if d == 0 else (ALU.max, ALU.min)
                            step(v.tensor_tensor(o[:, d::2, 0], a[0][:, d::2], a[1][:, d::2], low))
                            step(v.tensor_tensor(o[:, d::2, 1], a[0][:, d::2], a[1][:, d::2], high))
                        cur, nxt = nxt, cur
                        step.settle()
                        for bit in reversed(range(KEPT_LEVEL - 1)):
                            cur, nxt = stage(w, cur, nxt, bit, KEPT_LEVEL)
                        first += 1
                    for level in range(first, net.lane_bits):
                        for bit in reversed(range(level)):
                            cur, nxt = stage(w, cur, nxt, bit, level)
                    step.settle()
                    step(v.tensor_scalar(nxt[:, 0:w], cur[:, 0:w], sign[:, 0:1], None, ALU.mult))
                    cur, nxt = nxt, cur
                    for bit in reversed(range(net.lane_bits)):
                        cur, nxt = stage(w, cur, nxt, bit, None)
                    for n in range(len(net.sides)):
                        step.settle()
                        assert cur is net.sides[n][0]
                        dve.sem_inc(run_sorted, 1)
                        for k in range(1, net.groups, 2):
                            dve.wait_ge(transposed, n * net.groups + k + 1)
                            for dst, src, factor in net.halves(n, k):
                                v.tensor_scalar(dst, src, factor, None, ALU.mult).then_inc(out[1], 1)
                        dve.wait_ge(out[0], (n + 1) * net.groups)
                        dve.wait_ge(out[1], (n + 1) * net.groups)
                        cur, nxt = nxt, cur
                        level = net.upper[n // 2]
                        bits, direction = (level - net.lane_bits, level - net.lane_bits) if n % 2 == 0 else (net.lane_bits, None)
                        for bit in reversed(range(bits)):
                            cur, nxt = stage(w, cur, nxt, bit, direction if level < net.lane_bits + PB else None)
                    step.settle()
                    assert (cur is x) == net.ends_in_x
                    dve.sem_inc(keys_made, 1)
                    xw, yw, zw = net.sorted.bitcast(I32), net.spare.bitcast(I32), zi[:, 0:w]
                    for n, top in enumerate((NODES, GROUPS)):
                        step(v.tensor_scalar(z[:, 0:w], net.sorted, float_of((top + OFF) << SRC_BITS), 0.0, ALU.is_lt, ALU.add,
                                             accum_out=below[:, n:n + 1]))
                        step.settle()
                    dve.sem_inc(counted_dve, 1)
                    dve.wait_ge(counted, 1)
                    one(counts[:, :], ps[0][:, 0:2], float(CHUNK - 1), None, ALU.add, ALU.bypass)
                    one(counts[:, :], counts[:, :], CHUNK.bit_length() - 1, None, ALU.logical_shift_right, ALU.bypass)
                    one(counts[:, 0:1], counts[:, 0:1], 7, None, ALU.max, ALU.bypass)
                    one(counts[:, 1:2], counts[:, 1:2], float(NODES // 512), None, ALU.subtract, ALU.bypass)
                    one(counts[:, 1:2], counts[:, 1:2], 1, None, ALU.max, ALU.bypass)
                    dve.wait_ge(reloaded, 16)
                    one(yw, yw, SRC_BITS, None, ALU.logical_shift_right, ALU.bypass)
                    v.tensor_scalar(zw, xw, SRC_MASK, None, ALU.bitwise_and).then_inc(src_made, 1)
                    dve.wait_ge(stored, 16)
                    dve.wait_ge(src_made, 1)
                    one(xw, xw, SRC_BITS, None, ALU.logical_shift_right, ALU.bypass)
                    two(yw, yw, xw, ALU.is_equal)
                    dve.wait_ge(src_stored, 16)
                    v.scalar_tensor_tensor(zw, yw, float(4 * GROUPS), xw, ALU.mult, ALU.add).then_inc(idx_made, 1)
                    dve.wait_ge(idx_made, 1)
                    v.tensor_scalar(yw, xw, OFF, NODES - 1, ALU.subtract, ALU.min).then_inc(dst_made, 1)
                either(dve, rest)

            @block.tensor
            def _(pe):
                pe.wait_ge(const, 4)
                pe.wait_ge(counted_dve, 1)
                nc.tensor.matmul(ps[0][:, 0:1], ones[:, :], below[:, 0:1], start=True, stop=True).then_inc(full_runs, 1)

                def run(net):
                    for n, (src, _) in enumerate(net.sides):
                        pe.wait_ge(run_sorted, n + 1)
                        for k in range(net.groups):
                            g = n * net.groups + k
                            if g >= 4:
                                pe.wait_ge(out[g % 2], 2 * ((g - 4) // 2 + 1))
                            for q in range(GROUP):
                                t = k * GROUP + q
                                last = nc.tensor.transpose(ps[g % 4][:, q * P:(q + 1) * P], src[:, t * P:(t + 1) * P], ident[:, :])
                            last.then_inc(transposed, 1)
                    pe.wait_ge(counted_dve, 2)
                    pe.wait_ge(out[0], len(net.sides) * net.groups)
                    nc.tensor.matmul(ps[0][:, 0:2], ones[:, :], below[:, :], start=True, stop=True).then_inc(counted, 1)
                either(pe, run)

            @block.scalar
            def _(act):
                def run(net):
                    for n in range(len(net.sides)):
                        for k in range(0, net.groups, 2):
                            act.wait_ge(transposed, n * net.groups + k + 1)
                            for dst, src, factor in net.halves(n, k):
                                nc.scalar.activation(dst, src, ACT.Copy, scale=factor).then_inc(out[0], 1)
                either(act, run)

T = 512
CHUNKS = NODES // T
PER_BATCH = 4096 // T
CT = 2
DT = 4
NS = 16
GQ = 4
NGR = NS // GQ
STEPS = NGR * DT
POOL_STEPS = (4, 8, 11, 15)
DA_OF = [s % 3 for s in range(STEPS - 1)] + [1]
OWN_STEPS = [s for s in range(STEPS) if s not in POOL_STEPS]
SOFT_AT = (13, 14, 15, 17)
DELTA_AT = (13, 14, 15, 16)
HALO = 3
LOG_EXP = "natural_log_exp_and_others"
TAPS = 4
SRC_F = 20
DST_F = 4
H_F = SRC_F + DST_F

PRE = ["mean", "var"] + [f"u{d}" for d in range(DT)] + [f"conv{d}" for d in range(DT)] + [f"res{d}" for d in range(DT)] \
    + ["dbc"] + [f"dt{d}" for d in range(DT)]
POST = ["out0", "out1", "mean2", "var2", "h"]
PE_AT = {"mean": 0, "out0": 0.5, "out1": 0.5, "var": 1.5, "mean2": 2.5, "u0": 4, "u1": 4, "u2": 4,
         "u3": 4, "conv0": 6, "conv1": 6, "var2": 7.5, "conv2": 7, "conv3": 7, "res0": 7.5, "res1": 7.5,
         "res2": 8.5, "res3": 8.5, "dbc": 9.5, "h": 10, "dt0": 11, "dt1": 11, "dt2": 12.5, "dt3": 12.5}
VEC_AT = {"centre": 0, "x2": 1, "norm": 3, "centre2": 3, "norm2": 8, "low_parts": 10, "lowest_part": 10}
ACT_AT = {"square": 1, "rstd": 3, "square2": 5, "u_out01": 5, "u_out23": 5, "u_silu01": 7, "u_silu23": 8,
          "rstd2": 8, "res_silu01": 9, "res_silu23": 9, "dbc_out": 12, "mid_part": 12, "h_out": 12}


def mamba(nc, x_dram, w, tables, ends_at_dram, ends_dram, counts):
    with ExitStack() as ctx:
        sb = lambda name, shape, dt=F32: ctx.enter_context(nc.sbuf_tensor(name, shape, dt))
        sem = lambda name: ctx.enter_context(nc.semaphore(name))
        xt = [sb(f"x_in{k}", [P, CT, T]) for k in range(2)]
        xn, sq, rs, rs2 = sb("xn", [P, CT, T]), sb("sq", [P, CT, T]), sb("rs", [P, T]), sb("rs2", [P, T])
        upre = sb("upre", [P, DT, HALO + T])
        u = [sb(f"u{k}", [P, DT, T]) for k in range(2)]
        sres = [sb(f"sres{k}", [P, DT, T]) for k in range(2)]
        delta, du = sb("delta", [P, DT, T]), sb("du", [P, DT, T])
        yt = upre[:, :, HALO:HALO + T]
        soft = [xn[:, 0, :], xn[:, 1, :], sq[:, 0, :], sq[:, 1, :]]
        hb = [sb(f"hb{k}", [P, GQ, T]) for k in range(4)]
        da = [sb(f"da{k}", [P, GQ, T]) for k in range(3)]
        bb = [sb(f"bb{k}", [P, GQ, T]) for k in range(2)]
        cb = [sb(f"cb{k}", [P, GQ, T]) for k in range(2)]
        x2, xn2, hst = sb("x2", [P, CT, T]), sb("xn2", [P, CT, T]), sb("hst", [P, T // P, H_F])
        parts = [sb(f"bc_parts{k}", [96, T], BF16) for k in range(2)]
        rest, mid, dtr = sb("bc_rest", [64, T]), sb("bc_mid", [64, T], BF16), sb("dtr", [32, T])
        carry, keep = sb("carry", [P, DT, NS]), sb("keep", [P, CHUNKS + 1])
        w_in, w_x = sb("w_in", [P, CT, 2 * DT * P]), sb("w_x", [P, DT, 64])
        w_dt, w_out = sb("w_dt", [32, DT * P]), sb("w_out", [P, DT, CT * P])
        w_g, att = sb("w_g", [P, CT, H_F]), sb("att", [P, 2, 16])
        w_att = sb("w_att", [P, CT, 2, 16])
        w_conv, diag = sb("w_conv", [P, DT, TAPS]), sb("diag", [P, DT * TAPS, P])
        conv_b, dt_b, skip = sb("conv_b", [P, DT]), sb("dt_b", [P, DT]), sb("skip", [P, DT])
        a_neg, eps = sb("a_neg", [P, DT, NS]), sb("eps", [P, 3])
        ident, mean_w, sel = sb("ident", [P, P]), sb("mean_w", [P, P]), sb("sel", [96, 2 * NS], BF16)
        end_idx, end_pos = sb("end_idx", [P, CW], I32), sb("end_pos", [P, CW], I32)
        chunk_step = sb("chunk_step", [P, CW], I32)
        psy = ctx.enter_context(nc.psum_tensor("psy", [P, DT, T], F32))
        pst = [ctx.enter_context(nc.psum_tensor(f"pst{k}", [P, T], F32)) for k in range(2)]
        psg = [ctx.enter_context(nc.psum_tensor(f"psg{k}", [P, T], F32)) for k in range(2)]

        w_loaded, const, weights_made, setup = sem("w_loaded"), sem("mamba_const"), sem("weights_made"), sem("setup_steps")
        x_loaded = [sem(f"x_loaded{k}") for k in range(2)]
        xres_loaded, x2_stored, xn2_stored, h_stored = sem("xres_loaded"), sem("x2_stored"), sem("xn2_stored"), sem("h_stored")
        pre_full, post_full = sem("pre_psum_full"), sem("post_psum_full")
        centred, squared, rstd_made, normed = sem("centred"), sem("squared"), sem("rstd_made"), sem("normed")
        upre_made, u_made, res_made, dbc_out = sem("upre_made"), sem("u_made"), sem("res_made"), sem("dbc_out")
        rest_made, mid_made, parts_made = sem("rest_made"), sem("mid_made"), sem("parts_made")
        abs_made, relu_made = sem("abs_made"), sem("relu_made")
        soft_made, delta_made, du_made = sem("soft_made"), sem("delta_made"), sem("du_made")
        bc_full, bc_made, da_made = sem("bc_psum_full"), sem("bc_made"), sem("da_made")
        dbu_made, pool_dbu_made, scanned, carried, products = sem("dbu_made"), sem("pool_dbu_made"), sem("scanned"), sem("carried"), sem("products")
        summed, y_read, gated = sem("summed"), sem("y_read"), sem("gated")
        x2_made, centred2, squared2, rstd2_made = sem("x2_made"), sem("centred2"), sem("squared2"), sem("rstd2_made")
        normed2, h_out = sem("normed2"), sem("h_out")
        idx_loaded, pos_made, scattered = sem("idx_loaded"), sem("pos_made"), sem("scattered")
        scattered_beyond = [sem(f"scattered_beyond{k}") for k in range(2)]

        def order(pre, post):
            names = (POST if post else []) + (PRE if pre else [])
            return sorted(names, key=lambda n: PE_AT[n])

        class Body:

            def __init__(self, i, next_pair, par, scan=True, pre=True, post=True, first=0, before=()):
                self.i, self.next_pair, self.par, self.scan, self.pre, self.post = i, next_pair, par, scan, pre, post
                self.first, self.before, self.order = first, before, order(pre, post)

            def slot(self, name):
                return (self.order.index(name) + self.first) % 2

        def bodies(eng, run):
            a, last = len(PRE), PRE[-2:]
            run(Body(-1, 0, 1, scan=False, post=False))
            run(Body(0, 0, 0, post=False, first=a % 2, before=last))
            assert (len(PRE) + len(POST)) % 2 == 0
            with eng.Fori(0, (CHUNKS - 2) // 2) as j:
                run(Body(j * 2 + 1, j + 1, 1, before=last))
                run(Body(j * 2 + 2, j + 1, 0, before=last))
            run(Body(CHUNKS - 1, CHUNKS // 2, 1, pre=False, before=last))
            run(Body(CHUNKS, CHUNKS // 2, 0, scan=False, pre=False, first=len(POST) % 2, before=POST[-2:]))

        sp_passed, pool_passed = sem("m_sp_passed"), sem("m_pool_passed")
        with nc.Block() as block:
            @block.sync
            def _(sp):
                loads = [(w_in, w["in"], "(c p) e -> p c e"), (w_x, w["x"], "(c p) e -> p c e"),
                         (w_out, w["out"], "(c p) e -> p c e"), (w_conv, w["conv"], "(c p) e -> p c e")]
                for t, d, how in loads:
                    sp.dma_start(t[:, :, :], d.rearrange(how, p=P)).then_inc(w_loaded, 16)
                sp.dma_start(w_g[:, :, 0:16], w["gat"].rearrange("(c p) e -> p c e", p=P)).then_inc(w_loaded, 16)
                sp.dma_start(w_dt[:, :], w["dt"]).then_inc(w_loaded, 16)
                sp.dma_start(a_neg[:, :, :], w["a_log"].rearrange("(c p) e -> p c e", p=P)).then_inc(w_loaded, 16)
                for t, d in ((conv_b, w["conv_b"]), (dt_b, w["dt_b"]), (skip, w["skip"])):
                    sp.dma_start(t[:, :], d).then_inc(w_loaded, 16)
                for k in range(2):
                    sp.dma_start(att[:, k, :], w["att"][k:k + 1, :].to_broadcast([P, 16])).then_inc(w_loaded, 16)
                def run(b):
                    i = b.i
                    if b.pre:
                        if not (isinstance(i, int) and i < 1):
                            wait_alone(sp, centred, i, sp_passed)
                        sp.dma_start(xt[1 - b.par][:, :, :], x_dram[bass.ds(i + 1, 1)].rearrange("o p (c t) -> (o p) c t", c=CT)).then_inc(x_loaded[1 - b.par], 16)
                    if b.post:
                        wait_alone(sp, x2_made, i * 2, sp_passed)
                        sp.dma_start(tables["x2"][bass.ds(i - 1, 1)].rearrange("o p (c t) -> (o p) c t", c=CT), x2[:, :, :]).then_inc(x2_stored, 16)
                    if b.post:
                        wait_alone(sp, normed2, i, sp_passed)
                        sp.dma_start(tables["xn2"][bass.ds(i - 1, 1)].rearrange("o p (c t) -> (o p) c t", c=CT), xn2[:, :, :]).then_inc(xn2_stored, 16)
                        wait_alone(sp, h_out, i, sp_passed)
                        rows = bass.ds((i - 1) * T, T)
                        sp.dma_start(tables["src"][rows, :].rearrange("(k p) f -> p k f", p=P), hst[:, :, 0:SRC_F]).then_inc(h_stored, 16)
                        sp.dma_start(tables["dst"][rows, :].rearrange("(k p) f -> p k f", p=P), hst[:, :, SRC_F:H_F]).then_inc(h_stored, 16)
                    if b.scan:
                        if b.post:
                            wait_alone(sp, x2_stored, i * 16, sp_passed)
                            wait_alone(sp, centred2, i, sp_passed)
                        sp.dma_start(x2[:, :, :], x_dram[bass.ds(i, 1)].rearrange("o p (c t) -> (o p) c t", c=CT)).then_inc(xres_loaded, 16)
                bodies(sp, run)
                sp.wait_ge(x2_stored, CHUNKS * 16)
                sp.wait_ge(xn2_stored, CHUNKS * 16)
                sp.wait_ge(h_stored, CHUNKS * 32)

            @block.gpsimd
            def _(pool):
                g = nc.gpsimd
                g.memset(mean_w[:, :], 1.0 / (CT * P)).then_inc(const, 1)
                g.memset(eps[:, 0:1], 1e-6).then_inc(const, 1)
                g.memset(eps[:, 1:2], 1e-5).then_inc(const, 1)
                g.memset(eps[:, 2:3], 1.0).then_inc(const, 1)
                g.memset(carry[:, :, :], 0.0).then_inc(const, 1)
                g.memset(upre[:, :, 0:HALO], 0.0).then_inc(const, 1)
                g.memset(keep[:, :], 1.0).then_inc(const, 1)
                g.memset(ident[:, :], 0.0).then_inc(const, 1)
                g.memset(sel[:, :], 0.0).then_inc(const, 1)
                g.memset(chunk_step[:, :], CHUNK).then_inc(const, 1)
                pool.wait_ge(const, 10)
                g.memset(keep[:, 0:CHUNKS + 1:PER_BATCH], 0.0).then_inc(const, 1)
                g.affine_select(out=ident[:, :], in_=ident[:, :], compare_op=ALU.not_equal, fill=1.0, base=0,
                                pattern=[[-1, P]], channel_multiplier=1).then_inc(const, 1)
                for k in range(3):
                    g.affine_select(out=sel[:, :], in_=sel[:, :], compare_op=ALU.not_equal, fill=1.0, base=-32 * k,
                                    pattern=[[-1, 2 * NS]], channel_multiplier=1).then_inc(const, 1)
                    pool.wait_ge(const, 13 + k)
                def load_ends(c):
                    g.dma_start(end_idx[:, :], ends_at_dram[bass.ds(c * CHUNK, CHUNK), :].rearrange("(p c) o -> p (c o)", p=P)).then_inc(idx_loaded, 16)

                def scatter(k, done=scattered):
                    g.indirect_dma_start(ends_dram, bass.IndirectOffsetOnAxis(ap=end_idx[:, k:k + 1].bitcast(U32), axis=0),
                                         end_pos[:, k:k + 1], None, bounds_check=GROUPS + OFF - 1, oob_is_err=False).then_inc(done, 16)

                g.iota(end_pos[:, :], pattern=[[1, CW]], base=1 + CHUNKS * CHUNK, channel_multiplier=CW).then_inc(pos_made, 1)
                beyond = pool.value_load(counts[0:1, 1:2], min_val=1, max_val=EDGES // CHUNK - CHUNKS)
                with pool.Fori(0, beyond) as done:
                    load_ends(done + CHUNKS)
                    wait_alone(pool, idx_loaded, done * 16 + 16, pool_passed)
                    wait_alone(pool, pos_made, done + 1, pool_passed)
                    for k in range(CW):
                        scatter(k, scattered_beyond[k % 2])
                    for half in scattered_beyond:
                        wait_alone(pool, half, done * (8 * CW) + 8 * CW, pool_passed)
                    g.tensor_tensor(end_pos[:, :], end_pos[:, :], chunk_step[:, :], ALU.add).then_inc(pos_made, 1)
                wait_alone(pool, pos_made, beyond + 1, pool_passed)
                g.iota(end_pos[:, :], pattern=[[1, CW]], base=1, channel_multiplier=CW).then_inc(pos_made, 1)

                def run(b):
                    if not b.scan:
                        return
                    i = b.i
                    done = beyond + i
                    load_ends(i)
                    wait_alone(pool, idx_loaded, done * 16 + 16, pool_passed)
                    wait_alone(pool, pos_made, done + 2, pool_passed)
                    scatters = iter(range(CW))
                    for s in range(STEPS):
                        if s in POOL_STEPS:
                            group, d = divmod(s, DT)
                            if s >= 4 or not (isinstance(i, int) and i == 0):
                                wait_alone(pool, summed, i * STEPS + s - 3, pool_passed)
                            wait_alone(pool, du_made, i * 4 + d + 1, pool_passed)
                            wait_alone(pool, bc_made, i * 32 + 8 * group + GQ, pool_passed)
                            g.tensor_tensor(hb[s % 4][:, :, :], bb[group % 2][:, :, :], du[:, d:d + 1, :].to_broadcast([P, GQ, T]), ALU.mult).then_inc(pool_dbu_made, 1)
                            for k in range(CW // len(POOL_STEPS)):
                                scatter(next(scatters))
                    wait_alone(pool, scattered, i * (16 * CW) + 16 * CW, pool_passed)
                    g.tensor_tensor(end_pos[:, :], end_pos[:, :], chunk_step[:, :], ALU.add).then_inc(pos_made, 1)
                bodies(pool, run)

            @block.vector
            def _(dve):
                v = nc.vector
                st = Steps(dve, setup)
                dve.wait_ge(w_loaded, 16 * 12)
                dve.wait_ge(const, 15)
                for d in range(DT):
                    for k in range(TAPS):
                        st(v.tensor_scalar(diag[:, d * TAPS + k, :], ident[:, :], w_conv[:, d, k:k + 1], None, ALU.mult))
                for c in range(CT):
                    for k in range(2):
                        st(v.tensor_tensor(w_att[:, c, k, :], w_g[:, c, 0:16], att[:, k, :], ALU.mult))
                st.settle()
                for c in range(CT):
                    (v.tensor_reduce(w_g[:, c, 16:24], w_att[:, c, :, :].rearrange("p k (h e) -> p (k h) e", e=4),
                                       mybir.AxisListType.X, ALU.add)).then_inc(weights_made, 1)
                dve.wait_ge(weights_made, 1 + CT)
                v.tensor_scalar(a_neg[:, :, :], a_neg[:, :, :], -1.0, None, ALU.mult).then_inc(weights_made, 1)

                def piece(b, name):
                    i, n, l = b.i, b.i + 1, b.i - 1
                    if name == "centre":
                        s = b.slot("mean")
                        dve.wait_ge(pre_full, n * 19 + 1)
                        if b.scan:
                            dve.wait_ge(delta_made, b.i * 4 + 2)
                        v.tensor_tensor(xn[:, :, :], xt[1 - b.par][:, :, :], psg[s][:, None, :].to_broadcast([P, CT, T]), ALU.subtract).then_inc(centred, 1)
                    elif name == "norm":
                        dve.wait_ge(rstd_made, n * 2 + 2)
                        v.tensor_tensor(xn[:, :, :], xn[:, :, :], rs[:, None, :].to_broadcast([P, CT, T]), ALU.mult).then_inc(normed, 1)
                    elif name == "low_parts":
                        s = b.slot("dbc")
                        dve.wait_ge(dbc_out, n * 2 + 2)
                        v.tensor_tensor(rest[32:64, :], psg[s][32:64, :], parts[1 - b.par][32:64, :], ALU.subtract).then_inc(rest_made, 1)
                    elif name == "lowest_part":
                        dve.wait_ge(mid_made, n * 2 + 2)
                        v.tensor_tensor(parts[1 - b.par][0:32, :], rest[32:64, :], mid[32:64, :], ALU.subtract).then_inc(parts_made, 1)
                    elif name == "y":
                        if b.scan:
                            dve.wait_ge(pre_full, b.i * 19 + 10)
                            dve.wait_ge(upre_made, b.i * 5 + 5)
                        for d in range(DT):
                            dve.wait_ge(summed, l * STEPS + STEPS - DT + d + 1)
                            v.scalar_tensor_tensor(yt[:, d, :], u[1 - b.par][:, d, :], skip[:, d:d + 1], psy[:, d, :],
                                                   ALU.mult, ALU.add).then_inc(y_read, 1)
                        dve.wait_ge(y_read, l * 4 + 4)
                        v.tensor_tensor(yt[:, :, :], yt[:, :, :], sres[1 - b.par][:, :, :], ALU.mult).then_inc(gated, 1)
                    elif name == "x2":
                        for c in range(CT):
                            s = b.slot(f"out{c}")
                            dve.wait_ge(post_full, l * 5 + c + 1)
                            if c == 0:
                                dve.wait_ge(xres_loaded, l * 16 + 16)
                            v.tensor_tensor(x2[:, c, :], psg[s][:, :], x2[:, c, :], ALU.add).then_inc(x2_made, 1)
                    elif name == "centre2":
                        s = b.slot("mean2")
                        dve.wait_ge(post_full, l * 5 + 3)
                        v.tensor_tensor(xn2[:, :, :], x2[:, :, :], psg[s][:, None, :].to_broadcast([P, CT, T]), ALU.subtract).then_inc(centred2, 1)
                    elif name == "norm2":
                        dve.wait_ge(rstd2_made, l * 2 + 2)
                        v.tensor_tensor(xn2[:, :, :], xn2[:, :, :], rs2[:, None, :].to_broadcast([P, CT, T]), ALU.mult).then_inc(normed2, 1)

                def deltas(c, par, d):
                    dve.wait_ge(soft_made, c * 4 + d + 1)
                    v.tensor_tensor(delta[:, d, :], delta[:, d, :], soft[d], ALU.add).then_inc(delta_made, 1)
                    dve.wait_ge(delta_made, c * 4 + d + 1)
                    if not (isinstance(c, int) and c == 0):
                        if STEPS - DT + d in POOL_STEPS:
                            dve.wait_ge(pool_dbu_made, c * len(POOL_STEPS))
                        else:
                            dve.wait_ge(dbu_made, (c - 1) * len(OWN_STEPS) + OWN_STEPS.index(STEPS - DT + d) + 1)
                    v.tensor_tensor(du[:, d, :], delta[:, d, :], u[par][:, d, :], ALU.mult).then_inc(du_made, 1)

                def inputs(i, s):
                    if s in POOL_STEPS:
                        return
                    g, d = divmod(s, DT)
                    if s >= 4 or not (isinstance(i, int) and i == 0):
                        dve.wait_ge(summed, i * STEPS + s - 3)
                    if g == 0:
                        dve.wait_ge(du_made, i * 4 + d + 1)
                    dve.wait_ge(bc_made, i * 32 + 8 * g + GQ)
                    v.tensor_tensor(hb[s % 4][:, :, :], bb[g % 2][:, :, :], du[:, d:d + 1, :].to_broadcast([P, GQ, T]), ALU.mult).then_inc(dbu_made, 1)

                def scans(i, s):
                    g, d = divmod(s, DT)
                    if s in POOL_STEPS:
                        dve.wait_ge(pool_dbu_made, i * len(POOL_STEPS) + POOL_STEPS.index(s) + 1)
                    else:
                        dve.wait_ge(dbu_made, i * len(OWN_STEPS) + OWN_STEPS.index(s) + 1)
                    if not (isinstance(i, int) and i == 0):
                        dve.wait_ge(carried, (i - 1) * STEPS + s + 1)
                    for q in range(GQ):
                        dve.wait_ge(da_made, i * 64 + GQ * s + q + 1)
                        v.tensor_tensor_scan(hb[s % 4][:, q, :], da[DA_OF[s]][:, q, :], hb[s % 4][:, q, :],
                                             carry[:, d, GQ * g + q:GQ * g + q + 1], ALU.mult, ALU.add).then_inc(scanned, 1)

                def carries(b, s):
                    g, d = divmod(s, DT)
                    i = b.i
                    dve.wait_ge(scanned, i * 64 + GQ * (s + 1))
                    v.tensor_scalar(carry[:, d, GQ * g:GQ * (g + 1)], hb[s % 4][:, :, T - 1], keep[:, bass.ds(i + 1, 1)], None,
                                    ALU.mult).then_inc(carried, 1)

                def outputs(i, s):
                    g, d = divmod(s, DT)
                    dve.wait_ge(carried, i * STEPS + s + 1)
                    dve.wait_ge(bc_made, i * 32 + 8 * (g + 1))
                    v.tensor_tensor(hb[s % 4][:, :, :], hb[s % 4][:, :, :], cb[g % 2][:, :, :], ALU.mult).then_inc(products, 1)

                def run(b):
                    at = lambda s: [n for n, k in VEC_AT.items() if k == s and (b.post if n.endswith("2") else b.pre)]

                    def made(s):
                        for d in range(DT):
                            if DELTA_AT[d] == s and b.pre:
                                deltas(b.i + 1, 1 - b.par, d)
                            if DELTA_AT[d] == s + STEPS and b.scan:
                                deltas(b.i, b.par, d)
                    if b.post:
                        piece(b, "y")
                    if b.scan:
                        inputs(b.i, 0)
                        scans(b.i, 0)
                        for s in range(STEPS):
                            if s + 1 < STEPS:
                                inputs(b.i, s + 1)
                            carries(b, s)
                            if s + 1 < STEPS:
                                scans(b.i, s + 1)
                            outputs(b.i, s)
                            made(s)
                            for name in at(s):
                                piece(b, name)
                    else:
                        for s in range(STEPS):
                            made(s)
                            for name in at(s):
                                piece(b, name)
                    if b.post:
                        dve.wait_ge(xn2_stored, b.i * 16)
                bodies(dve, run)

            @block.tensor
            def _(pe):
                mm = nc.tensor.matmul
                pe.wait_ge(weights_made, 2 + CT)
                pe.wait_ge(const, 15)

                def read(name, n, l):
                    tile = int(name[-1]) if name[-1].isdigit() else 0
                    for prefix, made, value in (
                            ("mean2", centred2, l + 1), ("var2", rstd2_made, l * 2 + 1), ("h", h_out, l + 1),
                            ("out", x2_made, l * 2 + tile + 1), ("mean", centred, n + 1), ("var", rstd_made, n * 2 + 1),
                            ("u", upre_made, n * 5 + tile + 1), ("conv", u_made, n * 4 + tile + 1),
                            ("res", res_made, n * 4 + tile + 1), ("dbc", rest_made, n + 1),
                            ("dt", relu_made, n * 4 + tile + 1)):
                        if name.startswith(prefix):
                            pe.wait_ge(made, value)
                            if prefix == "dt":
                                pe.wait_ge(abs_made, n * 8 + 2 * tile + 1)
                            return

                def use(b, name):
                    i, n, l = b.i, b.i + 1, b.i - 1
                    k = b.order.index(name)
                    ps = psg[b.slot(name)]
                    nxt = 1 - b.par
                    if k >= 2:
                        read(b.order[k - 2], n, l)
                    elif b.before:
                        read(b.before[k], i, l - 1)
                    kind, d = (name[:-1], int(name[-1])) if name[-1].isdigit() and name not in ("mean2", "var2") else (name, 0)
                    if kind == "mean":
                        pe.wait_ge(x_loaded[nxt], b.next_pair * 16 + 16)
                        terms = [(mean_w[:, :], xt[nxt][:, c, :]) for c in range(CT)]
                    elif kind == "var":
                        pe.wait_ge(squared, n + 1)
                        terms = [(mean_w[:, :], sq[:, c, :]) for c in range(CT)]
                    elif kind == "u" or kind == "res":
                        pe.wait_ge(normed, n + 1)
                        e = (d + DT * (kind == "res")) * P
                        terms = [(w_in[:, c, e:e + P], xn[:, c, :]) for c in range(CT)]
                    elif kind == "conv":
                        pe.wait_ge(upre_made, n * 5 + d + 1)
                        terms = [(diag[:, d * TAPS + t, :], upre[:, d, t:t + T]) for t in range(TAPS)]
                    elif kind == "dbc":
                        pe.wait_ge(u_made, n * 4 + 4)
                        terms = [(w_x[:, c, :], u[nxt][:, c, :]) for c in range(DT)]
                        ps = ps[0:64, :]
                    elif kind == "dt":
                        pe.wait_ge(dbc_out, n * 2 + 1)
                        terms = [(w_dt[:, d * P:(d + 1) * P], dtr[:, :])]
                    elif kind == "out":
                        pe.wait_ge(gated, l + 1)
                        terms = [(w_out[:, c, d * P:(d + 1) * P], yt[:, c, :]) for c in range(DT)]
                    elif kind == "mean2":
                        pe.wait_ge(x2_made, l * 2 + 2)
                        terms = [(mean_w[:, :], x2[:, c, :]) for c in range(CT)]
                    elif kind == "var2":
                        pe.wait_ge(squared2, l + 1)
                        terms = [(mean_w[:, :], sq[:, c, :]) for c in range(CT)]
                    elif kind == "h":
                        pe.wait_ge(normed2, l + 1)
                        for t in range(T // P):
                            for c in range(CT):
                                last = mm(ps[:, t * H_F:(t + 1) * H_F], xn2[:, c, t * P:(t + 1) * P], w_g[:, c, :],
                                          start=(c == 0), stop=(c == CT - 1))
                        last.then_inc(post_full, 1)
                        return
                    out = ps if kind == "dbc" else ps[:, :]
                    for k, (a, x) in enumerate(terms):
                        last = mm(out, a, x, start=(k == 0), stop=(k == len(terms) - 1))
                    last.then_inc(pre_full if name in PRE else post_full, 1)

                def broadcast(b, g):
                    i = b.i
                    if g == 0:
                        pe.wait_ge(parts_made, i + 1)
                        pe.wait_ge(mid_made, i * 2 + 2)
                    for k in range(2 * GQ):
                        n = GQ * g + k if k < GQ else NS + GQ * g + k - GQ
                        t = 8 * g + k
                        if t >= 2 or not (isinstance(i, int) and i == 0):
                            pe.wait_ge(bc_made, i * 32 + t - 1)
                        mm(pst[t % 2][:, :], sel[:, n:n + 1].to_broadcast([96, P]), parts[b.par][:, :], start=True, stop=True).then_inc(bc_full, 1)

                def total(b, s):
                    g, d = divmod(s, DT)
                    i = b.i
                    pe.wait_ge(products, i * STEPS + s + 1)
                    if g == 0 and not (isinstance(i, int) and i == 0):
                        pe.wait_ge(y_read, (i - 1) * 4 + d + 1)
                    for q in range(GQ):
                        last = mm(psy[:, d, :], ident[:, :], hb[s % 4][:, q, :], start=(g == 0 and q == 0), stop=(g == NGR - 1 and q == GQ - 1))
                    last.then_inc(summed, 1)

                def run(b):
                    if b.scan:
                        broadcast(b, 0)
                    for s in range(STEPS):
                        if b.scan and s % DT == 1 and s // DT + 1 < NGR:
                            broadcast(b, s // DT + 1)
                        for name in b.order:
                            if int(PE_AT[name]) == s:
                                use(b, name)
                        if b.scan:
                            total(b, s)
                bodies(pe, run)

            @block.scalar
            def _(act):
                f = nc.scalar.activation
                act.wait_ge(w_loaded, 16 * 12)
                act.wait_ge(const, 15)
                nc.scalar.preload_act_table_set(LOG_EXP)
                f(a_neg[:, :, :], a_neg[:, :, :], ACT.Exp).then_inc(weights_made, 1)
                act.wait_ge(weights_made, 2 + CT)

                def piece(b, name):
                    i, n, l = b.i, b.i + 1, b.i - 1
                    nxt = 1 - b.par
                    if name == "square":
                        act.wait_ge(centred, n + 1)
                        if b.scan:
                            act.wait_ge(delta_made, b.i * 4 + 4)
                        f(sq[:, :, :], xn[:, :, :], ACT.Square).then_inc(squared, 1)
                    elif name == "rstd":
                        s = b.slot("var")
                        act.wait_ge(pre_full, n * 19 + 2)
                        f(rs[:, :], psg[s][:, :], ACT.Ln, bias=eps[:, 0:1]).then_inc(rstd_made, 1)
                        act.wait_ge(rstd_made, n * 2 + 1)
                        f(rs[:, :], rs[:, :], ACT.Exp, scale=-0.5).then_inc(rstd_made, 1)
                    elif name.startswith("u_out"):
                        for d in (int(name[-2]), int(name[-1])):
                            s = b.slot(f"u{d}")
                            act.wait_ge(pre_full, n * 19 + 3 + d)
                            if b.post and d == 0:
                                act.wait_ge(post_full, l * 5 + 2)
                            f(upre[:, d, HALO:HALO + T], psg[s][:, :], ACT.Copy).then_inc(upre_made, 1)
                    elif name.startswith("u_silu"):
                        for d in (int(name[-2]), int(name[-1])):
                            s = b.slot(f"conv{d}")
                            act.wait_ge(pre_full, n * 19 + 7 + d)
                            if b.post and d == 0:
                                act.wait_ge(gated, l + 1)
                            f(u[nxt][:, d, :], psg[s][:, :], ACT.Silu, bias=conv_b[:, d:d + 1]).then_inc(u_made, 1)
                        nc.scalar.preload_act_table_set(LOG_EXP)
                        if d == DT - 1:
                            f(upre[:, :, 0:HALO], upre[:, :, T:T + HALO], ACT.Copy, scale=keep[:, bass.ds(n + 1, 1)] if not isinstance(n, int) or n + 1 <= CHUNKS else 0.0).then_inc(upre_made, 1)
                    elif name.startswith("res_silu"):
                        for d in (int(name[-2]), int(name[-1])):
                            s = b.slot(f"res{d}")
                            act.wait_ge(pre_full, n * 19 + 11 + d)
                            f(sres[nxt][:, d, :], psg[s][:, :], ACT.Silu).then_inc(res_made, 1)
                        nc.scalar.preload_act_table_set(LOG_EXP)
                    elif name == "dbc_out":
                        s = b.slot("dbc")
                        act.wait_ge(pre_full, n * 19 + 15)
                        f(dtr[:, :], psg[s][0:32, :], ACT.Copy).then_inc(dbc_out, 1)
                        f(parts[nxt][32:64, :], psg[s][32:64, :], ACT.Copy).then_inc(dbc_out, 1)
                    elif name == "mid_part":
                        act.wait_ge(rest_made, n + 1)
                        f(mid[32:64, :], rest[32:64, :], ACT.Copy).then_inc(mid_made, 1)
                        act.wait_ge(mid_made, n * 2 + 1)
                        f(parts[nxt][64:96, :], mid[32:64, :], ACT.Copy).then_inc(mid_made, 1)
                    elif name == "square2":
                        act.wait_ge(centred2, l + 1)
                        if b.pre:
                            act.wait_ge(pre_full, n * 19 + 2)
                        if b.scan:
                            act.wait_ge(delta_made, b.i * 4 + 4)
                        f(sq[:, :, :], xn2[:, :, :], ACT.Square).then_inc(squared2, 1)
                    elif name == "rstd2":
                        s = b.slot("var2")
                        act.wait_ge(post_full, l * 5 + 4)
                        f(rs2[:, :], psg[s][:, :], ACT.Ln, bias=eps[:, 1:2]).then_inc(rstd2_made, 1)
                        act.wait_ge(rstd2_made, l * 2 + 1)
                        f(rs2[:, :], rs2[:, :], ACT.Exp, scale=-0.5).then_inc(rstd2_made, 1)
                    elif name == "h_out":
                        s = b.slot("h")
                        act.wait_ge(post_full, l * 5 + 5)
                        f(hst[:, :, :], psg[s][:, 0:T // P * H_F], ACT.Copy).then_inc(h_out, 1)

                def softs(c, bank, d):
                    act.wait_ge(pre_full, c * 19 + 16 + d)
                    if not (isinstance(c, int) and c == 0):
                        act.wait_ge(da_made, (c - 1) * 64 + GQ * (STEPS - DT + d + 1))
                    f(soft[d], psg[bank][:, :], ACT.Abs, bias=dt_b[:, d:d + 1]).then_inc(abs_made, 1)
                    f(delta[:, d, :], psg[bank][:, :], ACT.Relu, bias=dt_b[:, d:d + 1]).then_inc(relu_made, 1)
                    act.wait_ge(relu_made, c * 4 + d + 1)
                    f(soft[d], soft[d], ACT.Exp, scale=-1.0).then_inc(abs_made, 1)
                    act.wait_ge(abs_made, c * 8 + 2 * d + 2)
                    f(soft[d], soft[d], ACT.Ln, bias=eps[:, 2:3]).then_inc(soft_made, 1)

                def spread(b, g, which):
                    i = b.i
                    if g >= 2:
                        act.wait_ge(products, i * STEPS + (g - 1) * DT)
                    elif not (isinstance(i, int) and i == 0):
                        act.wait_ge(products, (i - 1) * STEPS + (g + 3) * DT)
                    dst = (bb, cb)[which][g % 2]
                    for q in range(GQ):
                        t = 8 * g + GQ * which + q
                        act.wait_ge(bc_full, i * 32 + t + 1)
                        f(dst[:, q, :], pst[t % 2][:, :], ACT.Copy).then_inc(bc_made, 1)

                def decays(b, s):
                    g, d = divmod(s, DT)
                    i = b.i
                    if g == 0:
                        act.wait_ge(delta_made, i * 4 + d + 1)
                    earlier = [k for k in range(s) if DA_OF[k] == DA_OF[s]]
                    if earlier:
                        act.wait_ge(scanned, i * 64 + GQ * (earlier[-1] + 1))
                    elif not (isinstance(i, int) and i == 0):
                        last = max(k for k in range(STEPS) if DA_OF[k] == DA_OF[s])
                        act.wait_ge(scanned, (i - 1) * 64 + GQ * (last + 1))
                    for q in range(GQ):
                        n = GQ * g + q
                        f(da[DA_OF[s]][:, q, :], delta[:, d, :], ACT.Exp, scale=a_neg[:, d, n:n + 1]).then_inc(da_made, 1)

                def run(b):
                    at = lambda s: [n for n, k in ACT_AT.items() if k == s and (b.post if n in ("square2", "rstd2", "h_out") else b.pre)]
                    if b.scan:
                        spread(b, 0, 0)
                    for s in range(STEPS):
                        if b.scan:
                            decays(b, s)
                            if s == 0:
                                spread(b, 0, 1)
                            if s % DT == 2 and s // DT + 1 < NGR:
                                spread(b, s // DT + 1, 0)
                                spread(b, s // DT + 1, 1)
                        for d in range(DT):
                            if SOFT_AT[d] == s and b.pre:
                                softs(b.i + 1, b.slot(f"dt{d}"), d)
                            if SOFT_AT[d] == s + STEPS and b.scan:
                                softs(b.i, (b.first + d) % 2, d)
                        for name in at(s):
                            piece(b, name)
                    if b.post:
                        act.wait_ge(h_stored, b.i * 32)
                bodies(act, run)

HEADS = 4
EXPERTS = 4
GH = HEADS * EXPERTS
SEG_F = GH + HEADS + HEADS
NT = NODES // P
BIG = 1e30
PEAKS_AT, PEAK_LANES_AT, SUMS_AT, SUM_LANES_AT, GRAPH_STEPS = 17, 19, 59, 61, 83
AX = mybir.AxisListType.X

FF = 512
FT = FF // P
UNITS = EXPERTS * FT
RING = 4
LAG = 3
BESIDE_EDGES, BESIDE_GATES = 6, 2
EARLY = 2 * (BESIDE_EDGES + BESIDE_GATES)
PE_UNIT = {"peaks": 2, "peak_lanes": 3, "sums": 9, "sum_lanes": 10}
ACT_UNIT = {"exps": 5, "store": 15}
PE_UNIT_FIRST = {"peaks": 14, "peak_lanes": 15, "sums": 17, "sum_lanes": 18}
ACT_UNIT_FIRST = {"exps": 16, "store": 18}

GATE_UNITS = {"weights": (1, 0, 10), "rstd": (1, 1, 2), "softmax": (1, 1, 12)}


class EarlyExperts:

    def __init__(self, nc, sb, sem, weights, xn2_dram, y_dram, ps_up, ps_down):
        self.nc, self.xn2_dram, self.y_dram, self.ps_up, self.ps_down = nc, xn2_dram, y_dram, ps_up, ps_down
        self.w1, self.w2, self.b1, self.b2, self.w_loaded = weights
        self.xn = [sb(f"e_xn{k}", [P, CT, T]) for k in range(2)]
        self.hid = [sb(f"e_hid{k}", [P, T]) for k in range(RING)]
        self.y = [sb(f"e_y{e}", [P, CT, T]) for e in range(EXPERTS)]
        self.loaded = [sem(f"e_xn_loaded{k}") for k in range(2)]
        self.y_stored = [sem(f"e_y_stored{e}") for e in range(EXPERTS)]
        self.up, self.gelu, self.down, self.y_out = sem("e_up_full"), sem("e_gelu_made"), sem("e_down_done"), sem("e_y_out")

    def load(self, sp, n, par, passed):
        if not (isinstance(n, int) and n == 0):
            wait_alone(sp, self.gelu, (n * 2 + (par - 1)) * UNITS, passed)
        sp.dma_start(self.xn[par][:, :, :], self.xn2_dram[bass.ds(n * 2 + par, 1)].rearrange("o p (c t) -> (o p) c t", c=CT)).then_inc(self.loaded[par], 16)

    def products(self, pe, n, par, beside=lambda k: None):
        mm = self.nc.tensor.matmul
        c = n * 2 + par
        later = not (isinstance(c, int) and c == 0)
        pe.wait_ge(self.loaded[par], n * 16 + 16)
        for k in range(UNITS + LAG):
            beside(k)
            if k < UNITS:
                e, ft = divmod(k, FT)
                if k >= RING or later:
                    pe.wait_ge(self.gelu, c * UNITS + (k - RING + 1))
                for t in range(CT):
                    last = mm(self.ps_up[k % RING][:, :], self.w1[:, e, t, ft * P:(ft + 1) * P], self.xn[par][:, t, :], start=(t == 0), stop=(t == CT - 1))
                last.then_inc(self.up, 1)
            if k >= LAG:
                q = k - LAG
                e, ft = divmod(q, FT)
                pe.wait_ge(self.gelu, c * UNITS + (q + 1))
                if ft == 0 and (e > 0 or later):
                    pe.wait_ge(self.y_out, c * (CT * EXPERTS) + CT * e)
                for t in range(CT):
                    last = mm(self.ps_down[t][:, :], self.w2[:, q, t * P:(t + 1) * P], self.hid[q % RING][:, :], start=(ft == 0), stop=(ft == FT - 1))
                last.then_inc(self.down, 1)

    def gelus(self, act, n, par, beside=lambda k: None):
        f = self.nc.scalar.activation
        c = n * 2 + par
        later = not (isinstance(c, int) and c == 0)
        for k in range(UNITS + LAG):
            beside(k)
            if k < UNITS:
                act.wait_ge(self.up, c * UNITS + (k + 1))
                if k >= RING or later:
                    act.wait_ge(self.down, c * UNITS + (k - RING + 1))
                f(self.hid[k % RING][:, :], self.ps_up[k % RING][:, :], ACT.Gelu, bias=self.b1[:, k:k + 1]).then_inc(self.gelu, 1)
            if k >= LAG and (k - LAG) % FT == FT - 1:
                e = (k - LAG) // FT
                act.wait_ge(self.down, c * UNITS + (e + 1) * FT)
                if later:
                    act.wait_ge(self.y_stored[e], c * 16)
                for t in range(CT):
                    f(self.y[e][:, t, :], self.ps_down[t][:, :], ACT.Identity, bias=self.b2[:, e * CT + t:e * CT + t + 1]).then_inc(self.y_out, 1)
                act.wait_ge(self.y_out, c * (CT * EXPERTS) + CT * (e + 1))
                act.dma_start(self.y_dram[bass.ds(c, 1), :, e * CT * T:(e + 1) * CT * T].rearrange("o p (c t) -> (o p) c t", c=CT), self.y[e][:, :, :]).then_inc(self.y_stored[e], 16)


def attention(nc, keys_dram, src_dram, dst_dram, ends_dram, tables, w, seg_dram, gates_dram, counts, weights, y_dram, placed_dram):
    with ExitStack() as ctx:
        sb = lambda name, shape, dt=F32: ctx.enter_context(nc.sbuf_tensor(name, shape, dt))
        sem = lambda name: ctx.enter_context(nc.semaphore(name))
        pair = lambda name, shape, dt=F32: [sb(f"{name}{k}", shape, dt) for k in range(2)]
        ident, ones = sb("g_ident", [P, P]), sb("g_ones", [P, P])
        zero_row, eps = sb("zero_row", [P, CW]), sb("g_eps", [P, 1])
        ends_i = sb("ends_i", [P, 2, NT], I32)
        ends = sb("ends_f", [P, 2, NT + 1])
        tail_row, last = sb("tail_row", [1, 2 * P]), sb("carry_row", [1, 2 * P + 1])
        node_q = sb("node_q", [P, 4, NT])
        end_idx, start_idx = sb("g_end_idx", [P, NT], I32), sb("g_start_idx", [P, NT], I32)
        node_ad, first_ad, edge_ad = sb("node_a_dst", [P, NT, DST_F]), pair("first_a_dst", [P, DST_F]), sb("edge_a_dst", [P, DST_F, CW])
        has0, none0, none1 = sb("has0", [P, NT]), sb("none0", [P, NT]), sb("none1", [P, NT])
        count1 = sb("count1", [P, NT])
        s_idx, d_idx = pair("s_idx", [P, CW], I32), pair("d_idx", [P, CW], I32)
        keys, prev = pair("keys", [P, CW], I32), pair("prev_keys", [P, CW], I32)
        grow, arow = pair("src_rows", [P, CW, SRC_F]), pair("dst_rows", [P, CW, DST_F])
        start, fresh, same, seen = (sb(n, [P, CW]) for n in ("start", "fresh", "same", "seen"))
        peak = sb("peak", [P, HEADS, CW + 1])
        tails, tail_t, lanes = sb("tails", [P, 2 * HEADS]), sb("tails_t", [HEADS, 2 * P]), sb("lane_peaks", [HEADS, P + 1])
        score = sb("score", [P, 3, HEADS * CW])
        expo = sb("expo", [P, 2, HEADS * CW])
        vals, decay = sb("vals", [P, SRC_F, CW]), sb("decay", [P, HEADS, CW])
        prod = sb("prod", [P, HEADS, CW])
        seg = pair("seg", [P, CW, SEG_F])
        stails, stail_t = sb("stails", [P, 2 * SRC_F]), sb("stails_t", [SRC_F, 2 * P])
        slanes, scarry = sb("lane_sums", [SRC_F, P + 1]), sb("scarry", [P, SRC_F])
        psa = ctx.enter_context(nc.psum_tensor("ps_tails", [P, 512], F32))
        psb = ctx.enter_context(nc.psum_tensor("ps_back", [P, 512], F32))
        ps_down = [ctx.enter_context(nc.psum_tensor(f"ps_early_down{k}", [P, 512], F32)) for k in range(CT)]
        psc = [ctx.enter_context(nc.psum_tensor(f"ps_nodes{k}", [P, 512], F32)) for k in range(4)]

        const, ends_loaded = sem("g_const"), sem("ends_loaded")
        node_steps, graph_steps, node_t = sem("node_steps"), sem("graph_steps"), sem("node_transposed")
        idx_loaded, keys_loaded = [sem(f"g_idx_loaded{k}") for k in range(2)], [sem(f"keys_loaded{k}") for k in range(2)]
        gathered = [[sem(f"gathered{k}_{half}") for half in range(2)] for k in range(2)]
        firsts = [sem(f"first_a_dst_gathered{k}") for k in range(2)]
        node_ad_loaded, placed, ad_loaded = sem("node_a_dst_loaded"), sem("a_dst_placed"), [sem(f"a_dst_loaded{k}") for k in range(2)]
        started, seg_made = sem("starts_made"), sem("seg_made")
        tails_t, weights_made = sem("tails_transposed"), sem("weights_exp")
        expo_made = sem("expo_made")
        seg_stored = [sem(f"seg_stored{k}") for k in range(2)]

        early = EarlyExperts(nc, sb, sem, weights, tables["xn2"], y_dram, psc, ps_down)

        def chunks(eng, run):
            n = eng.value_load(counts[0:1, 0:1], min_val=BESIDE_EDGES + 1, max_val=EDGES // CHUNK)
            run(0, 0, True)
            run(1, 1, True)
            with eng.Fori(1, BESIDE_EDGES // 2) as j:
                run(j * 2, 0, True)
                run(j * 2 + 1, 1, True)
            with eng.Fori(BESIDE_EDGES, n, 2) as c:
                c = c.with_bounds(min_val=BESIDE_EDGES, max_val=EDGES // CHUNK - 2)
                run(c, 0, False)
                run(c + 1, 1, False)

        sp_passed, pool_passed, pe_passed = sem("g_sp_passed"), sem("g_pool_passed"), sem("g_pe_passed")
        with nc.Block() as block:
            @block.gpsimd
            def _(pool):
                g = nc.gpsimd
                g.memset(ones[:, :], 1.0).then_inc(const, 1)
                g.memset(zero_row[:, :], 0.0).then_inc(const, 1)
                g.memset(last[:, 0:1], 0.0).then_inc(const, 1)
                g.memset(lanes[:, 0:1], -BIG).then_inc(const, 1)
                g.memset(slanes[:, 0:1], 0.0).then_inc(const, 1)
                pool.wait_ge(const, 1)
                g.affine_select(out=ident[:, :], in_=ones[:, :], compare_op=ALU.is_equal, fill=0.0, base=0,
                                pattern=[[-1, P]], channel_multiplier=1).then_inc(const, 1)

                pool.wait_ge(node_ad_loaded, 16)
                pool.wait_ge(node_steps, 16)
                for k in range(NT):
                    g.indirect_dma_start(placed_dram, bass.IndirectOffsetOnAxis(ap=start_idx[:, k:k + 1].bitcast(U32), axis=0),
                                         node_ad[:, k, :].bitcast(I32), None, bounds_check=EDGES - 1, oob_is_err=False).then_inc(placed, 16)

                def run(n, par, experts):
                    first = isinstance(n, int)
                    wait_alone(pool, idx_loaded[par], 32 if first else (n - par) * 16 + 32, pool_passed)
                    if not first:
                        wait_alone(pool, seg_made, n - 1, pool_passed)
                    g.indirect_dma_start(first_ad[par][:, :], None, tables["dst"], bass.IndirectOffsetOnAxis(ap=d_idx[par][:, 0:1].bitcast(U32), axis=0)).then_inc(firsts[par], 16)
                    for k in range(CW):
                        g.indirect_dma_start(grow[par][:, k, :], None, tables["src"], bass.IndirectOffsetOnAxis(ap=s_idx[par][:, k:k + 1].bitcast(U32), axis=0)).then_inc(gathered[par][k % 2], 16)
                chunks(pool, run)

            @block.sync
            def _(sp):
                w1, w2, b1, b2, w_loaded = weights
                sp.dma_start(ends_i[:, :, :], ends_dram[OFF:OFF + GROUPS, :].rearrange("(k q c) o -> q k (c o)", k=2, q=P)).then_inc(ends_loaded, 16)
                sp.dma_start(node_ad[:, :, :], tables["dst"].rearrange("(k p) f -> p k f", p=P)).then_inc(node_ad_loaded, 16)
                for t, d in ((w1[:, :, :, :], w["w1"].rearrange("e (c p) f -> p (e c) f", p=P)), (w2[:, :, :], w["w2"].rearrange("e (c p) d -> p (e c) d", p=P)),
                             (b1[:, :], w["b1"]), (b2[:, :], w["b2_lanes"])):
                    sp.dma_start(t, d).then_inc(w_loaded, 16)

                def run(n, par, experts):
                    first = isinstance(n, int)
                    if not first:
                        wait_alone(sp, firsts[par], (n - par) * 8, sp_passed)
                        for half in gathered[par]:
                            wait_alone(sp, half, (n - par) * (4 * CW), sp_passed)
                        wait_alone(sp, seg_made, n - 1, sp_passed)
                    at = lambda t, off: t[bass.ds(n * CHUNK + off, CHUNK), :].rearrange("(p c) o -> p (c o)", p=P)
                    sp.dma_start(s_idx[par][:, :], at(src_dram, 0)).then_inc(idx_loaded[par], 16)
                    sp.dma_start(d_idx[par][:, :], at(dst_dram, 0)).then_inc(idx_loaded[par], 16)
                    sp.dma_start(keys[par][:, :], at(keys_dram, 1)).then_inc(keys_loaded[par], 16)
                    sp.dma_start(prev[par][:, :], at(keys_dram, 0)).then_inc(keys_loaded[par], 16)

                    def load_ad():
                        sp.dma_start(arow[par][:, :, :].rearrange("p c f -> p (c f)").bitcast(I32),
                                     placed_dram[bass.ds(n * CHUNK, CHUNK), :].rearrange("(p c) f -> p (c f)", p=P)).then_inc(ad_loaded[par], 16)
                    if not first or n > 0:
                        load_ad()
                    if experts:
                        early.load(sp, n, 0, sp_passed)
                        early.load(sp, n, 1, sp_passed)
                    if first and n == 0:
                        sp.wait_ge(placed, 16 * NT)
                        load_ad()
                chunks(sp, run)

            @block.vector
            def _(dve):
                v = nc.vector
                st = Steps(dve, node_steps)

                def do(instruction):
                    st(instruction)
                    st.settle()
                dve.wait_ge(ends_loaded, 16)
                dve.wait_ge(const, 6)
                do(v.tensor_copy(node_q[:, 0:2, :], ends_i[:, :, :]))
                for k in range(2):
                    do(v.tensor_tensor_scan(ends[:, k, 1:NT + 1], node_q[:, k, :], node_q[:, k, :], 0.0, ALU.max, ALU.max))
                ends_tail = st.n
                dve.wait_ge(node_t, 2)
                do(v.tensor_copy(tail_row[:, :], psa[0:1, 0:2 * P]))
                do(v.tensor_tensor_scan(last[:, 1:2 * P + 1], tail_row[:, :], tail_row[:, :], last[:, 0:1], ALU.max, ALU.max))
                dve.wait_ge(node_t, 4)
                do(v.tensor_copy(ends[:, :, 0], psb[:, 0:2]))
                for k in range(2):
                    do(v.tensor_scalar(ends[:, k, 1:NT + 1], ends[:, k, 1:NT + 1], ends[:, k, 0:1], None, ALU.max))
                do(v.tensor_tensor(node_q[:, 1:3, :], ends[:, :, 1:NT + 1], ends[:, :, 0:NT], ALU.subtract))
                do(v.tensor_scalar(node_q[:, 0, :], ends[:, 0, 1:NT + 1], -1.0, 0.0, ALU.add, ALU.max))
                do(v.tensor_scalar(node_q[:, 3, :], node_q[:, 1, :], 0.0, float(2 * EDGES), ALU.is_equal, ALU.mult))
                do(v.tensor_tensor(node_q[:, 3, :], node_q[:, 3, :], ends[:, 0, 0:NT], ALU.add))
                dve.wait_ge(node_t, 8)
                do(v.tensor_copy(end_idx[:, :], psc[0][:, 0:NT]))
                do(v.tensor_scalar(has0[:, :], psc[1][:, 0:NT], 0.0, None, ALU.is_gt))
                do(v.tensor_copy(count1[:, :], psc[2][:, 0:NT]))
                do(v.tensor_copy(start_idx[:, :], psc[3][:, 0:NT]))
                do(v.tensor_scalar(none0[:, :], has0[:, :], -1.0, BIG, ALU.add, ALU.mult))
                do(v.tensor_scalar(none1[:, :], count1[:, :], 0.0, None, ALU.is_gt))
                do(v.tensor_scalar(none1[:, :], none1[:, :], -1.0, BIG, ALU.add, ALU.mult))

                def run(n, par, experts):
                    st = Steps(dve, graph_steps, n * GRAPH_STEPS)
                    first = isinstance(n, int)
                    pairs = 0 if first else n - par

                    def do(instruction):
                        st(instruction)
                        st.settle()
                    gf = grow[par][:, :, :].rearrange("p c f -> p f c")
                    af = edge_ad[:, :, :]
                    a_src = gf[:, GH:SRC_F, :]
                    out = seg[par][:, :, :].rearrange("p c f -> p f c")
                    heads = lambda t: t.rearrange("p (h c) -> p h c", h=HEADS)
                    dve.wait_ge(keys_loaded[par], pairs * 16 + 32)
                    st(v.tensor_scalar(keys[par][:, :], keys[par][:, :], SRC_BITS, None, ALU.logical_shift_right))
                    do(v.tensor_scalar(prev[par][:, :], prev[par][:, :], SRC_BITS, None, ALU.logical_shift_right))
                    v.tensor_tensor(start[:, :], keys[par][:, :], prev[par][:, :], ALU.not_equal).then_inc(started, 1)
                    dve.wait_ge(started, n + 1)
                    st(v.tensor_scalar(fresh[:, :], start[:, :], -BIG, None, ALU.mult))
                    st(v.tensor_scalar(same[:, :], start[:, :], -1.0, 1.0, ALU.mult, ALU.add))
                    do(v.tensor_tensor_scan(seen[:, :], start[:, :], start[:, :], 0.0, ALU.max, ALU.max))
                    do(v.tensor_scalar(seen[:, :], seen[:, :], -BIG, None, ALU.mult))
                    dve.wait_ge(firsts[par], pairs * 8 + 16)
                    for half in gathered[par]:
                        dve.wait_ge(half, pairs * (4 * CW) + 8 * CW)
                    dve.wait_ge(ad_loaded[par], pairs * 8 + 16)
                    do(v.tensor_copy(arow[par][:, 0, :], first_ad[par][:, :]))
                    for h in range(HEADS):
                        st(v.tensor_tensor_scan(edge_ad[:, h, :], same[:, :], arow[par][:, :, h], 0.0, ALU.mult, ALU.add))
                    for h in range(HEADS):
                        st(v.tensor_tensor_scan(peak[:, h, 1:CW + 1], fresh[:, :], a_src[:, h, :], -BIG, ALU.add, ALU.max))
                    st.settle()
                    st(v.tensor_copy(tails[:, 0:HEADS], peak[:, :, CW]))
                    st(v.tensor_copy(tails[:, HEADS:2 * HEADS], seen[:, CW - 1:CW].to_broadcast([P, HEADS])))
                    dve.wait_ge(tails_t, n * 6 + 2)
                    do(v.tensor_copy(tail_t[:, :], psa[0:HEADS, 0:2 * P]))
                    do(v.tensor_tensor_scan(lanes[:, 1:P + 1], tail_t[:, P:2 * P], tail_t[:, 0:P], lanes[:, 0:1], ALU.add, ALU.max))
                    dve.wait_ge(tails_t, n * 6 + 3)
                    st(v.tensor_copy(peak[:, :, 0], psb[:, 0:HEADS]))
                    do(v.tensor_copy(lanes[:, 0:1], lanes[:, P:P + 1]))
                    for h in range(HEADS):
                        st(v.scalar_tensor_tensor(peak[:, h, 1:CW + 1], seen[:, :], peak[:, h, 0:1], peak[:, h, 1:CW + 1], ALU.add, ALU.max))
                    st.settle()
                    st(v.tensor_tensor(heads(score[:, 0, :]), a_src, af, ALU.add))
                    st(v.tensor_tensor(heads(score[:, 1, :]), peak[:, :, 1:CW + 1], af, ALU.add))
                    do(v.tensor_tensor(heads(score[:, 2, :]), peak[:, :, 0:CW], af, ALU.add))
                    do(v.scalar_tensor_tensor(score[:, :, :], score[:, :, :], 0.2, score[:, :, :], ALU.mult, ALU.max))
                    do(v.tensor_tensor(expo[:, :, :], score[:, 0:3:2, :], score[:, 1:2, :].to_broadcast([P, 2, HEADS * CW]), ALU.subtract))
                    v.tensor_scalar(expo[:, :, :], expo[:, :, :], 0.0, None, ALU.min).then_inc(expo_made, 1)
                    dve.wait_ge(weights_made, n * 2 + 2)
                    st(v.tensor_tensor(decay[:, :, :], decay[:, :, :], same[:, None, :].to_broadcast([P, HEADS, CW]), ALU.mult))
                    per_expert = lambda t: t[:, :, None, :].to_broadcast([P, HEADS, EXPERTS, CW])
                    do(v.tensor_tensor(vals[:, 0:GH, :].rearrange("p (h e) c -> p h e c", h=HEADS), per_expert(vals[:, GH:SRC_F, :]),
                                       gf[:, 0:GH, :].rearrange("p (h e) c -> p h e c", h=HEADS), ALU.mult))
                    if not first:
                        dve.wait_ge(seg_stored[par], pairs * 8)
                    for f in range(SRC_F):
                        h = f // EXPERTS if f < GH else f - GH
                        st(v.tensor_tensor_scan(out[:, f, :], decay[:, h, :], vals[:, f, :], 0.0, ALU.mult, ALU.add))
                    for h in range(HEADS):
                        st(v.tensor_tensor_scan(prod[:, h, :], decay[:, h, :], zero_row[:, :], 1.0, ALU.mult, ALU.add))
                    st.settle()
                    st(v.tensor_copy(stails[:, 0:SRC_F], out[:, 0:SRC_F, CW - 1]))
                    st(v.tensor_copy(stails[:, SRC_F:SRC_F + GH].rearrange("p (h e) -> p h e", h=HEADS), prod[:, :, CW - 1:CW].to_broadcast([P, HEADS, EXPERTS])))
                    st(v.tensor_copy(stails[:, SRC_F + GH:2 * SRC_F], prod[:, :, CW - 1]))
                    dve.wait_ge(tails_t, n * 6 + 5)
                    do(v.tensor_copy(stail_t[:, :], psa[0:SRC_F, 0:2 * P]))
                    do(v.tensor_tensor_scan(slanes[:, 1:P + 1], stail_t[:, P:2 * P], stail_t[:, 0:P], slanes[:, 0:1], ALU.mult, ALU.add))
                    dve.wait_ge(tails_t, n * 6 + 6)
                    st(v.tensor_copy(scarry[:, :], psb[:, 0:SRC_F]))
                    do(v.tensor_copy(slanes[:, 0:1], slanes[:, P:P + 1]))
                    for f in range(SRC_F):
                        h = f // EXPERTS if f < GH else f - GH
                        st(v.scalar_tensor_tensor(out[:, f, :], prod[:, h, :], scarry[:, f:f + 1], out[:, f, :], ALU.mult, ALU.add))
                    st.settle()
                    v.tensor_copy(out[:, SRC_F:SEG_F, :], peak[:, :, 1:CW + 1]).then_inc(seg_made, 1)
                    dve.wait_ge(seg_made, n + 1)
                    assert st.n == GRAPH_STEPS, st.n
                chunks(dve, run)

            @block.tensor
            def _(pe):
                t = nc.tensor.transpose
                pe.wait_ge(const, 6)
                pe.wait_ge(node_steps, 3)
                for k in range(2):
                    t(psa[0:1, k * P:(k + 1) * P], ends[:, k, NT:NT + 1], ident[:, :]).then_inc(node_t, 1)
                pe.wait_ge(node_steps, 5)
                for k in range(2):
                    t(psb[:, k:k + 1], last[0:1, k * P:(k + 1) * P], ident[0:1, 0:1]).then_inc(node_t, 1)
                pe.wait_ge(node_steps, 12)
                for k in range(4):
                    t(psc[k][:, 0:NT], node_q[:, k, :], ident[:, :]).then_inc(node_t, 1)

                def run(n, par, experts):
                    base = n * GRAPH_STEPS

                    def step(name):
                        if name == "peaks":
                            pe.wait_ge(graph_steps, base + PEAKS_AT)
                            for k in range(2):
                                t(psa[0:HEADS, k * P:(k + 1) * P], tails[:, k * HEADS:(k + 1) * HEADS], ident[:, :]).then_inc(tails_t, 1)
                        elif name == "peak_lanes":
                            wait_alone(pe, graph_steps, base + PEAK_LANES_AT, pe_passed)
                            t(psb[:, 0:HEADS], lanes[:, 0:P], ident[0:HEADS, 0:HEADS]).then_inc(tails_t, 1)
                        elif name == "sums":
                            pe.wait_ge(graph_steps, base + SUMS_AT)
                            for k in range(2):
                                t(psa[0:SRC_F, k * P:(k + 1) * P], stails[:, k * SRC_F:(k + 1) * SRC_F], ident[:, :]).then_inc(tails_t, 1)
                        elif name == "sum_lanes":
                            wait_alone(pe, graph_steps, base + SUM_LANES_AT, pe_passed)
                            t(psb[:, 0:SRC_F], slanes[:, 0:P], ident[0:SRC_F, 0:SRC_F]).then_inc(tails_t, 1)

                    def beside(k):
                        for name, unit in (PE_UNIT_FIRST if isinstance(n, int) and n == 0 else PE_UNIT).items():
                            if unit == k:
                                step(name)
                    if experts:
                        early.products(pe, n, 0)
                        early.products(pe, n, 1, beside)
                    else:
                        for name in PE_UNIT:
                            step(name)
                pe.wait_ge(weights[-1], 64)
                pe.wait_ge(node_steps, 16)
                chunks(pe, run)

            @block.scalar
            def _(act):
                act.wait_ge(weights[-1], 64)

                def run(n, par, experts):
                    def step(name):
                        if name == "exps":
                            act.wait_ge(expo_made, n + 1)
                            for k, dst in enumerate((vals[:, GH:SRC_F, :], decay[:, :, :])):
                                nc.scalar.activation(dst, expo[:, k, :].rearrange("p (h c) -> p h c", h=HEADS), ACT.Exp).then_inc(weights_made, 1)
                        else:
                            act.wait_ge(seg_made, n + 1)
                            act.dma_start(seg_dram[bass.ds(n * CHUNK, CHUNK), :].rearrange("(p c) f -> p (c f)", p=P),
                                          seg[par][:, :, :].rearrange("p c f -> p (c f)").bitcast(I32)).then_inc(seg_stored[par], 16)

                    def beside(k):
                        for name, unit in (ACT_UNIT_FIRST if isinstance(n, int) and n == 0 else ACT_UNIT).items():
                            if unit == k:
                                step(name)
                    if experts:
                        early.gelus(act, n, 0)
                        early.gelus(act, n, 1, beside)
                    else:
                        step("exps")
                        step("store")
                        if par == 1:
                            for k in range(2):
                                act.wait_ge(seg_stored[k], n * 8 + 8)
                chunks(act, run)

        gate_nodes(nc, ctx, sb, sem, ident, eps, end_idx, has0, none0, none1, count1, psc, seg_dram, tables, w, gates_dram, early, node_ad)


def gate_nodes(nc, ctx, sb, sem, ident, eps, end_idx, has0, none0, none1, count1, psc, seg_dram, tables, w, gates_dram, early, ad):
    K4 = NT * HEADS
    last_row, gamma, beta, bias = sb("last_row", [P, SRC_F]), sb("gamma", [P, GH]), sb("beta", [P, GH]), sb("b_gat", [P, GH])
    rows, node = sb("seg_rows", [P, NT, SEG_F]), sb("node_rows", [P, NT, SRC_F])
    a4 = sb("node_scores", [P, 4, K4])
    wts = sb("node_weights", [P, 3, K4])
    den, agg, tmp = sb("den", [P, K4]), sb("agg", [P, NT * GH]), sb("agg_tmp", [P, NT * GH])
    mean, var = sb("node_mean", [P, NT]), sb("node_var", [P, NT])
    sc, ties = sb("expert_scores", [P, K4]), sb("ties", [P, EXPERTS * EXPERTS])
    beats, even, rank, top = sb("beats", [P, NT * GH]), sb("even", [P, NT * GH]), sb("rank", [P, K4]), sb("top", [P, NT])
    gt = [sb(f"gates_t{k}", [EXPERTS, 512]) for k in range(4)]
    loaded, gathered, steps, exps = sem("node_loaded"), sem("seg_gathered"), sem("gate_steps"), sem("node_exps")
    var_made, gates_t, gates_out = sem("var_made"), sem("gates_transposed"), sem("gates_out")
    stored = [sem(f"gates_stored{k}") for k in range(4)]
    passed = sem("n_sp_passed")
    rest = range(BESIDE_EDGES, BESIDE_EDGES + BESIDE_GATES)
    tie_made, weights_ready, gates_made = sem("ties_made"), sem("node_exponents"), sem("gates_made")

    with nc.Block() as block:
        @block.sync
        def _(sp):
            sp.dma_start(node[:, :, :], tables["src"].rearrange("(k p) f -> p k f", p=P)).then_inc(loaded, 16)
            sp.dma_start(last_row[:, :], tables["src"][NODES - 1:NODES, :].to_broadcast([P, SRC_F])).then_inc(loaded, 16)
            for t, d in ((gamma, w["gamma"]), (beta, w["beta"]), (bias, w["b_gat"])):
                sp.dma_start(t[:, :], d.to_broadcast([P, GH])).then_inc(loaded, 16)
            for n in rest:
                early.load(sp, n, 0, passed)
                early.load(sp, n, 1, passed)
            for k in range(NT // 4):
                sp.wait_ge(gates_out, k + 1)
                sp.dma_start(gates_dram[:, k * 512:(k + 1) * 512], gt[k % 4][:, :]).then_inc(stored[k % 4], 16)
            for k in range(4):
                sp.wait_ge(stored[k], NT // 16 * 16)

        @block.gpsimd
        def _(pool):
            g = nc.gpsimd
            g.memset(eps[:, :], 1e-5).then_inc(tie_made, 1)
            g.memset(ties[:, :], 1.0).then_inc(tie_made, 1)
            pool.wait_ge(tie_made, 2)
            g.affine_select(out=ties[:, :].rearrange("p (e j) -> p e j", j=EXPERTS), in_=ties[:, :].rearrange("p (e j) -> p e j", j=EXPERTS),
                            compare_op=ALU.is_gt, fill=0.0, base=0, pattern=[[1, EXPERTS], [-1, EXPERTS]], channel_multiplier=0).then_inc(tie_made, 1)
            for k in range(NT):
                g.indirect_dma_start(rows[:, k, :].bitcast(I32), None, seg_dram, bass.IndirectOffsetOnAxis(ap=end_idx[:, k:k + 1].bitcast(U32), axis=0)).then_inc(gathered, 16)

        @block.vector
        def _(dve):
            v = nc.vector
            st = Steps(dve, steps)

            def do(instruction):
                st(instruction)
                st.settle()
            kh = lambda t: t.rearrange("p (k h) -> p k h", h=HEADS)
            khe = lambda t: t.rearrange("p (k h e) -> p k h e", h=HEADS, e=EXPERTS)
            over_h = lambda t: t[:, :, None].to_broadcast([P, NT, HEADS])
            over_e = lambda t: kh(t)[:, :, :, None].to_broadcast([P, NT, HEADS, EXPERTS])
            over_k = lambda t: t[:, None, :].to_broadcast([P, NT, HEADS])
            a_self, a_last = node[:, :, GH:SRC_F], over_k(last_row[:, GH:SRC_F])
            dve.wait_ge(loaded, 16 * 5)
            do(v.tensor_tensor(kh(a4[:, 1, :]), a_self, ad[:, :, :], ALU.add))
            do(v.tensor_tensor(kh(a4[:, 2, :]), a_last, ad[:, :, :], ALU.add))
            dve.wait_ge(gathered, 16 * NT)
            do(v.tensor_tensor(kh(a4[:, 0, :]), rows[:, :, SRC_F:SEG_F], ad[:, :, :], ALU.add))
            do(v.tensor_tensor(kh(den[:, :]), rows[:, :, SRC_F:SEG_F], over_h(none0[:, :]), ALU.add))
            do(v.tensor_tensor(kh(den[:, :]), kh(den[:, :]), a_self, ALU.max))
            do(v.tensor_tensor(kh(sc[:, :]), over_h(none1[:, :]), a_last, ALU.add))
            do(v.tensor_tensor(den[:, :], den[:, :], sc[:, :], ALU.max))
            do(v.tensor_tensor(kh(a4[:, 3, :]), kh(den[:, :]), ad[:, :, :], ALU.add))
            do(v.scalar_tensor_tensor(a4[:, :, :], a4[:, :, :], 0.2, a4[:, :, :], ALU.mult, ALU.max))
            do(v.tensor_tensor(wts[:, :, :], a4[:, 0:3, :], a4[:, 3:4, :].to_broadcast([P, 3, K4]), ALU.subtract))
            v.tensor_scalar(wts[:, :, :], wts[:, :, :], 0.0, None, ALU.min).then_inc(weights_ready, 1)
            dve.wait_ge(exps, 1)
            do(v.tensor_tensor(kh(wts[:, 0, :]), kh(wts[:, 0, :]), over_h(has0[:, :]), ALU.mult))
            do(v.tensor_tensor(kh(wts[:, 2, :]), kh(wts[:, 2, :]), over_h(count1[:, :]), ALU.mult))
            do(v.tensor_tensor(kh(den[:, :]), rows[:, :, GH:SRC_F], kh(wts[:, 0, :]), ALU.mult))
            do(v.tensor_tensor(den[:, :], den[:, :], wts[:, 1, :], ALU.add))
            do(v.tensor_tensor(den[:, :], den[:, :], wts[:, 2, :], ALU.add))
            do(v.tensor_scalar(den[:, :], den[:, :], 1e-16, None, ALU.add))
            do(v.reciprocal(den[:, :], den[:, :]))
            he = lambda t: t.rearrange("p k (h e) -> p k h e", h=HEADS)
            do(v.tensor_tensor(khe(agg[:, :]), he(rows[:, :, 0:GH]), over_e(wts[:, 0, :]), ALU.mult))
            do(v.tensor_tensor(khe(tmp[:, :]), he(node[:, :, 0:GH]), over_e(wts[:, 1, :]), ALU.mult))
            do(v.tensor_tensor(agg[:, :], agg[:, :], tmp[:, :], ALU.add))
            last_he = last_row[:, 0:GH].rearrange("p (h e) -> p h e", h=HEADS)
            for h in range(HEADS):
                do(v.tensor_tensor(khe(tmp[:, :])[:, :, h, :], last_he[:, h:h + 1, :].to_broadcast([P, NT, EXPERTS]), over_e(wts[:, 2, :])[:, :, h, :], ALU.mult))
            do(v.tensor_tensor(agg[:, :], agg[:, :], tmp[:, :], ALU.add))
            do(v.tensor_tensor(khe(agg[:, :]), khe(agg[:, :]), over_e(den[:, :]), ALU.mult))
            kf = lambda t: t.rearrange("p (k f) -> p k f", f=GH)
            f_over_k = lambda t: t[:, None, :].to_broadcast([P, NT, GH])
            over_f = lambda t: t[:, :, None].to_broadcast([P, NT, GH])
            do(v.tensor_tensor(kf(agg[:, :]), kf(agg[:, :]), f_over_k(bias[:, :]), ALU.add))
            do(v.tensor_reduce(mean[:, :], kf(agg[:, :]), AX, ALU.add))
            do(v.tensor_scalar(mean[:, :], mean[:, :], 1.0 / GH, None, ALU.mult))
            do(v.tensor_tensor(kf(agg[:, :]), kf(agg[:, :]), over_f(mean[:, :]), ALU.subtract))
            do(v.tensor_tensor(tmp[:, :], agg[:, :], agg[:, :], ALU.mult))
            v.tensor_reduce(var[:, :], kf(tmp[:, :]), AX, ALU.add).then_inc(var_made, 1)
            dve.wait_ge(exps, 3)
            do(v.tensor_tensor(kf(agg[:, :]), kf(agg[:, :]), over_f(var[:, :]), ALU.mult))
            do(v.tensor_tensor(kf(agg[:, :]), kf(agg[:, :]), f_over_k(gamma[:, :]), ALU.mult))
            do(v.tensor_tensor(kf(agg[:, :]), kf(agg[:, :]), f_over_k(beta[:, :]), ALU.add))
            do(v.tensor_reduce(kh(sc[:, :]), khe(agg[:, :]).rearrange("p k h e -> p k e h"), AX, ALU.add))
            do(v.tensor_scalar(sc[:, :], sc[:, :], 1.0 / HEADS, None, ALU.mult))
            mine = kh(sc[:, :])[:, :, :, None].to_broadcast([P, NT, EXPERTS, EXPERTS])
            theirs = kh(sc[:, :])[:, :, None, :].to_broadcast([P, NT, EXPERTS, EXPERTS])
            do(v.tensor_tensor(khe(beats[:, :]), theirs, mine, ALU.is_gt))
            do(v.tensor_tensor(khe(even[:, :]), theirs, mine, ALU.is_equal))
            dve.wait_ge(tie_made, 3)
            do(v.tensor_tensor(kf(even[:, :]), kf(even[:, :]), f_over_k(ties[:, :]), ALU.mult))
            do(v.tensor_tensor(beats[:, :], beats[:, :], even[:, :], ALU.add))
            do(v.tensor_reduce(kh(rank[:, :]), khe(beats[:, :]), AX, ALU.add))
            do(v.tensor_scalar(rank[:, :], rank[:, :], 2.0, None, ALU.is_lt))
            do(v.tensor_reduce(top[:, :], kh(sc[:, :]), AX, ALU.max))
            v.tensor_tensor(kh(sc[:, :]), kh(sc[:, :]), over_h(top[:, :]), ALU.subtract).then_inc(var_made, 1)
            dve.wait_ge(exps, 4)
            do(v.tensor_tensor(sc[:, :], sc[:, :], rank[:, :], ALU.mult))
            do(v.tensor_reduce(top[:, :], kh(sc[:, :]), AX, ALU.add))
            do(v.reciprocal(top[:, :], top[:, :]))
            v.tensor_tensor(kh(sc[:, :]), kh(sc[:, :]), over_h(top[:, :]), ALU.mult).then_inc(gates_made, 1)
            for k in range(NT // 4):
                dve.wait_ge(gates_t, 4 * k + 4)
                if k >= 4:
                    dve.wait_ge(stored[k % 4], k // 4 * 16)
                v.tensor_copy(gt[k % 4][:, :], psc[k % 4][0:EXPERTS, :]).then_inc(gates_out, 1)

        @block.scalar
        def _(act):
            f = nc.scalar.activation
            act.wait_ge(tie_made, 1)

            def step(name):
                if name == "weights":
                    act.wait_ge(weights_ready, 1)
                    f(wts[:, :, :], wts[:, :, :], ACT.Exp).then_inc(exps, 1)
                elif name == "rstd":
                    act.wait_ge(var_made, 1)
                    f(var[:, :], var[:, :], ACT.Ln, scale=1.0 / GH, bias=eps[:, 0:1]).then_inc(exps, 1)
                    act.wait_ge(exps, 2)
                    f(var[:, :], var[:, :], ACT.Exp, scale=-0.5).then_inc(exps, 1)
                elif name == "softmax":
                    act.wait_ge(var_made, 2)
                    f(sc[:, :], sc[:, :], ACT.Exp).then_inc(exps, 1)

            for n in rest:
                for par in range(2):
                    early.gelus(act, n, par, lambda k: [step(name) for name, at in GATE_UNITS.items() if at == (n - rest[0], par, k)])
            for e in range(EXPERTS):
                act.wait_ge(early.y_stored[e], EARLY * 16)

        @block.tensor
        def _(pe):
            for n in rest:
                early.products(pe, n, 0)
                early.products(pe, n, 1)
            pe.wait_ge(early.gelu, EARLY * UNITS)
            pe.wait_ge(gates_made, 1)
            for k in range(NT):
                if k % 4 == 0 and k >= 16:
                    pe.wait_ge(gates_out, k // 4 - 3)
                nc.tensor.transpose(psc[k // 4 % 4][0:EXPERTS, (k % 4) * P:(k % 4 + 1) * P], sc[:, k * EXPERTS:(k + 1) * EXPERTS], ident[:, :]).then_inc(gates_t, 1)

LATE = CHUNKS - EARLY


def experts(nc, tables, gates_dram, y_dram, w, weights, out_dram):
    assert LATE == EARLY
    with ExitStack() as ctx:
        sb = lambda name, shape, dt=F32: ctx.enter_context(nc.sbuf_tensor(name, shape, dt))
        sem = lambda name: ctx.enter_context(nc.semaphore(name))
        pair = lambda name, shape: [sb(f"{name}{k}", shape) for k in range(2)]
        w1, w2, b1, _, _ = weights
        b2 = sb("b2", [EXPERTS, CT * P])
        xn, res, gate, out = pair("f_xn", [P, CT, T]), pair("f_x2", [P, CT, T]), pair("f_gates", [EXPERTS, T]), pair("f_out", [P, CT, T])
        spread = pair("f_gates_spread", [P, EXPERTS, T])
        y, y_spread, y_sum = pair("y_in", [P, EXPERTS, CT, T]), pair("y_gates_spread", [P, EXPERTS, T]), pair("y_sum", [P, CT, T])
        hid = [sb(f"hid{k}", [P, T]) for k in range(RING)]
        ps_up = [ctx.enter_context(nc.psum_tensor(f"ps_up{k}", [P, T], F32)) for k in range(RING)]
        ps_down = [ctx.enter_context(nc.psum_tensor(f"ps_down{k}", [P, T], F32)) for k in range(2 * CT)]
        b2_loaded = sem("f_b2_loaded")
        loaded, stored = [sem(f"f_loaded{k}") for k in range(2)], [sem(f"f_stored{k}") for k in range(2)]
        y_loaded, y_stored = [sem(f"y_loaded{k}") for k in range(2)], [sem(f"y_stored{k}") for k in range(2)]
        up, gelu, gated, down, added = sem("up_full"), sem("gelu_made"), sem("f_gated"), sem("down_done"), sem("f_added")
        y_gated, y_added = sem("y_gated"), sem("y_added")

        def bodies(eng, run):
            run(0, 0, 0)
            run(1, 0, 1)
            with eng.Fori(1, LATE // 2) as j:
                run(j * 2, j, 0)
                run(j * 2 + 1, j, 1)

        chunk_of = lambda t, i: t[bass.ds(i, 1)].rearrange("o p (c t) -> (o p) c t", c=CT)
        gates_of = lambda i: gates_dram[:, bass.ds(i * T, T)]
        sp_passed, pool_passed = sem("f_sp_passed"), sem("f_pool_passed")
        with nc.Block() as block:
            @block.sync
            def _(sp):
                sp.dma_start(b2[:, :], w["b2"]).then_inc(b2_loaded, 16)

                def run(i, j, par):
                    if not isinstance(i, int):
                        wait_alone(sp, added, i * 2 - 2, sp_passed)
                        wait_alone(sp, gelu, i * UNITS - UNITS, sp_passed)
                        wait_alone(sp, gated, i * UNITS - UNITS, sp_passed)
                    sp.dma_start(xn[par][:, :, :], chunk_of(tables["xn2"], i + EARLY)).then_inc(loaded[par], 16)
                    sp.dma_start(gate[par][:, :], gates_of(i + EARLY)).then_inc(loaded[par], 16)
                    sp.dma_start(spread[par][:, :, :], gates_of(i + EARLY)[None, :, :].to_broadcast([P, EXPERTS, T])).then_inc(loaded[par], 16)
                    sp.dma_start(res[par][:, :, :], chunk_of(tables["x2"], i + EARLY)).then_inc(loaded[par], 16)
                    if not isinstance(i, int):
                        wait_alone(sp, y_stored[par], j * 16, sp_passed)
                        wait_alone(sp, y_added, (i - 1) * EXPERTS, sp_passed)
                    sp.dma_start(y[par][:, :, :, :], y_dram[bass.ds(i, 1)].rearrange("o p (e c t) -> (o p) e c t", e=EXPERTS, c=CT)).then_inc(y_loaded[par], 16)
                    sp.dma_start(y_spread[par][:, :, :], gates_of(i)[None, :, :].to_broadcast([P, EXPERTS, T])).then_inc(y_loaded[par], 16)
                    sp.dma_start(y_sum[par][:, :, :], chunk_of(tables["x2"], i)).then_inc(y_loaded[par], 16)
                bodies(sp, run)

            @block.gpsimd
            def _(pool):
                def run(i, j, par):
                    wait_alone(pool, y_added, i * EXPERTS + EXPERTS, pool_passed)
                    pool.dma_start(chunk_of(out_dram, i), y_sum[par][:, :, :]).then_inc(y_stored[par], 16)
                    wait_alone(pool, added, i * 2 + 2, pool_passed)
                    pool.dma_start(chunk_of(out_dram, i + EARLY), out[par][:, :, :]).then_inc(stored[par], 16)
                bodies(pool, run)
                for k in range(2):
                    pool.wait_ge(stored[k], LATE // 2 * 16)
                    pool.wait_ge(y_stored[k], LATE // 2 * 16)

            @block.tensor
            def _(pe):
                mm = nc.tensor.matmul
                pe.wait_ge(b2_loaded, 16)

                def run(i, j, par):
                    pe.wait_ge(loaded[par], j * 64 + 64)
                    later = not isinstance(i, int) or i > 0
                    sums = ps_down[CT * par:CT * (par + 1)]
                    for k in range(UNITS + LAG):
                        if k < UNITS:
                            e, ft = divmod(k, FT)
                            if k >= RING or later:
                                pe.wait_ge(gelu, i * UNITS + k - RING + 1)
                            for c in range(CT):
                                last = mm(ps_up[k % RING][:, :], w1[:, e, c, ft * P:(ft + 1) * P], xn[par][:, c, :], start=(c == 0), stop=(c == CT - 1))
                            last.then_inc(up, 1)
                        if k == LAG:
                            if not isinstance(i, int):
                                pe.wait_ge(added, i * 2 - 2)
                            for c in range(CT):
                                mm(sums[c][:, :], b2[:, c * P:(c + 1) * P], gate[par][:, :], start=True, stop=False)
                        if k >= LAG:
                            q = k - LAG
                            pe.wait_ge(gated, i * UNITS + q + 1)
                            for c in range(CT):
                                last = mm(sums[c][:, :], w2[:, q, c * P:(c + 1) * P], hid[q % RING][:, :], start=False, stop=(q == UNITS - 1))
                            last.then_inc(down, 1)
                bodies(pe, run)

            @block.scalar
            def _(act):
                def run(i, j, par):
                    later = not isinstance(i, int) or i > 0
                    for k in range(UNITS):
                        act.wait_ge(up, i * UNITS + k + 1)
                        if k >= RING or later:
                            act.wait_ge(down, i * UNITS + k - RING + 1)
                        nc.scalar.activation(hid[k % RING][:, :], ps_up[k % RING][:, :], ACT.Gelu, bias=b1[:, k:k + 1]).then_inc(gelu, 1)
                bodies(act, run)

            @block.vector
            def _(dve):
                v = nc.vector

                def merge(i, j, par, k):
                    e = k // 2
                    if k == 0:
                        dve.wait_ge(y_loaded[par], j * 48 + 48)
                    if k % 2 == 0:
                        v.tensor_tensor(y[par][:, e, :, :], y[par][:, e, :, :], y_spread[par][:, e:e + 1, :].to_broadcast([P, CT, T]), ALU.mult).then_inc(y_gated, 1)
                    else:
                        dve.wait_ge(y_gated, i * EXPERTS + e + 1)
                        if e:
                            dve.wait_ge(y_added, i * EXPERTS + e)
                        v.tensor_tensor(y_sum[par][:, :, :], y_sum[par][:, :, :], y[par][:, e, :, :], ALU.add).then_inc(y_added, 1)

                def run(i, j, par):
                    dve.wait_ge(loaded[par], j * 64 + 64)
                    for k in range(UNITS):
                        dve.wait_ge(gelu, i * UNITS + k + 1)
                        v.tensor_tensor(hid[k % RING][:, :], hid[k % RING][:, :], spread[par][:, k // FT, :], ALU.mult).then_inc(gated, 1)
                        if k % 2 == 1:
                            merge(i, j, par, k // 2)
                    dve.wait_ge(down, i * UNITS + UNITS)
                    if not isinstance(i, int):
                        dve.wait_ge(stored[par], j * 16)
                    for c in range(CT):
                        v.tensor_tensor(out[par][:, c, :], ps_down[CT * par + c][:, :], res[par][:, c, :], ALU.add).then_inc(added, 1)
                bodies(dve, run)


INPUTS = ["x", "in", "x_proj", "dt", "out_proj", "conv", "conv_b", "dt_b", "skip", "a_log", "gat", "att", "b_gat",
          "gamma", "beta", "w1", "b1", "w2", "b2", "b2_lanes", "edge_src", "edge_dst"]


def metaformer_block(nc, a, out):
    dram = lambda name, shape, dt=F32: nc.dram_tensor(name, shape, dt, kind="Internal").ap()
    keys, ends_at = dram("keys_sorted", [EDGES + 2, 1], I32), dram("ends_at", [EDGES, 1], I32)
    ends = dram("ends", [GROUPS + OFF, 1], I32)
    src, dst = dram("edge_src_sorted", [EDGES, 1], I32), dram("edge_dst_sorted", [EDGES, 1], I32)
    placed = dram("a_dst_at_starts", [EDGES, DST_F], I32)
    seg = dram("segments", [EDGES, SEG_F], I32)
    gates = dram("gates", [EXPERTS, NODES])
    y = dram("early_expert_outputs", [EARLY, P, EXPERTS * CT * T])
    tables = {"x2": dram("x_after_mamba", [CHUNKS, P, CT * T]), "xn2": dram("x_normed", [CHUNKS, P, CT * T]),
              "src": dram("node_src", [NODES, SRC_F]), "dst": dram("node_dst_scores", [NODES, DST_F])}
    w = {"in": a["in"], "x": a["x_proj"], "dt": a["dt"], "out": a["out_proj"], "conv": a["conv"], "conv_b": a["conv_b"],
         "dt_b": a["dt_b"], "skip": a["skip"], "a_log": a["a_log"], "gat": a["gat"], "att": a["att"]}
    with nc.sbuf_tensor("chunk_counts", [P, 2], I32) as counts:
        sort_edges(nc, a["edge_src"], a["edge_dst"], keys, ends_at, ends, src, dst, placed, counts)
        mamba(nc, a["x"], w, tables, ends_at, ends, counts)
        with (nc.sbuf_tensor("w1", [P, EXPERTS, CT, FF], F32) as w1, nc.sbuf_tensor("w2", [P, UNITS, CT * P], F32) as w2,
              nc.sbuf_tensor("b1", [P, UNITS], F32) as b1, nc.sbuf_tensor("b2_lanes", [P, EXPERTS * CT], F32) as b2,
              nc.semaphore("expert_weights_loaded") as w_loaded):
            weights = (w1, w2, b1, b2, w_loaded)
            attention(nc, keys, src, dst, ends, tables, a, seg, gates, counts, weights, y, placed)
            experts(nc, tables, gates, y, a, weights, out)


def kernel(x, L0_conv_in_proj_w, L0_conv_conv_w, L0_conv_conv_b, L0_conv_x_proj_w, L0_conv_dt_proj_w, L0_conv_dt_proj_b,
           L0_conv_A_log, L0_conv_D, L0_conv_out_proj_w, L0_ffn_W_gat, L0_ffn_att_src, L0_ffn_att_dst, L0_ffn_b_gat,
           L0_ffn_ln_gamma, L0_ffn_ln_beta, L0_ffn_W1, L0_ffn_b1, L0_ffn_W2, L0_ffn_b2, L0_ffn_edge_index):
    import concourse.bacc as bacc
    from concourse.bass_utils import run_bass_kernel_spmd

    lay = np.ascontiguousarray
    arr = np.asarray
    column = lambda v: lay(arr(v).reshape(-1, P).T)
    xs = lay(arr(x).reshape(4, CT, P, PER_BATCH, T).transpose(0, 3, 2, 1, 4)).reshape(CHUNKS, P, CT * T)
    xp, dtw = arr(L0_conv_x_proj_w).T, arr(L0_conv_dt_proj_w).T
    x_proj = np.zeros((xp.shape[0], 64), xp.dtype)
    x_proj[:, 0:16], x_proj[:, 32:64] = xp[:, 0:16], xp[:, 16:48]
    dt = np.zeros((32, dtw.shape[1]), dtw.dtype)
    dt[0:16] = dtw
    edges = arr(L0_ffn_edge_index)
    inputs = {
        "x": xs, "in": lay(arr(L0_conv_in_proj_w).T), "x_proj": x_proj, "dt": dt, "out_proj": lay(arr(L0_conv_out_proj_w).T),
        "conv": lay(arr(L0_conv_conv_w).reshape(-1, TAPS)), "conv_b": column(L0_conv_conv_b), "dt_b": column(L0_conv_dt_proj_b),
        "skip": column(L0_conv_D), "a_log": lay(arr(L0_conv_A_log)), "gat": lay(arr(L0_ffn_W_gat)),
        "att": lay(np.stack([arr(L0_ffn_att_src).reshape(-1), arr(L0_ffn_att_dst).reshape(-1)])),
        "b_gat": lay(arr(L0_ffn_b_gat).reshape(1, -1)), "gamma": lay(arr(L0_ffn_ln_gamma).reshape(1, -1)),
        "beta": lay(arr(L0_ffn_ln_beta).reshape(1, -1)), "w1": lay(arr(L0_ffn_W1)), "b1": column(L0_ffn_b1),
        "w2": lay(arr(L0_ffn_W2)), "b2": lay(arr(L0_ffn_b2)), "b2_lanes": column(L0_ffn_b2),
        "edge_src": lay(edges[0].reshape(P, EC)), "edge_dst": lay(edges[1].reshape(P, EC)),
    }
    nc = bacc.Bacc("TRN2", target_bir_lowering=False, num_devices=1)
    arrays, args = {}, {}
    for name in INPUTS:
        arrays[f"in_{name}"] = inputs[name]
        args[name] = nc.dram_tensor(f"in_{name}", inputs[name].shape, mybir.dt.from_np(inputs[name].dtype), kind="ExternalInput").ap()
    out = nc.dram_tensor("out", [CHUNKS, P, CT * T], F32, kind="ExternalOutput").ap()
    metaformer_block(nc, args, out)
    got = run_bass_kernel_spmd(nc, [arrays], core_ids=[0]).results[0]["out"]
    return lay(got.reshape(4, PER_BATCH, P, CT, T).transpose(0, 3, 2, 1, 4)).reshape(4, CT * P, 64, 64)
```
